# Optimizing a Trainium2 kernel written in Bass

```python
import numpy as np
import jax
import jax.numpy as jnp

def _softmax(x, axis=-1):
    return jax.nn.softmax(x, axis=axis)
def _gelu(x):
    return jax.nn.gelu(x, approximate=True)
def _silu(x):
    return jax.nn.silu(x)
def _sigmoid(x):
    return jax.nn.sigmoid(x)
def _layernorm(x, axis=-1, eps=1e-5):
    m = jnp.mean(x, axis=axis, keepdims=True)
    v = jnp.var(x, axis=axis, keepdims=True)
    return (x - m) / jnp.sqrt(v + eps)
def _scatter_add(tgt, idx, src, axis=0):
    return tgt.at[idx].add(src)
def _segment_sum(src, seg, n):
    return jax.ops.segment_sum(src, seg, n)

kernel_name = 'mk_metaformer_d2_conv_nchw256_64aa11'

def setup_inputs(seed: int = 0):
    np.random.seed(seed)
    _w = jnp.asarray
    def _rec_inputs():
        import jax
        import jax.numpy as jnp
        _gk = jax.random.key(seed)
        x = -0.000929 + 1 * jax.random.normal(jax.random.fold_in(_gk, 1), (4, 256, 32, 32), jnp.float32)
        return x
    x = _rec_inputs()
    def _L0_conv_setup():
        import jax, jax.numpy as jnp
        import numpy as np
        EPS = 1e-05

        def _ln(x, g, b):
            m = jnp.mean(x, -1, keepdims=True)
            v = jnp.mean((x - m) ** 2, -1, keepdims=True)
            return (x - m) * jax.lax.rsqrt(v + EPS) * g + b
        key = jax.random.key(seed)
        ks = jax.random.split(key, 8)
        B, C, H, W = (4, 256, 32, 32)
        Di = 2 * C
        N = 16
        R = C // 16
        return {'x': jax.random.normal(ks[0], (B, C, H, W), jnp.float32), 'ln_g': jnp.ones((C,), jnp.float32), 'ln_b': jnp.zeros((C,), jnp.float32), 'w_in': jax.random.normal(ks[1], (C, 2 * Di), jnp.float32) / np.sqrt(C).astype(np.float32), 'w_conv': jax.random.normal(ks[2], (Di, 1, 3, 3), jnp.float32) / 3.0, 'b_conv': jnp.zeros((Di,), jnp.float32), 'w_xproj': jax.random.normal(ks[3], (4, R + 2 * N, Di), jnp.float32) / np.sqrt(Di).astype(np.float32), 'w_dt': jax.random.normal(ks[4], (4, Di, R), jnp.float32) / np.sqrt(R).astype(np.float32), 'b_dt': jnp.log(jnp.expm1(0.01 * jnp.ones((4, Di), jnp.float32))), 'A_log': jnp.log(jnp.tile(jnp.arange(1, N + 1, dtype=jnp.float32), (4, Di, 1))), 'Ds': jnp.ones((4, Di), jnp.float32), 'onorm_g': jnp.ones((Di,), jnp.float32), 'onorm_b': jnp.zeros((Di,), jnp.float32), 'w_out': jax.random.normal(ks[5], (Di, C), jnp.float32) / np.sqrt(Di).astype(np.float32)}
    _L0_conv_all = _L0_conv_setup()
    _L0_conv_in = {k: v for k, v in _L0_conv_all.items() if k in ('ln_g', 'ln_b', 'w_in', 'w_conv', 'b_conv', 'w_xproj', 'w_dt', 'b_dt', 'A_log', 'Ds', 'onorm_g', 'onorm_b', 'w_out', )}
    del _L0_conv_all

    def _L0_ffn_setup():
        import jax, jax.numpy as jnp
        import numpy as np
        BN_EPS = 0.001

        def _bn(h, g, b, m, v):
            return g * (h - m) * jax.lax.rsqrt(v + BN_EPS) + b
        key = jax.random.key(seed)
        ks = jax.random.split(key, 8)
        B, F, Df = (256, 64, 256)
        E, H, D = (8, 256, 256)
        s1 = 1.0 / np.sqrt(Df)
        s2 = 1.0 / np.sqrt(H)
        return {'x': jax.random.normal(ks[0], (B, F, Df), jnp.float32), 'Wr': jax.random.normal(ks[1], (Df, E), jnp.float32) * s1, 'br': jnp.zeros((E,), jnp.float32), 'W1': jax.random.normal(ks[2], (E, Df, H), jnp.float32) * s1, 'b1': jnp.zeros((E, H), jnp.float32), 'g1': jnp.ones((E, H), jnp.float32), 'be1': jnp.zeros((E, H), jnp.float32), 'm1': jnp.zeros((E, H), jnp.float32), 'v1': jnp.ones((E, H), jnp.float32), 'W2': jax.random.normal(ks[3], (E, H, H), jnp.float32) * s2, 'b2': jnp.zeros((E, H), jnp.float32), 'g2': jnp.ones((E, H), jnp.float32), 'be2': jnp.zeros((E, H), jnp.float32), 'm2': jnp.zeros((E, H), jnp.float32), 'v2': jnp.ones((E, H), jnp.float32), 'Wo': jax.random.normal(ks[4], (E, H, D), jnp.float32) * s2, 'bo': jnp.zeros((E, D), jnp.float32)}
    _L0_ffn_all = _L0_ffn_setup()
    _L0_ffn_in = {k: v for k, v in _L0_ffn_all.items() if k in ('Wr', 'br', 'W1', 'b1', 'g1', 'be1', 'm1', 'v1', 'W2', 'b2', 'g2', 'be2', 'm2', 'v2', 'Wo', 'bo', )}
    del _L0_ffn_all

    def _L1_conv_setup():
        import jax, jax.numpy as jnp
        import numpy as np
        HEIGHT = 128
        WIDTH = 128

        def dct_filter(n: int) -> jnp.ndarray:
            v = jnp.arange(n, dtype=jnp.float32)[:, None]
            j = jnp.arange(n, dtype=jnp.float32)[None, :]
            f = jnp.cos(jnp.pi * (0.5 + j) * v / n) / jnp.sqrt(jnp.float32(n))
            scale = jnp.where(v != 0, jnp.sqrt(jnp.float32(2.0)), jnp.float32(1.0))
            return f * scale
        key = jax.random.key(seed)
        x = jax.random.normal(key, (16, 256, HEIGHT, WIDTH), dtype=jnp.float32)
        return {'x': x}
    _L1_conv_all = _L1_conv_setup()
    _L1_conv_in = {k: v for k, v in _L1_conv_all.items() if k in ()}
    del _L1_conv_all

    def _L1_ffn_setup():
        import jax, jax.numpy as jnp
        import numpy as np
        N_EXPERTS = 8
        TOP_K = 2
        key = jax.random.key(seed)
        ks = jax.random.split(key, 5)
        B, T, C, E, H = (8, 2048, 256, 8, 682)
        scale = 1.0 / np.sqrt(C)
        return {'x': jax.random.normal(ks[0], (B, T, C), dtype=jnp.float32), 'router_w': jax.random.normal(ks[1], (E, C), dtype=jnp.float32) * scale, 'w1': jax.random.normal(ks[2], (E, H, C), dtype=jnp.float32) * scale, 'w2': jax.random.normal(ks[3], (E, C, H), dtype=jnp.float32) * (1.0 / np.sqrt(H)), 'w3': jax.random.normal(ks[4], (E, H, C), dtype=jnp.float32) * scale}
    _L1_ffn_all = _L1_ffn_setup()
    _L1_ffn_in = {k: v for k, v in _L1_ffn_all.items() if k in ('router_w', 'w1', 'w2', 'w3', )}
    del _L1_ffn_all

    return {
        "x": x,
        "L0_conv_ln_g": _L0_conv_in["ln_g"],
        "L0_conv_ln_b": _L0_conv_in["ln_b"],
        "L0_conv_w_in": _L0_conv_in["w_in"],
        "L0_conv_w_conv": _L0_conv_in["w_conv"],
        "L0_conv_b_conv": _L0_conv_in["b_conv"],
        "L0_conv_w_xproj": _L0_conv_in["w_xproj"],
        "L0_conv_w_dt": _L0_conv_in["w_dt"],
        "L0_conv_b_dt": _L0_conv_in["b_dt"],
        "L0_conv_A_log": _L0_conv_in["A_log"],
        "L0_conv_Ds": _L0_conv_in["Ds"],
        "L0_conv_onorm_g": _L0_conv_in["onorm_g"],
        "L0_conv_onorm_b": _L0_conv_in["onorm_b"],
        "L0_conv_w_out": _L0_conv_in["w_out"],
        "L0_ffn_Wr": _L0_ffn_in["Wr"],
        "L0_ffn_br": _L0_ffn_in["br"],
        "L0_ffn_W1": _L0_ffn_in["W1"],
        "L0_ffn_b1": _L0_ffn_in["b1"],
        "L0_ffn_g1": _L0_ffn_in["g1"],
        "L0_ffn_be1": _L0_ffn_in["be1"],
        "L0_ffn_m1": _L0_ffn_in["m1"],
        "L0_ffn_v1": _L0_ffn_in["v1"],
        "L0_ffn_W2": _L0_ffn_in["W2"],
        "L0_ffn_b2": _L0_ffn_in["b2"],
        "L0_ffn_g2": _L0_ffn_in["g2"],
        "L0_ffn_be2": _L0_ffn_in["be2"],
        "L0_ffn_m2": _L0_ffn_in["m2"],
        "L0_ffn_v2": _L0_ffn_in["v2"],
        "L0_ffn_Wo": _L0_ffn_in["Wo"],
        "L0_ffn_bo": _L0_ffn_in["bo"],
        "L1_ffn_router_w": _L1_ffn_in["router_w"],
        "L1_ffn_w1": _L1_ffn_in["w1"],
        "L1_ffn_w2": _L1_ffn_in["w2"],
        "L1_ffn_w3": _L1_ffn_in["w3"],
    }

def reference(x, L0_conv_ln_g, L0_conv_ln_b, L0_conv_w_in, L0_conv_w_conv, L0_conv_b_conv, L0_conv_w_xproj, L0_conv_w_dt, L0_conv_b_dt, L0_conv_A_log, L0_conv_Ds, L0_conv_onorm_g, L0_conv_onorm_b, L0_conv_w_out, L0_ffn_Wr, L0_ffn_br, L0_ffn_W1, L0_ffn_b1, L0_ffn_g1, L0_ffn_be1, L0_ffn_m1, L0_ffn_v1, L0_ffn_W2, L0_ffn_b2, L0_ffn_g2, L0_ffn_be2, L0_ffn_m2, L0_ffn_v2, L0_ffn_Wo, L0_ffn_bo, L1_ffn_router_w, L1_ffn_w1, L1_ffn_w2, L1_ffn_w3):
    import jax
    import jax.numpy as jnp
    def _L0_conv_ref(x, ln_g, ln_b, w_in, w_conv, b_conv, w_xproj, w_dt, b_dt, A_log, Ds, onorm_g, onorm_b, w_out):
        import jax, jax.numpy as jnp
        import numpy as np
        EPS = 1e-05

        def _ln(x, g, b):
            m = jnp.mean(x, -1, keepdims=True)
            v = jnp.mean((x - m) ** 2, -1, keepdims=True)
            return (x - m) * jax.lax.rsqrt(v + EPS) * g + b
        B, C, H, W = x.shape
        Di = w_conv.shape[0]
        K = 4
        R = w_dt.shape[2]
        N = A_log.shape[2]
        L = H * W
        xt = jnp.transpose(x, (0, 2, 3, 1))
        resid = xt
        xn = _ln(xt, ln_g, ln_b)
        xz = xn @ w_in
        xin, z = jnp.split(xz, 2, axis=-1)
        xc = jnp.transpose(xin, (0, 3, 1, 2))
        xc = jax.lax.conv_general_dilated(xc, w_conv, (1, 1), 'SAME', feature_group_count=Di, dimension_numbers=('NCHW', 'OIHW', 'NCHW'))
        xc = jax.nn.silu(xc + b_conv[None, :, None, None])
        x0 = xc.reshape(B, Di, L)
        x1 = jnp.transpose(xc, (0, 1, 3, 2)).reshape(B, Di, L)
        xhw = jnp.stack([x0, x1], axis=1)
        xs = jnp.concatenate([xhw, jnp.flip(xhw, -1)], axis=1)
        xdbl = jnp.einsum('bkdl,kcd->bkcl', xs, w_xproj)
        dts = xdbl[:, :, :R]
        Bs = xdbl[:, :, R:R + N]
        Cs = xdbl[:, :, R + N:]
        dt = jnp.einsum('bkrl,kdr->bkdl', dts, w_dt) + b_dt[None, :, :, None]
        dt = jax.nn.softplus(dt)
        A = -jnp.exp(A_log)

        def step(h, inp):
            x_l, dt_l, B_l, C_l = inp
            da = jnp.exp(dt_l[..., None] * A)
            h = da * h + (dt_l * x_l)[..., None] * B_l[:, :, None, :]
            y = jnp.einsum('bkdn,bkn->bkd', h, C_l)
            return (h, y)
        h0 = jnp.zeros((B, K, Di, N), x.dtype)
        _, ys = jax.lax.scan(step, h0, (jnp.moveaxis(xs, -1, 0), jnp.moveaxis(dt, -1, 0), jnp.moveaxis(Bs, -1, 0), jnp.moveaxis(Cs, -1, 0)))
        ys = jnp.moveaxis(ys, 0, -1)
        ys = ys + Ds[None, :, :, None] * xs

        def untr(y):
            return jnp.transpose(y.reshape(B, Di, W, H), (0, 1, 3, 2)).reshape(B, Di, L)
        y = ys[:, 0] + untr(ys[:, 1]) + jnp.flip(ys[:, 2], -1) + untr(jnp.flip(ys[:, 3], -1))
        y = jnp.transpose(y.reshape(B, Di, H, W), (0, 2, 3, 1))
        y = _ln(y, onorm_g, onorm_b)
        y = y * jax.nn.silu(z)
        out = resid + y @ w_out
        return jnp.transpose(out, (0, 3, 1, 2))

    def _L0_ffn_ref(x, Wr, br, W1, b1, g1, be1, m1, v1, W2, b2, g2, be2, m2, v2, Wo, bo):
        import jax, jax.numpy as jnp
        import numpy as np
        BN_EPS = 0.001

        def _bn(h, g, b, m, v):
            return g * (h - m) * jax.lax.rsqrt(v + BN_EPS) + b
        feat = jnp.mean(x, axis=0)
        w = jax.nn.softmax(feat @ Wr + br, axis=-1)
        h = jnp.einsum('bfd,edh->bfeh', x, W1) + b1
        h = jax.nn.relu(_bn(h, g1, be1, m1, v1))
        h = jnp.einsum('bfeh,ehk->bfek', h, W2) + b2
        h = jax.nn.relu(_bn(h, g2, be2, m2, v2))
        y = jnp.einsum('bfeh,ehd->bfed', h, Wo) + bo
        return jnp.einsum('bfed,fe->bfd', y, w)

    def _L1_conv_ref(x):
        import jax, jax.numpy as jnp
        import numpy as np
        HEIGHT = 128
        WIDTH = 128

        def dct_filter(n: int) -> jnp.ndarray:
            v = jnp.arange(n, dtype=jnp.float32)[:, None]
            j = jnp.arange(n, dtype=jnp.float32)[None, :]
            f = jnp.cos(jnp.pi * (0.5 + j) * v / n) / jnp.sqrt(jnp.float32(n))
            scale = jnp.where(v != 0, jnp.sqrt(jnp.float32(2.0)), jnp.float32(1.0))
            return f * scale
        B, C, H, W = x.shape
        Wx = dct_filter(W)
        Wy = dct_filter(H)
        y = jnp.einsum('bchw,vw->bchv', x, Wx)
        out = jnp.einsum('bchv,kh->bckv', y, Wy)
        return out

    def _L1_ffn_ref(x, router_w, w1, w2, w3):
        import jax, jax.numpy as jnp
        import numpy as np
        N_EXPERTS = 8
        TOP_K = 2
        B, T, C = x.shape
        flat = x.reshape(-1, C)
        logits = flat @ router_w.T
        probs = jax.nn.softmax(logits, axis=-1)
        topk_probs, topk_idx = jax.lax.top_k(probs, TOP_K)
        topk_probs = topk_probs / (jnp.sum(topk_probs, axis=-1, keepdims=True) + 1e-09)
        onehot = jax.nn.one_hot(topk_idx, N_EXPERTS, dtype=flat.dtype)
        gates = jnp.einsum('nk,nke->ne', topk_probs, onehot)
        h1 = jnp.einsum('nc,ehc->neh', flat, w1)
        h3 = jnp.einsum('nc,ehc->neh', flat, w3)
        h = jax.nn.silu(h1) * h3
        y = jnp.einsum('neh,ech->nec', h, w2)
        out = jnp.einsum('ne,nec->nc', gates, y)
        return out.reshape(B, T, C)

    def _gn(v, G=32, eps=1e-5):
        B_, C_, H_, W_ = v.shape
        g = v.reshape(B_, G, C_ // G, H_, W_)
        m = jnp.mean(g, axis=(2, 3, 4), keepdims=True)
        s = jnp.var(g, axis=(2, 3, 4), keepdims=True)
        return ((g - m) / jnp.sqrt(s + eps)).reshape(v.shape)

    def _ln_c(v, eps=1e-6):
        m = jnp.mean(v, axis=1, keepdims=True)
        s = jnp.var(v, axis=1, keepdims=True)
        return (v - m) / jnp.sqrt(s + eps)

    def _ln_t(v, eps=1e-5):
        m = jnp.mean(v, axis=-1, keepdims=True)
        s = jnp.var(v, axis=-1, keepdims=True)
        return (v - m) / jnp.sqrt(s + eps)

    def _to_tokens(v):
        B_, C_, H_, W_ = v.shape
        return v.reshape(B_, C_, H_ * W_).transpose(0, 2, 1)
    def _from_tokens(t, like):
        B_, C_, H_, W_ = like.shape
        return t.transpose(0, 2, 1).reshape(B_, C_, H_, W_)

    x = x + _L0_conv_ref(_ln_c(x), L0_conv_ln_g, L0_conv_ln_b, L0_conv_w_in, L0_conv_w_conv, L0_conv_b_conv, L0_conv_w_xproj, L0_conv_w_dt, L0_conv_b_dt, L0_conv_A_log, L0_conv_Ds, L0_conv_onorm_g, L0_conv_onorm_b, L0_conv_w_out)
    t = _to_tokens(x)
    t = t + _L0_ffn_ref(_ln_t(t), L0_ffn_Wr, L0_ffn_br, L0_ffn_W1, L0_ffn_b1, L0_ffn_g1, L0_ffn_be1, L0_ffn_m1, L0_ffn_v1, L0_ffn_W2, L0_ffn_b2, L0_ffn_g2, L0_ffn_be2, L0_ffn_m2, L0_ffn_v2, L0_ffn_Wo, L0_ffn_bo)
    x = _from_tokens(t, x)
    x = x + _L1_conv_ref(_ln_c(x))
    t = _to_tokens(x)
    t = t + _L1_ffn_ref(_ln_t(t), L1_ffn_router_w, L1_ffn_w1, L1_ffn_w2, L1_ffn_w3)
    x = _from_tokens(t, x)
    return x


_drawn_inputs = setup_inputs


def setup_inputs(seed=0):
    import zlib

    import numpy as np

    out = dict(_drawn_inputs(seed))
    spreads = {'L0_conv_ln_g': (1.0, 0.2),
     'L0_conv_ln_b': (0.0, 0.1),
     'L0_conv_b_conv': (0.0, 0.1),
     'L0_conv_b_dt': (-4.600166320800781, 0.6),
     'L0_conv_Ds': (1.0, 0.2),
     'L0_conv_onorm_g': (1.0, 0.2),
     'L0_conv_onorm_b': (0.0, 0.1),
     'L0_ffn_br': (0.0, 0.321),
     'L0_ffn_b1': (0.0, 0.428),
     'L0_ffn_g1': (1.0, 0.2),
     'L0_ffn_be1': (0.0, 0.446),
     'L0_ffn_m1': (0.0, 0.417),
     'L0_ffn_v1': (1.0, 0.6),
     'L0_ffn_b2': (0.0, 0.348),
     'L0_ffn_g2': (1.0, 0.2),
     'L0_ffn_be2': (0.0, 0.36),
     'L0_ffn_m2': (0.0, 0.34),
     'L0_ffn_v2': (1.0, 0.6),
     'L0_ffn_bo': (0.0, 0.274)}
    factors = {'L0_conv_w_dt': 3.16, 'L0_conv_A_log': 3.226}
    for name, (base, spread) in spreads.items():
        noise = np.random.default_rng([zlib.crc32(name.encode()), seed]).standard_normal(out[name].shape)
        drawn = base * np.exp(spread * noise) if base else spread * noise
        out[name] = jnp.asarray(drawn.astype(out[name].dtype))
    for name, factor in factors.items():
        out[name] = (out[name] * factor).astype(out[name].dtype)
    return out
```

```python
import concourse.bass as bass
from concourse import mybir
from contextlib import ExitStack
F32 = mybir.dt.float32
BF16 = mybir.dt.bfloat16
ALU = mybir.AluOpType
ACT = mybir.ActivationFunctionType
AX_X = mybir.AxisListType.X
P = 128
B, C, H, W = 4, 256, 32, 32
L = H * W
DI = 2 * C
DB = DI // P
NST = 16
NE = 8
R = C // 16


def front_stage(nc, x_d, win_d, lng_d, wconv_d, bconv_d, ident_d, xu_d, xc_d, sz_d):
    CB = C // P
    WP = W + 2
    FREE = 16
    with ExitStack() as ctx:
        def sb(name, shape, dt=F32):
            return ctx.enter_context(nc.sbuf_tensor("fr_" + name, shape, dt))

        def ps(name, shape):
            return ctx.enter_context(nc.psum_tensor("fr_" + name, shape, F32))

        def sem(name):
            return ctx.enter_context(nc.semaphore("fr_" + name))

        x = sb("x", [P, CB, L])
        xm = sb("xm", [P, CB, L])
        sq = sb("sq", [P, CB, L])
        u = sb("u", [P, CB, L])
        xu = sb("xu", [P, CB, L])
        xn = sb("xn", [P, CB, L])
        sd = sb("sd", [P, L // P])
        rs = sb("rs", [P, L // P])
        dg = sb("dg", [P, L // P, P])
        win = sb("win", [P, CB, 2 * DI])
        lng = sb("lng", [P, CB, 2])
        wcv = sb("wcv", [P, DB, 9])
        bcv = sb("bcv", [P, DB])
        ident = sb("ident", [P, P])
        ones = sb("ones", [P, P])
        mean = sb("mean", [P, P])
        eps = sb("eps", [P, 2])
        dconv = sb("dconv", [P, DB, 9, P])
        xpad = sb("xpad", [P, DB, H + 2, WP])
        xco = sb("xco", [P, DB, L])
        sz = sb("sz", [P, DB, L])
        stp = ps("stp", [P, 2, L // 2])
        vap = ps("vap", [P, L // P])
        xip = ps("xip", [P, L // 2])
        zp = ps("zp", [P, L // 2])
        cvp = ps("cvp", [P, 2, L // 2])

        s_w, s_x, s_cst, s_dcv = sem("weights_in"), sem("x_in"), sem("consts"), sem("taps_built")
        s_mean, s_xm, s_sq, s_var = sem("mean"), sem("centred"), sem("squared"), sem("var")
        s_sd, s_rs, s_dg, s_rb, s_nrm = sem("dev"), sem("rdev"), sem("rdev_diag"), sem("rdev_bcast"), sem("normed")
        s_xu, s_xust, s_xn = sem("xu"), sem("xu_stored"), sem("xn")
        s_pxi, s_xi, s_pz, s_z, s_szst = (sem("xin_psum"), sem("xin"), sem("z_psum"), sem("z"), sem("sz_stored"))
        s_pad = sem("border_zeroed")
        s_pcv, s_xc, s_xcst = sem("conv_psum"), sem("xc"), sem("xc_stored")

        def halves(ap):
            return ap.rearrange("p (h l) -> p h l", h=2)

        block = ctx.enter_context(nc.Block())

        def rounds(eng, body):
            body(0, True, False)
            with eng.Fori(1, B) as i:
                body(i, True, True)
            body(B, False, True)

        @block.sync
        def _(sp):
            for dst, s in ((win, win_d), (lng, lng_d), (wcv, wconv_d), (bcv, bconv_d), (ident, ident_d)):
                sp.dma_start(dst[:], s).then_inc(s_w, 16)
            sp.sem_inc(s_xust, FREE)
            sp.sem_inc(s_xcst, FREE)
            sp.sem_inc(s_szst, FREE)
            sp.dma_start(x[:], x_d[0]).then_inc(s_x, 16)

            def body(i, front, conv):
                if front:
                    sp.wait_ge(s_xu, i + 1)
                    sp.dma_start(xu_d[i], xu[:]).then_inc(s_xust, 16)
                    if not (isinstance(i, int) and i == B - 1):
                        nxt = i + 1
                        sp.dma_start(x[:], x_d[nxt]).then_inc(s_x, 16)
                if conv:
                    sp.wait_ge(s_xc, 2 * DB * i + FREE)
                    sp.dma_start(xc_d[i - 1], xco[:]).then_inc(s_xcst, 16)
                if front:
                    sp.wait_ge(s_z, 2 * DB * i + 2 * DB + FREE)
                    sp.dma_start(sz_d[i], sz[:]).then_inc(s_szst, 16)
            body(0, True, False)
            with sp.Fori(1, B - 1) as i:
                body(i, True, True)
            body(B - 1, True, True)
            body(B, False, True)
            sp.wait_ge(s_xust, 16 * B + FREE)
            sp.wait_ge(s_xcst, 16 * B + FREE)
            sp.wait_ge(s_szst, 16 * B + FREE)

        @block.tensor
        def _(pe):
            def means(i, r, t):
                for h in range(2):
                    for c in range(CB):
                        mm = pe.matmul(stp[:, h, :], mean[:], halves(t[:, c, :])[:, h, :],
                                       start=(c == 0), stop=(c == CB - 1))
                mm.then_inc(s_mean, 1)

            def variances(i, r):
                pe.wait_ge(s_sq, 2 * i + r + 1)
                for t in range(L // P):
                    for c in range(CB):
                        mm = pe.matmul(vap[:, t:t + 1], sq[:, c, t * P:(t + 1) * P], mean[:, 0:1],
                                       start=(c == 0), stop=(c == CB - 1))
                mm.then_inc(s_var, 1)

            def spread(i, r):
                pe.wait_ge(s_dg, 2 * i + r + 1)
                for t in range(L // P):
                    mm = pe.matmul(stp[:, t // 4, t % 4 * P:(t % 4 + 1) * P], ones[:], dg[:, t, :],
                                   start=True, stop=True)
                mm.then_inc(s_rb, 1)

            def project(i):
                pe.wait_ge(s_xn, 2 * i + 2)
                for v in range(2 * DB):
                    d, h = v // 2, v % 2
                    pe.wait_ge(s_xi, 2 * DB * i + v + FREE)
                    for c in range(CB):
                        mm = pe.matmul(xip[:], win[:, c, d * P:(d + 1) * P], halves(xn[:, c, :])[:, h, :],
                                       start=(c == 0), stop=(c == CB - 1))
                    mm.then_inc(s_pxi, 1)
                    pe.wait_ge(s_z, 2 * DB * i + v + FREE)
                    for c in range(CB):
                        mm = pe.matmul(zp[:], win[:, c, DI + d * P:DI + (d + 1) * P], halves(xn[:, c, :])[:, h, :],
                                       start=(c == 0), stop=(c == CB - 1))
                    mm.then_inc(s_pz, 1)

            def convolve(i, c):
                for h in range(2):
                    pe.wait_ge(s_xc, 2 * DB * (i - 1) + 2 * c + h - 1 + FREE)
                    for t in range(9):
                        r0 = t // 3 + h * (H // 2)
                        mm = pe.matmul(cvp[:, h, :], dconv[:, c, t, :],
                                       xpad[:, c, r0:r0 + H // 2, t % 3:t % 3 + W], start=(t == 0), stop=(t == 8))
                    mm.then_inc(s_pcv, 1)

            def body(i, front, conv):
                if front:
                    pe.wait_ge(s_x, 16 * i + 16)
                    means(i, 0, x)
                if conv:
                    pe.wait_ge(s_xi, 2 * DB * i + FREE)
                    convolve(i, 0)
                if front:
                    variances(i, 0)
                if conv:
                    convolve(i, 1)
                if front:
                    spread(i, 0)
                if conv:
                    convolve(i, 2)
                if front:
                    pe.wait_ge(s_nrm, 2 * i + 1)
                    means(i, 1, u)
                if conv:
                    convolve(i, 3)
                if front:
                    variances(i, 1)
                    spread(i, 1)
                    project(i)
            pe.wait_ge(s_w, 16 * 5)
            pe.wait_ge(s_cst, 3)
            pe.wait_ge(s_dcv, 1)
            rounds(pe, body)

        @block.scalar
        def _(act):
            act.sem_inc(s_z, FREE)
            act.sem_inc(s_xc, FREE)

            def square(i, r):
                act.wait_ge(s_xm, 2 * i + r + 1)
                act.activation(sq[:], xm[:], ACT.Square).then_inc(s_sq, 1)

            def deviation(i, r):
                act.wait_ge(s_var, 2 * i + r + 1)
                act.activation(sd[:], vap[:], ACT.Sqrt, bias=eps[:, r:r + 1]).then_inc(s_sd, 1)

            def gate(i):
                act.wait_ge(s_szst, 16 * i + FREE)
                for v in range(2 * DB):
                    act.wait_ge(s_pz, 2 * DB * i + v + 1)
                    act.activation(halves(sz[:, v // 2, :])[:, v % 2, :], zp[:], ACT.Silu).then_inc(s_z, 1)

            def conv_out(i, c):
                if c == 0:
                    act.wait_ge(s_xcst, 16 * i)
                for h in range(2):
                    act.wait_ge(s_pcv, 2 * DB * (i - 1) + 2 * c + h + 1)
                    act.activation(halves(xco[:, c, :])[:, h, :], cvp[:, h, :], ACT.Silu,
                                   bias=bcv[:, c:c + 1]).then_inc(s_xc, 1)

            def body(i, front, conv):
                if front:
                    square(i, 0)
                if conv:
                    conv_out(i, 0)
                if front:
                    deviation(i, 0)
                if conv:
                    conv_out(i, 1)
                    conv_out(i, 2)
                if front:
                    square(i, 1)
                if conv:
                    conv_out(i, 3)
                if front:
                    deviation(i, 1)
                    gate(i)
            act.wait_ge(s_w, 16 * 5)
            act.wait_ge(s_cst, 3)
            rounds(act, body)

        @block.gpsimd
        def _(pool):
            pool.memset(ones[:], 1.0).then_inc(s_cst, 1)
            pool.memset(mean[:], 1.0 / C).then_inc(s_cst, 1)
            pool.memset(eps[:, 0:1], 1e-6)
            pool.memset(eps[:, 1:2], 1e-5).then_inc(s_cst, 1)

            def body(i):
                pool.wait_ge(s_xust, 16 * i + FREE)
                pool.wait_ge(s_nrm, 2 * i + 1)
                pool.tensor_tensor(xu[:], x[:], u[:], ALU.add).then_inc(s_xu, 1)
            with pool.Fori(0, B) as i:
                body(i)

        @block.vector
        def _(dve):
            dve.sem_inc(s_xi, FREE)

            def centre(i, r, t):
                dve.wait_ge(s_mean, 2 * i + r + 1)
                for c in range(CB):
                    op = dve.tensor_tensor(halves(xm[:, c, :]), halves(t[:, c, :]), stp[:], ALU.subtract)
                op.then_inc(s_xm, 1)

            def rdev(i, r):
                dve.wait_ge(s_sd, 2 * i + r + 1)
                dve.reciprocal(rs[:], sd[:]).then_inc(s_rs, 1)
                dve.wait_ge(s_rs, 2 * i + r + 1)
                for t in range(L // P):
                    op = dve.tensor_scalar(dg[:, t, :], ident[:], rs[:, t:t + 1], None, ALU.mult)
                op.then_inc(s_dg, 1)

            def scale(i, r, t):
                dve.wait_ge(s_rb, 2 * i + r + 1)
                for c in range(CB):
                    op = dve.tensor_tensor(halves(t[:, c, :]), halves(xm[:, c, :]), stp[:], ALU.mult)
                op.then_inc(s_nrm, 1)

            def body(i):
                centre(i, 0, x)
                rdev(i, 0)
                scale(i, 0, u)
                centre(i, 1, u)
                rdev(i, 1)
                scale(i, 1, xn)
                dve.wait_ge(s_nrm, 2 * i + 2)
                for c in range(CB):
                    dve.tensor_scalar(xn[:, c, :], xn[:, c, :], lng[:, c, 0:1], lng[:, c, 1:2],
                                      ALU.mult, ALU.add).then_inc(s_xn, 1)
                for v in range(2 * DB):
                    d, h = v // 2, v % 2
                    dve.wait_ge(s_pxi, 2 * DB * i + v + 1)
                    dve.tensor_copy(xpad[:, d, 1 + h * (H // 2):1 + (h + 1) * (H // 2), 1:1 + W],
                                    xip[:].rearrange("p (a b) -> p a b", b=W)).then_inc(s_xi, 1)
            dve.memset(xpad[:], 0.0).then_inc(s_pad, 1)
            dve.wait_ge(s_w, 16 * 5)
            for c in range(DB):
                for t in range(9):
                    op = dve.tensor_scalar(dconv[:, c, t, :], ident[:], wcv[:, c, t:t + 1], None, ALU.mult)
            op.then_inc(s_dcv, 1)
            dve.wait_ge(s_pad, 1)
            with dve.Fori(0, B) as i:
                body(i)


def scan_stage(nc, xc_d, wx_d, wdt_d, bdt_d, alog_d, ds_d, sel_d, ident_d, ysum_d):
    KORDER = (0, 2, 1, 3)
    HALF = L // 2
    GROUPS = 4 * 2 * 2
    STEPS = GROUPS * NST
    FREE_H, FREE_HC, FREE_NS, FREE_DB, FREE_DR, FREE_Y = 4, 4, 4, 4, 2, 16
    with ExitStack() as ctx:
        def sb(name, shape, dt=F32):
            return ctx.enter_context(nc.sbuf_tensor("sc_" + name, shape, dt))

        def ps(name, shape):
            return ctx.enter_context(nc.psum_tensor("sc_" + name, shape, F32))

        def sem(name):
            return ctx.enter_context(nc.semaphore("sc_" + name))

        xc = sb("xc", [P, DB, L])
        xct = sb("xct", [P, DB, L])
        yacc = sb("yacc", [P, DB, L])
        wx = sb("wx", [P, 4, DB, P])
        wdt = sb("wdt", [P, 4, DI])
        bdt = sb("bdt", [P, 4, DB])
        nega = sb("nega", [P, 4, DB, NST])
        ds4 = sb("ds4", [P, DB, 4])
        dsum = sb("dsum", [P, DB])
        sel = sb("sel", [96, 2 * NST, P], BF16)
        ident = sb("ident", [P, P])
        xdbl = sb("xdbl", [P, HALF])
        rest = sb("rest", [96, HALF])
        bcs = sb("bcs", [96, 2, HALF], BF16)
        ab = sb("ab", [P, 2, HALF])
        rl = sb("rl", [P, 2, HALF])
        dt = sb("dt", [P, 2, 2, HALF])
        dtx = sb("dtx", [P, 2, 2, HALF])
        bsb = sb("bsb", [P, 2, HALF])
        dbx = sb("dbx", [P, 4, HALF])
        hst = sb("hst", [P, 2, NST, HALF])
        hc = sb("hc", [P, 4, HALF])
        yps = ps("yps", [P, 2, HALF])
        dap = ps("dap", [P, 2, HALF])
        cps = ps("cps", [P, 2, HALF])
        bps = ps("bps", [P, HALF])
        pps = ps("pps", [P, HALF])

        s_w, s_xc, s_yst, s_pass = sem("weights_in"), sem("xc_in"), sem("y_stored"), sem("passed")
        s_aexp, s_cst, s_xct = sem("a_exp"), sem("consts"), sem("xct_built")
        s_xp, s_xd, s_bcs = sem("xproj"), sem("xdbl"), sem("bcs_split")
        s_dtp, s_dtr, s_ab, s_e, s_ln = sem("dt_pre"), sem("dt_read"), sem("dt_abs"), sem("dt_exp"), sem("dt_ln")
        s_part1, s_rest, s_part2 = sem("part1"), sem("rest"), sem("part2")
        s_dt, s_dtx = sem("dt"), sem("dtx")
        s_bB, s_bc, s_cC = sem("b_bcast"), sem("b_copied"), sem("c_bcast")
        s_da, s_db, s_h, s_hc, s_ns, s_dr = (sem("da"), sem("dbx"), sem("scanned"), sem("hc"), sem("nsum"),
                                             sem("drained"))

        def info(gs):
            k, dp, half = KORDER[gs // 4], gs // 2 % 2, gs % 2
            mem_half = half if k < 2 else 1 - half
            return k, dp, half, mem_half

        def span(gs):
            m = info(gs)[3]
            return slice(m * HALF, (m + 1) * HALF)

        def src(gs):
            return xc if info(gs)[0] in (0, 2) else xct

        def segment(eng, lo, hi, body):
            if hi - lo == 1:
                body(lo)
            elif hi > lo:
                with eng.Fori(lo, hi) as p:
                    body(p)

        def batches(eng, image):
            with eng.Fori(0, B - 1) as b:
                image(b, False)
            image(B - 1, True)

        block = ctx.enter_context(nc.Block())

        @block.sync
        def _(sp):
            sp.sem_inc(s_yst, FREE_Y)
            for dst, s in ((wx, wx_d), (wdt, wdt_d), (bdt, bdt_d), (nega, alog_d), (ds4, ds_d),
                           (sel, sel_d), (ident, ident_d)):
                sp.dma_start(dst[:], s).then_inc(s_w, 16)
            sp.dma_start(xc[:], xc_d[0]).then_inc(s_xc, 16)

            def image(b, last):
                g = b * GROUPS
                if not last:
                    sp.wait_ge(s_xp, g + 8)
                    sp.wait_ge(s_dtx, g + 8)
                    sp.wait_ge(s_dr, 2 * g + 8 + FREE_DR)
                    sp.wait_ge(s_xct, 4 * b + 4)
                    sp.wait_ge(s_w, 16)
                    sp.dma_start(xc[:], xc_d[b + 1]).then_inc(s_xc, 16)
                sp.wait_ge(s_dr, 2 * g + 2 * GROUPS + FREE_DR)
                sp.wait_ge(s_w, 16)
                sp.dma_start(ysum_d[b], yacc[:]).then_inc(s_yst, 16)
            batches(sp, image)
            sp.wait_ge(s_yst, 16 * B + FREE_Y)

        @block.tensor
        def _(pe):
            pe.sem_inc(s_ns, FREE_NS)

            def xproj(b, gs):
                k = info(gs)[0]
                g = b * GROUPS + gs
                if k in (0, 2):
                    pe.wait_ge(s_xc, 16 * b + 16)
                else:
                    pe.wait_ge(s_xct, 4 * b + 4)
                pe.wait_ge(s_dtr, 2 * g + 2)
                for c in range(DB):
                    mm = pe.matmul(pps[:], wx[:, k, c, :], src(gs)[:, c, span(gs)],
                                   start=(c == 0), stop=(c == DB - 1))
                mm.then_inc(s_xp, 1)

            def dt_rows(b, gs, j):
                k, dp, _, _ = info(gs)
                g = b * GROUPS + gs
                pe.wait_ge(s_xd, g + 1)
                if j == 1:
                    pe.wait_ge(s_dtr, 2 * g + 1 + 2)
                d0 = (2 * dp + j) * P
                pe.matmul(pps[:], wdt[:, k, d0:d0 + P], xdbl[:], start=True, stop=True).then_inc(s_dtp, 1)

            def bcast_b(g, gs, n):
                pe.wait_ge(s_bc, g * NST + n + 1)
                pe.wait_ge(s_cst, 1)
                pe.matmul(bps[:], sel[:, n, :], bcs[:, gs % 2, :], start=True, stop=True).then_inc(s_bB, 1)

            def bcast_c(g, gs, n, u):
                pe.wait_ge(s_hc, (g * NST + n) * 2 - 2 + FREE_HC)
                pe.wait_ge(s_cst, 1)
                pe.matmul(cps[:, u % 2, :], sel[:, n + NST, :], bcs[:, gs % 2, :],
                          start=True, stop=True).then_inc(s_cC, 1)

            def nsum(g, n, j, u, first, stop):
                pe.wait_ge(s_hc, (g * NST + n) * 2 + j + 1 + FREE_HC)
                pe.matmul(yps[:, j, :], ident[:], hc[:, 2 * (u % 2) + j, :], start=first, stop=stop,
                          skip_group_check=True).then_inc(s_ns, 1)

            def image(b, last):
                for gs in range(GROUPS):
                    g = b * GROUPS + gs
                    nb, ngs = (b, gs + 1) if gs + 1 < GROUPS else (b + 1, 0)
                    more = not (last and gs + 1 == GROUPS)

                    def pair(p, edge=False):
                        for u in range(2):
                            n = 2 * p + u
                            if not edge or n + 3 < NST:
                                bcast_b(g, gs, n + 3)
                            elif more:
                                if n + 3 == NST:
                                    pe.wait_ge(s_bcs, nb * GROUPS + ngs + 2)
                                bcast_b(nb * GROUPS + ngs, ngs, n + 3 - NST)
                            if not edge or n + 1 < NST:
                                bcast_c(g, gs, n + 1, u + 1)
                            elif more:
                                bcast_c(nb * GROUPS + ngs, ngs, 0, 0)
                            if edge and n == 0:
                                pe.wait_ge(s_dr, 2 * g + FREE_DR)
                            for j in range(2):
                                nsum(g, n, j, u, edge and n == 0, edge and n == NST - 1)
                    pair(0, True)
                    if more:
                        xproj(nb, ngs)
                    segment(pe, 1, 3, pair)
                    if more:
                        dt_rows(nb, ngs, 0)
                    segment(pe, 3, 5, pair)
                    if more:
                        dt_rows(nb, ngs, 1)
                    segment(pe, 5, 6, pair)
                    pair(6, True)
                    pair(7, True)

            pe.wait_ge(s_w, 16 * 7)
            xproj(0, 0)
            dt_rows(0, 0, 0)
            dt_rows(0, 0, 1)
            pe.wait_ge(s_bcs, 2)
            for n in range(3):
                bcast_b(0, 0, n)
            bcast_c(0, 0, 0, 0)
            batches(pe, image)

        @block.scalar
        def _(act):
            act.preload_act_table_set("natural_log_exp_and_others")
            act.sem_inc(s_dtr, 2)
            act.sem_inc(s_bc, 1)
            act.wait_ge(s_w, 16 * 7)
            act.activation(nega[:], nega[:], ACT.Exp).then_inc(s_aexp, 1)

            def xdbl_copy(b, gs, first=False):
                g = b * GROUPS + gs
                act.wait_ge(s_xp, g + 1)
                act.wait_ge(s_rest, g + 1)
                if not first:
                    act.wait_ge(s_cC, (g - 1) * NST + 1)
                act.activation(bcs[:, gs % 2, :], pps[0:96, :], ACT.Copy).then_inc(s_part1, 1)
                act.activation(xdbl[:], pps[:], ACT.Copy).then_inc(s_xd, 1)

            def second_part(b, gs):
                act.wait_ge(s_rest, b * GROUPS + gs + 2)
                for q in (32, 64):
                    act.activation(bcs[q:q + 32, gs % 2, :], rest[q:q + 32, :], ACT.Copy).then_inc(s_part2, 1)

            def abs_relu(b, gs, j):
                k, dp, _, _ = info(gs)
                g = b * GROUPS + gs
                bias = bdt[:, k, 2 * dp + j:2 * dp + j + 1]
                act.wait_ge(s_dtp, 2 * g + j + 1)
                act.wait_ge(s_dt, g + 1)
                act.activation(ab[:, j, :], pps[:], ACT.Abs, bias=bias).then_inc(s_ab, 1)
                act.activation(rl[:, j, :], pps[:], ACT.Relu, bias=bias).then_inc(s_dtr, 1)

            def exp_ln(b, gs):
                g = b * GROUPS + gs
                act.wait_ge(s_ab, 2 * g + 2)
                act.activation(ab[:], ab[:], ACT.Exp, scale=-1.0).then_inc(s_e, 1)
                act.wait_ge(s_e, g + 1)
                act.activation(ab[:], ab[:], ACT.Ln, bias=1.0).then_inc(s_ln, 1)

            def copy_b(g, n, u):
                act.wait_ge(s_bB, g * NST + n + 1)
                act.wait_ge(s_db, 2 * (g * NST + n) - 2 + FREE_DB)
                act.activation(bsb[:, u % 2, :], bps[:], ACT.Copy).then_inc(s_bc, 1)

            def decay(g, gs, n, j):
                k, dp, _, _ = info(gs)
                act.wait_ge(s_h, (g * NST + n) * 2 + j - 1 + FREE_H)
                act.wait_ge(s_cst, 1)
                act.activation(dap[:, j, :], dt[:, gs % 2, j, :], ACT.Exp,
                               scale=nega[:, k, 2 * dp + j, bass.ds(n, 1)]).then_inc(s_da, 1)

            def image(b, last):
                for gs in range(GROUPS):
                    g = b * GROUPS + gs
                    nb, ngs = (b, gs + 1) if gs + 1 < GROUPS else (b + 1, 0)
                    more = not (last and gs + 1 == GROUPS)

                    def pair(p, edge=False):
                        for u in range(2):
                            n = 2 * p + u
                            for j in range(2):
                                decay(g, gs, n, j)
                            if not edge or n + 2 < NST:
                                copy_b(g, n + 2, u)
                            elif more:
                                copy_b(nb * GROUPS + ngs, n + 2 - NST, u)
                    act.wait_ge(s_dt, g + 2)
                    segment(act, 0, 2, pair)
                    if more:
                        xdbl_copy(nb, ngs)
                    segment(act, 2, 4, pair)
                    if more:
                        abs_relu(nb, ngs, 0)
                        second_part(nb, ngs)
                    segment(act, 4, 6, pair)
                    if more:
                        abs_relu(nb, ngs, 1)
                        exp_ln(nb, ngs)
                    segment(act, 6, 7, pair)
                    pair(7, True)

            xdbl_copy(0, 0, True)
            second_part(0, 0)
            abs_relu(0, 0, 0)
            abs_relu(0, 0, 1)
            exp_ln(0, 0)
            copy_b(0, 0, 0)
            copy_b(0, 1, 1)
            act.wait_ge(s_cst, 2)
            batches(act, image)

        @block.gpsimd
        def _(pool):
            pool.sem_inc(s_rest, 1)
            pool.sem_inc(s_dt, 1)
            pool.sem_inc(s_db, FREE_DB)

            def remainder(b, gs):
                g = b * GROUPS + gs
                pool.wait_ge(s_part1, g + 1)
                pool.wait_ge(s_xd, g + 1)
                pool.wait_ge(s_bcs, g + 1)
                pool.tensor_tensor(rest[:], xdbl[0:96, :], bcs[:, gs % 2, :], ALU.subtract).then_inc(s_rest, 1)

            def deltas(b, gs):
                _, dp, _, _ = info(gs)
                g = b * GROUPS + gs
                pool.wait_ge(s_ln, g + 1)
                pool.tensor_tensor(dt[:, gs % 2], rl[:], ab[:], ALU.add).then_inc(s_dt, 1)
                pool.wait_ge(s_dt, g + 2)
                pool.tensor_tensor(dtx[:, gs % 2], dt[:, gs % 2], src(gs)[:, 2 * dp:2 * dp + 2, span(gs)],
                                   ALU.mult).then_inc(s_dtx, 1)

            def image(b, last):
                for gs in range(GROUPS):
                    g = b * GROUPS + gs
                    nb, ngs = (b, gs + 1) if gs + 1 < GROUPS else (b + 1, 0)
                    more = not (last and gs + 1 == GROUPS)

                    def pair(p):
                        for u in range(2):
                            for j in range(2):
                                t = g * NST + 2 * p + u
                                pool.wait_ge(s_bc, t + 2)
                                pool.wait_ge(s_h, 2 * t + j - 3 + FREE_H)
                                pool.tensor_tensor(dbx[:, 2 * u + j, :], dtx[:, gs % 2, j, :], bsb[:, u, :],
                                                   ALU.mult).then_inc(s_db, 1)
                    pool.wait_ge(s_dtx, g + 1)
                    pool.sem_inc(s_pass, 1)
                    segment(pool, 0, 3, pair)
                    if more:
                        remainder(nb, ngs)
                    segment(pool, 3, 5, pair)
                    if 1 <= gs <= DB:
                        c = gs - 1
                        if c == 0:
                            pool.wait_ge(s_xc, 16 * b + 16)
                            pool.sem_inc(s_pass, 1)
                        pool.tensor_copy(xct[:, c, :].rearrange("p (w h) -> p w h", h=H),
                                         xc[:, c, :].rearrange("p (h w) -> p w h", w=W)).then_inc(s_xct, 1)
                    segment(pool, 5, 7, pair)
                    if more:
                        deltas(nb, ngs)
                    segment(pool, 7, 8, pair)

            remainder(0, 0)
            deltas(0, 0)
            batches(pool, image)

        @block.vector
        def _(dve):
            dve.sem_inc(s_h, FREE_H)
            dve.sem_inc(s_dr, FREE_DR)
            dve.sem_inc(s_bcs, 1)
            dve.sem_inc(s_hc, FREE_HC)
            dve.wait_ge(s_w, 16 * 7)
            dve.tensor_reduce(dsum[:], ds4[:], AX_X, ALU.add).then_inc(s_cst, 1)
            dve.wait_ge(s_aexp, 1)
            dve.tensor_scalar(nega[:], nega[:], -1.0, None, ALU.mult).then_inc(s_cst, 1)

            def drain(b, gs):
                k, dp, _, _ = info(gs)
                g = b * GROUPS + gs
                dve.wait_ge(s_ns, 2 * NST * (g + 1) + FREE_NS)
                if gs == 0:
                    dve.wait_ge(s_yst, 16 * b + FREE_Y)
                for j in range(2):
                    c = 2 * dp + j
                    if k == 0:
                        out = yacc[:, c, span(gs)]
                        op = dve.scalar_tensor_tensor(out=out, in0=xc[:, c, span(gs)], scalar=dsum[:, c:c + 1],
                                                      in1=yps[:, j, :], op0=ALU.mult, op1=ALU.add)
                    elif k == 2:
                        out = yacc[:, c, span(gs)]
                        op = dve.tensor_tensor(out, yps[:, j, :], out, ALU.add)
                    else:
                        w0 = info(gs)[3] * (W // 2)
                        out = yacc[:, c, :].rearrange("p (h w) -> p w h", w=W)[:, w0:w0 + W // 2, :]
                        op = dve.tensor_tensor(out, yps[:, j, :].rearrange("p (w h) -> p w h", h=H), out, ALU.add)
                    op.then_inc(s_dr, 1)

            def third_part(b, gs):
                g = b * GROUPS + gs
                part = bcs[64:96, gs % 2, :]
                dve.wait_ge(s_part2, 2 * g + 2)
                dve.tensor_tensor(part, rest[64:96, :], part, ALU.subtract).then_inc(s_bcs, 1)

            def image(b, last):
                for gs in range(GROUPS):
                    k, dp, half, _ = info(gs)
                    g = b * GROUPS + gs

                    def ordered(ap):
                        return ap if k < 2 else ap[:, ::-1]

                    def pair(p):
                        for u in range(2):
                            t = g * NST + 2 * p + u
                            n = 2 * p + u
                            for j in range(2):
                                hs = hst[:, j, n, :]
                                end = hst[:, j, n, HALF - 1:HALF]
                                dve.wait_ge(s_da, 2 * t + j + 1)
                                dve.wait_ge(s_db, 2 * t + j + 1 + FREE_DB)
                                dve.tensor_tensor_scan(hs, ordered(dap[:, j, :]), ordered(dbx[:, 2 * u + j, :]),
                                                       0.0 if half == 0 else end, ALU.mult, ALU.add).then_inc(s_h, 1)
                            dve.wait_ge(s_cC, t + 1)
                            for j in range(2):
                                dve.wait_ge(s_h, 2 * t + j + 1 + FREE_H)
                                dve.wait_ge(s_ns, 2 * t + j - 3 + FREE_NS)
                                dve.tensor_tensor(ordered(hc[:, 2 * u + j, :]), hst[:, j, n, :], ordered(cps[:, u, :]),
                                                  ALU.mult).then_inc(s_hc, 1)
                    pair(0)
                    if gs > 0:
                        drain(b, gs - 1)
                    segment(dve, 1, 5, pair)
                    if gs + 1 < GROUPS:
                        third_part(b, gs + 1)
                    elif not last:
                        third_part(b + 1, 0)
                    segment(dve, 5, 8, pair)
                drain(b, GROUPS - 1)

            third_part(0, 0)
            batches(dve, image)


def mix_stage(nc, ysum_d, sz_d, xu_d, on_d, wout_d, ident, wr_d, br_d, x1, tn, w0, w0t):
    CB = C // P
    TB = L // P
    FREE = 4
    with ExitStack() as ctx:
        def sb(name, shape, dt=F32):
            return ctx.enter_context(nc.sbuf_tensor("mx_" + name, shape, dt))

        def ps(name, shape):
            return ctx.enter_context(nc.psum_tensor("mx_" + name, shape, F32))

        def sem(name):
            return ctx.enter_context(nc.semaphore("mx_" + name))

        y = sb("y", [P, DB, L])
        sz = sb("sz", [P, DB, L])
        xu = sb("xu", [P, CB, L])
        sqa = sb("sqa", [P, DB, L])
        yg = sb("yg", [P, DB, L])
        xm = sb("xm", [P, CB, L])
        sqb = sb("sqb", [P, CB, L])
        sd = sb("sd", [P, 2, TB])
        rs = sb("rs", [P, 2, TB])
        dga = sb("dga", [P, TB, P])
        dgb = sb("dgb", [P, TB, P])
        ong = sb("ong", [P, DB, 2])
        wout = sb("wout", [P, DB, C])
        wr = sb("wr", [P, CB, NE])
        br = sb("br", [1, NE])
        ones = sb("ones", [P, P])
        meana = sb("meana", [P, P])
        meanb = sb("meanb", [P, P])
        eps = sb("eps", [P, 1])
        fs = sb("fs", [P, CB, L])
        mx = sb("mx", [P, TB])
        lg = sb("lg", [P, TB, NE])
        sm = sb("sm", [P, TB])
        sta = ps("sta", [P, 2, L // 2])
        stb = ps("stb", [P, 2, L // 2])
        outp = ps("outp", [P, 2, L // 2])
        vaa = ps("vaa", [P, TB])
        vab = ps("vab", [P, TB])

        s_w, s_y, s_sz, s_xu, s_cst = sem("weights_in"), sem("y_in"), sem("sz_in"), sem("xu_in"), sem("consts")
        s_pass = sem("passed")
        s_ma, s_ym, s_sqa, s_va, s_sda, s_rsa, s_dga, s_rba = [sem("gate_" + n) for n in
            ("mean", "centred", "squared", "var", "dev", "rdev", "rdev_diag", "rdev_bcast")]
        s_yn, s_yb, s_yg = sem("gate_normed"), sem("gate_affine"), sem("gated")
        s_out, s_x1 = sem("projected"), sem("x1")
        s_mb, s_xm, s_sqb, s_vb, s_sdb, s_rsb, s_dgb, s_rbb = [sem("tok_" + n) for n in
            ("mean", "centred", "squared", "var", "dev", "rdev", "rdev_diag", "rdev_bcast")]
        s_tn = sem("tn")
        s_fs, s_lg, s_sm, s_ex, s_wt = sem("feat"), sem("logits"), sem("softmax"), sem("exp"), sem("w0t_psum")
        s_w0t = sem("w0t")

        def halves(ap):
            return ap.rearrange("p (h l) -> p h l", h=2)

        def lgp(t):
            return outp[:, 0, t * NE:(t + 1) * NE]

        def rounds(eng, body):
            body(0, True, False)
            with eng.Fori(1, B) as i:
                body(i, True, True)
            body(B, False, True)

        block = ctx.enter_context(nc.Block())

        @block.sync
        def _(sp):
            sp.dma_start(y[:], ysum_d[0]).then_inc(s_y, 16)
            for dst, s in ((ong, on_d), (wout, wout_d), (wr, wr_d), (br, br_d)):
                sp.dma_start(dst[:], s).then_inc(s_w, 16)
            sp.dma_start(sz[:], sz_d[0]).then_inc(s_sz, 16)
            sp.dma_start(xu[:], xu_d[0]).then_inc(s_xu, 16)
            with sp.Fori(1, B) as i:
                sp.wait_ge(s_sqa, i)
                sp.wait_ge(s_yn, i)
                sp.sem_inc(s_pass, 1)
                sp.dma_start(y[:], ysum_d[i]).then_inc(s_y, 16)
                sp.wait_ge(s_yg, i + FREE)
                sp.sem_inc(s_pass, 1)
                sp.dma_start(sz[:], sz_d[i]).then_inc(s_sz, 16)
                sp.wait_ge(s_x1, 2 * CB * i + FREE)
                sp.sem_inc(s_pass, 1)
                sp.dma_start(xu[:], xu_d[i]).then_inc(s_xu, 16)

        @block.tensor
        def _(pe):
            def mean_y(i):
                pe.wait_ge(s_y, 16 * i + 16)
                for h in range(2):
                    for c in range(DB):
                        mm = pe.matmul(sta[:, h, :], meana[:], halves(y[:, c, :])[:, h, :],
                                       start=(c == 0), stop=(c == DB - 1))
                mm.then_inc(s_ma, 1)

            def variances(s_in, s_done, i, va, sq, mean, blocks):
                pe.wait_ge(s_in, i + 1)
                for t in range(TB):
                    for c in range(blocks):
                        mm = pe.matmul(va[:, t:t + 1], sq[:, c, t * P:(t + 1) * P], mean[:, 0:1],
                                       start=(c == 0), stop=(c == blocks - 1))
                mm.then_inc(s_done, 1)

            def spread(s_in, s_done, i, st, dg):
                pe.wait_ge(s_in, i + 1)
                for t in range(TB):
                    mm = pe.matmul(st[:, t // 4, t % 4 * P:(t % 4 + 1) * P], ones[:], dg[:, t, :],
                                   start=True, stop=True)
                mm.then_inc(s_done, 1)

            def project(i):
                pe.wait_ge(s_yg, i + 1 + FREE)
                for v in range(2 * CB):
                    c, h = v // 2, v % 2
                    pe.wait_ge(s_x1, 2 * CB * i + v - 1 + FREE)
                    for k in range(DB):
                        mm = pe.matmul(outp[:, h, :], wout[:, k, c * P:(c + 1) * P], halves(yg[:, k, :])[:, h, :],
                                       start=(k == 0), stop=(k == DB - 1))
                    mm.then_inc(s_out, 1)

            def mean_x(i):
                pe.wait_ge(s_x1, 2 * CB * i + 2 * CB + FREE)
                for h in range(2):
                    for c in range(CB):
                        mm = pe.matmul(stb[:, h, :], meanb[:], x1[:, c, bass.ds(i * L + h * (L // 2), L // 2)],
                                       start=(c == 0), stop=(c == CB - 1))
                mm.then_inc(s_mb, 1)

            def body(i, gate, token):
                if gate:
                    mean_y(i)
                if token:
                    project(i - 1)
                if gate:
                    variances(s_sqa, s_va, i, vaa, sqa, meana, DB)
                if token:
                    mean_x(i - 1)
                if gate:
                    spread(s_dga, s_rba, i, sta, dga)
                if token:
                    variances(s_sqb, s_vb, i - 1, vab, sqb, meanb, CB)
                    spread(s_dgb, s_rbb, i - 1, stb, dgb)
            pe.wait_ge(s_cst, 4)
            pe.wait_ge(s_w, 16 * 4)
            rounds(pe, body)
            pe.wait_ge(s_fs, 4)
            for t in range(TB):
                for c in range(CB):
                    pe.matmul(lgp(t), fs[:, c, t * P:(t + 1) * P], wr[:, c, :],
                              start=(c == 0), stop=False)
                mm = pe.matmul(lgp(t), ones[0:1, :], br[:], start=False, stop=True)
            mm.then_inc(s_lg, 1)
            pe.wait_ge(s_sm, 5)
            for t in range(TB):
                mm = pe.transpose(sta[0:NE, t // 4, t % 4 * P:(t % 4 + 1) * P], w0[:, t, :], ident[:])
            mm.then_inc(s_wt, 1)

        @block.scalar
        def _(act):
            def body(i, gate, token):
                if gate:
                    act.wait_ge(s_ym, i + 1)
                    act.wait_ge(s_yg, i + FREE)
                    act.activation(sqa[:], y[:], ACT.Square).then_inc(s_sqa, 1)
                    act.wait_ge(s_va, i + 1)
                    act.activation(sd[:, 0, :], vaa[:], ACT.Sqrt, bias=eps[:]).then_inc(s_sda, 1)
                if token:
                    act.wait_ge(s_xm, i)
                    act.activation(sqb[:], xm[:], ACT.Square).then_inc(s_sqb, 1)
                    act.wait_ge(s_vb, i)
                    act.activation(sd[:, 1, :], vab[:], ACT.Sqrt, bias=eps[:]).then_inc(s_sdb, 1)
            act.wait_ge(s_cst, 4)
            rounds(act, body)
            act.wait_ge(s_sm, 2)
            act.activation(lg[:], lg[:], ACT.Exp).then_inc(s_ex, 1)
            act.wait_ge(s_wt, 1)
            act.activation(w0t[:], sta[0:NE].rearrange("p a b -> p (a b)"), ACT.Copy).then_inc(s_w0t, 1)

        @block.gpsimd
        def _(pool):
            pool.memset(ones[:], 1.0).then_inc(s_cst, 1)
            pool.memset(meana[:], 1.0 / DI).then_inc(s_cst, 1)
            pool.memset(meanb[:], 1.0 / C).then_inc(s_cst, 1)
            pool.memset(eps[:], 1e-5).then_inc(s_cst, 1)
            pool.sem_inc(s_yg, FREE)
            with pool.Fori(0, B) as i:
                pool.wait_ge(s_sz, 16 * i + 16)
                pool.wait_ge(s_yb, DB * i + DB)
                pool.tensor_tensor(yg[:], sqa[:], sz[:], ALU.mult).then_inc(s_yg, 1)

        @block.vector
        def _(dve):
            def rdev(i, r, s_sd, s_rs, s_dg, dg):
                dve.wait_ge(s_sd, i + 1)
                dve.reciprocal(rs[:, r, :], sd[:, r, :]).then_inc(s_rs, 1)
                dve.wait_ge(s_rs, i + 1)
                for t in range(TB):
                    op = dve.tensor_scalar(dg[:, t, :], ident[:], rs[:, r, t:t + 1], None, ALU.mult)
                op.then_inc(s_dg, 1)

            def body(i, gate, token):
                if gate:
                    dve.wait_ge(s_ma, i + 1)
                    for c in range(DB):
                        op = dve.tensor_tensor(halves(y[:, c, :]), halves(y[:, c, :]), sta[:], ALU.subtract)
                    op.then_inc(s_ym, 1)
                if token:
                    dve.wait_ge(s_xu, 16 * i)
                    for v in range(2 * CB):
                        c, h = v // 2, v % 2
                        dve.wait_ge(s_out, 2 * CB * (i - 1) + v + 1)
                        dve.tensor_tensor(x1[:, c, bass.ds((i - 1) * L + h * (L // 2), L // 2)], outp[:, h, :],
                                          halves(xu[:, c, :])[:, h, :], ALU.add).then_inc(s_x1, 1)
                if gate:
                    rdev(i, 0, s_sda, s_rsa, s_dga, dga)
                if token:
                    dve.wait_ge(s_mb, i)
                    dve.wait_ge(s_x1, 2 * CB * i + FREE)
                    for c in range(CB):
                        op = dve.tensor_tensor(halves(xm[:, c, :]),
                                               halves(x1[:, c, bass.ds((i - 1) * L, L)]), stb[:], ALU.subtract)
                    op.then_inc(s_xm, 1)
                if gate:
                    dve.wait_ge(s_rba, i + 1)
                    for c in range(DB):
                        op = dve.tensor_tensor(halves(sqa[:, c, :]), halves(y[:, c, :]), sta[:], ALU.mult)
                    op.then_inc(s_yn, 1)
                    dve.wait_ge(s_yn, i + 1)
                    for c in range(DB):
                        dve.tensor_scalar(sqa[:, c, :], sqa[:, c, :], ong[:, c, 0:1], ong[:, c, 1:2],
                                          ALU.mult, ALU.add).then_inc(s_yb, 1)
                if token:
                    rdev(i - 1, 1, s_sdb, s_rsb, s_dgb, dgb)
                    dve.wait_ge(s_rbb, i)
                    for c in range(CB):
                        op = dve.tensor_tensor(halves(tn[:, c, bass.ds((i - 1) * L, L)]), halves(xm[:, c, :]),
                                               stb[:], ALU.mult)
                    op.then_inc(s_tn, 1)
            dve.sem_inc(s_x1, FREE)
            dve.wait_ge(s_w, 16 * 4)
            rounds(dve, body)
            dve.wait_ge(s_tn, B)
            dve.tensor_tensor(fs[:], tn[:, :, 0:L], tn[:, :, L:2 * L], ALU.add).then_inc(s_fs, 1)
            for b in range(2, B):
                dve.wait_ge(s_fs, b - 1)
                dve.tensor_tensor(fs[:], fs[:], tn[:, :, b * L:(b + 1) * L], ALU.add).then_inc(s_fs, 1)
            dve.wait_ge(s_fs, B - 1)
            dve.tensor_scalar(fs[:], fs[:], 1.0 / B, None, ALU.mult).then_inc(s_fs, 1)
            lgv = outp[:, 0, 0:TB * NE].rearrange("p (t e) -> p t e", e=NE)
            dve.wait_ge(s_lg, 1)
            dve.tensor_reduce(mx[:], lgv, AX_X, ALU.max).then_inc(s_sm, 1)
            dve.wait_ge(s_sm, 1)
            dve.tensor_tensor(lg[:], lgv, mx[:].unsqueeze(2).to_broadcast([P, TB, NE]), ALU.subtract).then_inc(s_sm, 1)
            dve.wait_ge(s_ex, 1)
            dve.tensor_reduce(sm[:], lg[:], AX_X, ALU.add).then_inc(s_sm, 1)
            dve.wait_ge(s_sm, 3)
            dve.reciprocal(sm[:], sm[:]).then_inc(s_sm, 1)
            dve.wait_ge(s_sm, 4)
            dve.tensor_tensor(w0[:], lg[:], sm[:].unsqueeze(2).to_broadcast([P, TB, NE]), ALU.mult).then_inc(s_sm, 1)
            dve.wait_ge(s_w0t, 1)


def soft_stage(nc, w1_d, w2_d, wo_d, bn_d, bo_d, ident, tn, x1, w0, w0t):
    CB = C // P
    TK = 512
    NB = TK // P
    CHUNKS = B * L // TK
    with ExitStack() as ctx:
        def sb(name, shape, dt=F32):
            return ctx.enter_context(nc.sbuf_tensor("so_" + name, shape, dt))

        def ps(name, shape):
            return ctx.enter_context(nc.psum_tensor("so_" + name, shape, F32))

        def sem(name):
            return ctx.enter_context(nc.semaphore("so_" + name))

        w1 = sb("w1", [P, NE, CB, C])
        w2 = sb("w2", [P, NE, CB, C])
        wo = sb("wo", [P, NE, CB, C])
        bn = sb("bn", [P, 2, 5, NE * CB])
        bns = sb("bns", [P, 2, NE * CB])
        bnt = sb("bnt", [P, 2, NE * CB])
        bo = sb("bo", [NE, C])
        eps = sb("eps", [P, 1])
        h1 = sb("h1", [P, 2, CB, TK])
        h2 = sb("h2", [P, 2, CB, TK])
        acc0 = sb("acc0", [P, NB, C])
        acc = sb("acc", [P, NB, C])
        ap = ps("ap", [P, CB, TK])
        bp = ps("bp", [P, CB, TK])
        yp = ps("yp", [P, NB, C])
        tp = ps("tp", [P, CB, TK])

        s_w, s_eps, s_bn, s_sd = sem("weights_in"), sem("eps"), sem("bn_step"), sem("bn_dev")
        s_pa, s_h1, s_pb, s_h2, s_py, s_acc = [sem(n) for n in ("h1_psum", "h1", "h2_psum", "h2", "y_psum", "acc")]
        s_pbo, s_acc0, s_pt, s_x2 = [sem(n) for n in ("bias_psum", "bias_acc", "acc_turned", "x2")]

        block = ctx.enter_context(nc.Block())

        @block.sync
        def _(sp):
            for dst, s in ((bn, bn_d), (bo, bo_d), (w1, w1_d), (w2, w2_d), (wo, wo_d)):
                sp.dma_start(dst[:], s).then_inc(s_w, 16)

        @block.tensor
        def _(pe):
            pe.sem_inc(s_pb, 4)
            pe.sem_inc(s_py, 4)
            pe.sem_inc(s_pt, 1)

            def first(s, i, e):
                for o in range(CB):
                    pe.wait_ge(s_h1, 2 * s + o + 1)
                    for k in range(CB):
                        mm = pe.matmul(ap[:, o, :], w1[:, e, k, o * P:(o + 1) * P],
                                       tn[:, k, bass.ds(i * TK, TK)], start=(k == 0), stop=(k == CB - 1))
                    mm.then_inc(s_pa, 1)

            def second(s, e):
                pe.wait_ge(s_h1, 2 * s + 2 + 2)
                for o in range(CB):
                    pe.wait_ge(s_h2, 2 * s + o + 1)
                    for k in range(CB):
                        mm = pe.matmul(bp[:, o, :], w2[:, e, k, o * P:(o + 1) * P], h1[:, e % 2, k, :],
                                       start=(k == 0), stop=(k == CB - 1))
                    mm.then_inc(s_pb, 1)

            def third(s, e):
                pe.wait_ge(s_h2, 2 * s + 2 + 2)
                for q in range(2):
                    pe.wait_ge(s_acc, 2 * s + q + 1)
                    for t in (2 * q, 2 * q + 1):
                        for k in range(CB):
                            mm = pe.matmul(yp[:, t, :], h2[:, e % 2, k, t * P:(t + 1) * P], wo[:, e, k, :],
                                           start=(k == 0), stop=(k == CB - 1))
                    mm.then_inc(s_py, 1)

            def bias_sums(i, half):
                pe.wait_ge(s_x2, CB * (i - 1) + 2)
                for t in range(NB):
                    tok = (half * NB + t) * P
                    mm = pe.matmul(tp[:, t // 2, t % 2 * C:(t % 2 + 1) * C], w0t[:, tok:tok + P], bo[:],
                                   start=True, stop=True)
                mm.then_inc(s_pbo, 1)

            def turn(i, last=False):
                pe.wait_ge(s_acc, 2 * NE * (i + 1) + 2)
                if not last:
                    pe.wait_ge(s_acc0, i + 2)
                else:
                    pe.wait_ge(s_x2, CB * i + 2)
                for t in range(NB):
                    for c in range(CB):
                        mm = pe.transpose(tp[:, c, t * P:(t + 1) * P], acc[:, t, c * P:(c + 1) * P], ident[:])
                mm.then_inc(s_pt, 1)

            def image(b):
                for half in range(2):
                    i = 2 * b + half
                    for e in range(NE):
                        s = i * NE + e
                        begun = not isinstance(b, int) or b > 0 or half > 0
                        first(s, i, e)
                        if begun or e >= 1:
                            second(s - 1, (e - 1) % NE)
                        if begun and e == 2:
                            turn(i - 1)
                        if begun or e >= 2:
                            third(s - 2, (e - 2) % NE)
                        if e == 4 and not (isinstance(b, int) and b == B - 1 and half == 1):
                            bias_sums(i + 1, 1 - half)
            pe.wait_ge(s_w, 16 * 5)
            for t in range(NB):
                mm = pe.matmul(tp[:, t // 2, t % 2 * C:(t % 2 + 1) * C], w0t[:, t * P:(t + 1) * P], bo[:],
                               start=True, stop=True)
            mm.then_inc(s_pbo, 1)
            pe.wait_ge(s_acc0, 1)
            image(0)
            with pe.Fori(1, B - 1) as b:
                image(b)
            image(B - 1)
            s_end = CHUNKS * NE
            second(s_end - 1, NE - 1)
            third(s_end - 2, NE - 2)
            third(s_end - 1, NE - 1)
            turn(CHUNKS - 1, True)

        @block.scalar
        def _(act):
            act.sem_inc(s_h1, 2)
            act.sem_inc(s_h2, 2)
            act.wait_ge(s_w, 16 * 5)
            act.wait_ge(s_eps, 1)
            act.activation(bns[:], bn[:, :, 4, :], ACT.Sqrt, bias=eps[:]).then_inc(s_sd, 1)
            act.wait_ge(s_bn, 5)

            def relu1(s, e):
                act.wait_ge(s_pb, 2 * s + 2)
                for o in range(CB):
                    col = e * CB + o
                    act.wait_ge(s_pa, 2 * s + o + 1)
                    act.activation(h1[:, e % 2, o, :], ap[:, o, :], ACT.Relu, scale=bns[:, 0, col:col + 1],
                                   bias=bnt[:, 0, col:col + 1]).then_inc(s_h1, 1)

            def relu2(s, e):
                act.wait_ge(s_py, 2 * s + 2)
                for o in range(CB):
                    col = e * CB + o
                    act.wait_ge(s_pb, 2 * s + o + 1 + 4)
                    act.activation(h2[:, e % 2, o, :], bp[:, o, :], ACT.Relu, scale=bns[:, 1, col:col + 1],
                                   bias=bnt[:, 1, col:col + 1]).then_inc(s_h2, 1)

            def copy_bias(i):
                act.wait_ge(s_pbo, i + 1)
                if not (isinstance(i, int) and i == 0):
                    act.wait_ge(s_acc, 2 * NE * (i - 1) + 2 + 2)
                act.activation(acc0[:], tp[:].rearrange("p a (t c) -> p (a t) c", c=C), ACT.Copy).then_inc(s_acc0, 1)

            def image(b):
                for half in range(2):
                    i = 2 * b + half
                    for e in range(NE):
                        s = i * NE + e
                        relu1(s, e)
                        if not isinstance(b, int) or b > 0 or half > 0 or e >= 1:
                            relu2(s - 1, (e - 1) % NE)
                        if e == 4 and not (isinstance(b, int) and b == B - 1 and half == 1):
                            copy_bias(i + 1)
            copy_bias(0)
            image(0)
            with act.Fori(1, B - 1) as b:
                image(b)
            image(B - 1)
            relu2(CHUNKS * NE - 1, NE - 1)

        @block.gpsimd
        def _(pool):
            pool.memset(eps[:], 1e-3).then_inc(s_eps, 1)

        @block.vector
        def _(dve):
            dve.sem_inc(s_acc, 2)
            dve.sem_inc(s_x2, 2)
            dve.wait_ge(s_w, 16 * 5)
            dve.wait_ge(s_sd, 1)
            dve.reciprocal(bns[:], bns[:]).then_inc(s_bn, 1)
            dve.tensor_tensor(bnt[:], bn[:, :, 0, :], bn[:, :, 3, :], ALU.subtract).then_inc(s_bn, 1)
            dve.wait_ge(s_bn, 2)
            dve.tensor_tensor(bns[:], bns[:], bn[:, :, 1, :], ALU.mult).then_inc(s_bn, 1)
            dve.wait_ge(s_bn, 3)
            dve.tensor_tensor(bnt[:], bnt[:], bns[:], ALU.mult).then_inc(s_bn, 1)
            dve.wait_ge(s_bn, 4)
            dve.tensor_tensor(bnt[:], bnt[:], bn[:, :, 2, :], ALU.add).then_inc(s_bn, 1)

            def add_step(s, i, half, e):
                if e == 0:
                    dve.wait_ge(s_pt, i + 1)
                    dve.wait_ge(s_acc0, i + 1)
                for q in range(2):
                    dve.wait_ge(s_py, 2 * s + q + 1 + 4)
                    if e > 0:
                        dve.wait_ge(s_acc, 2 * (s - 1) + q + 1 + 2)
                    for t in (2 * q, 2 * q + 1):
                        op = dve.scalar_tensor_tensor(out=acc[:, t, :], in0=yp[:, t, :],
                                                      scalar=w0[:, half * NB + t, e:e + 1],
                                                      in1=(acc0 if e == 0 else acc)[:, t, :],
                                                      op0=ALU.mult, op1=ALU.add)
                    op.then_inc(s_acc, 1)

            def add_chunk(i):
                dve.wait_ge(s_pt, i + 2)
                for c in range(CB):
                    part = x1[:, c, bass.ds(i * TK, TK)]
                    dve.tensor_tensor(part, tp[:, c, :], part, ALU.add).then_inc(s_x2, 1)

            def image(b):
                for half in range(2):
                    i = 2 * b + half
                    for e in range(NE):
                        s = i * NE + e
                        begun = not isinstance(b, int) or b > 0 or half > 0
                        if begun and e == 2:
                            add_chunk(i - 1)
                        if e >= 2:
                            add_step(s - 2, i, half, e - 2)
                        elif begun:
                            add_step(s - 2, i - 1, 1 - half, e - 2 + NE)
            image(0)
            with dve.Fori(1, B - 1) as b:
                image(b)
            image(B - 1)
            for e in (NE - 2, NE - 1):
                add_step((CHUNKS - 1) * NE + e, CHUNKS - 1, 1, e)
            add_chunk(CHUNKS - 1)


def dct_stage(nc, dct_d, rw_d, lower_d, ident, x1, tn, gates):
    CB = C // P
    TB = L // P
    FREE = 4
    with ExitStack() as ctx:
        def sb(name, shape, dt=F32):
            return ctx.enter_context(nc.sbuf_tensor("dc_" + name, shape, dt))

        def ps(name, shape):
            return ctx.enter_context(nc.psum_tensor("dc_" + name, shape, F32))

        def sem(name):
            return ctx.enter_context(nc.semaphore("dc_" + name))

        dct = sb("dct", [P, TB, L])
        rw = sb("rw", [P, CB, NE])
        lower = sb("lower", [P, NE, NE])
        xm = sb("xm", [P, 2, CB, L])
        sq = sb("sq", [P, 2, CB, L])
        v = sb("v", [P, CB, L])
        tnb = sb("tnb", [P, CB, L])
        vt = sb("vt", [P, TB, C])
        sd = sb("sd", [P, 2, TB])
        rs = sb("rs", [P, 2, TB])
        dg = sb("dg", [P, 2, TB, P])
        ones = sb("ones", [P, P])
        mean = sb("mean", [P, P])
        eps = sb("eps", [P, 2])
        mx = sb("mx", [P, TB])
        pr = sb("pr", [P, TB, NE])
        sm = sb("sm", [P, TB])
        above = sb("above", [P, TB, NE, NE])
        tie = sb("tie", [P, TB, NE, NE])
        rank = sb("rank", [P, TB, NE])
        sta = ps("sta", [P, 2, L // 2])
        stb = ps("stb", [P, 2, L // 2])
        outp = ps("outp", [P, 2, L // 2])
        vaa = ps("vaa", [P, TB])
        vab = ps("vab", [P, TB + TB * NE])
        st, va = (sta, stb), (vaa[:], vab[:, 0:TB])
        lgv = vab[:, TB:TB + TB * NE].rearrange("p (t e) -> p t e", e=NE)

        s_w, s_cst, s_pass, s_tnc = sem("weights_in"), sem("consts"), sem("passed"), sem("tn_kept")
        s_m, s_xm, s_sq, s_va, s_sd, s_rs, s_dg, s_rb = [[sem(f"norm{r}_{n}") for r in range(2)] for n in
            ("mean", "centred", "squared", "var", "dev", "rdev", "rdev_diag", "rdev_bcast")]
        s_v, s_tr, s_vt, s_dct, s_x3, s_tn = [sem(n) for n in ("v", "turn_psum", "turned", "dct_psum", "x3", "tn")]
        s_lg, s_ex, s_g, s_gate = [sem(n) for n in ("logits", "exp", "gate_step", "gates")]
        s_gr = sem("gate_scale")
        GS = 12

        def halves(ap):
            return ap.rearrange("p (h l) -> p h l", h=2)

        def rounds(eng, body):
            body(0, True, False)
            with eng.Fori(1, B) as i:
                body(i, True, True)
            body(B, False, True)

        block = ctx.enter_context(nc.Block())

        @block.sync
        def _(sp):
            for dst, s in ((rw, rw_d), (lower, lower_d), (dct, dct_d)):
                sp.dma_start(dst[:], s).then_inc(s_w, 16)

        @block.tensor
        def _(pe):
            def means(i, r):
                for h in range(2):
                    for c in range(CB):
                        mm = pe.matmul(st[r][:, h, :], mean[:], x1[:, c, bass.ds(i * L + h * (L // 2), L // 2)],
                                       start=(c == 0), stop=(c == CB - 1))
                mm.then_inc(s_m[r], 1)

            def variances(i, r):
                pe.wait_ge(s_sq[r], i + 1)
                for t in range(TB):
                    for c in range(CB):
                        mm = pe.matmul(va[r][:, t:t + 1], sq[:, r, c, t * P:(t + 1) * P], mean[:, 0:1],
                                       start=(c == 0), stop=(c == CB - 1))
                mm.then_inc(s_va[r], 1)

            def spread(i, r):
                pe.wait_ge(s_dg[r], i + 1)
                for t in range(TB):
                    mm = pe.matmul(st[r][:, t // 4, t % 4 * P:(t % 4 + 1) * P], ones[:], dg[:, r, t, :],
                                   start=True, stop=True)
                mm.then_inc(s_rb[r], 1)

            def turn(i):
                pe.wait_ge(s_v, i + 1)
                for u in range(4):
                    if u < 2:
                        pe.wait_ge(s_x3, 4 * i + FREE)
                    else:
                        pe.wait_ge(s_vt, 4 * i + u - 1)
                    for t in (2 * u, 2 * u + 1):
                        for c in range(CB):
                            col = (t % 2) * C + c * P
                            mm = pe.transpose(outp[:, u % 2, col:col + P], v[:, c, t * P:(t + 1) * P], ident[:])
                    mm.then_inc(s_tr, 1)

            def transform(i, c):
                for h in range(2):
                    if c == 0:
                        pe.wait_ge(s_vt, 4 * i + 4)
                    else:
                        pe.wait_ge(s_x3, 4 * i + 2 * c + h - 1 + FREE)
                    for t in range(TB):
                        mm = pe.matmul(outp[:, h, :], vt[:, t, c * P:(c + 1) * P], halves(dct[:, t, :])[:, h, :],
                                       start=(t == 0), stop=(t == TB - 1))
                    mm.then_inc(s_dct, 1)

            def route(i):
                pe.wait_ge(s_tn, i + 1)
                for t in range(TB):
                    for c in range(CB):
                        mm = pe.matmul(vab[:, TB + t * NE:TB + (t + 1) * NE],
                                       tnb[:, c, t * P:(t + 1) * P], rw[:, c, :],
                                       start=(c == 0), stop=(c == CB - 1))
                mm.then_inc(s_lg, 1)

            def body(i, norm, token):
                if norm:
                    means(i, 0)
                if token:
                    transform(i - 1, 0)
                if norm:
                    variances(i, 0)
                if token:
                    transform(i - 1, 1)
                if norm:
                    spread(i, 0)
                if token:
                    pe.wait_ge(s_x3, 4 * i + FREE)
                    means(i - 1, 1)
                if norm:
                    turn(i)
                if token:
                    variances(i - 1, 1)
                    spread(i - 1, 1)
                    route(i - 1)
            pe.wait_ge(s_cst, 3)
            pe.wait_ge(s_w, 16 * 3)
            rounds(pe, body)

        @block.scalar
        def _(act):
            def square(i, r):
                act.wait_ge(s_xm[r], i + 1)
                act.activation(sq[:, r], xm[:, r], ACT.Square).then_inc(s_sq[r], 1)

            def deviation(i, r):
                act.wait_ge(s_va[r], i + 1)
                act.activation(sd[:, r, :], va[r], ACT.Sqrt, bias=eps[:, r:r + 1]).then_inc(s_sd[r], 1)

            def body(i, norm, token):
                if norm:
                    square(i, 0)
                    deviation(i, 0)
                if token:
                    square(i - 1, 1)
                if norm:
                    for u in range(4):
                        act.wait_ge(s_tr, 4 * i + u + 1)
                        act.activation(vt[:, 2 * u:2 * u + 2, :], outp[:, u % 2, :].rearrange("p (t c) -> p t c", c=C),
                                       ACT.Copy).then_inc(s_vt, 1)
                if token:
                    deviation(i - 1, 1)
                    act.wait_ge(s_g, GS * (i - 1) + 2)
                    act.activation(pr[:], pr[:], ACT.Exp).then_inc(s_ex, 1)
            act.wait_ge(s_cst, 3)
            rounds(act, body)

        @block.gpsimd
        def _(pool):
            pool.sem_inc(s_tnc, 1)
            pool.memset(ones[:], 1.0).then_inc(s_cst, 1)
            pool.memset(mean[:], 1.0 / C).then_inc(s_cst, 1)
            pool.memset(eps[:, 0:1], 1e-6)
            pool.memset(eps[:, 1:2], 1e-5).then_inc(s_cst, 1)
            with pool.Fori(0, B) as i:
                pool.wait_ge(s_tn, i + 1)
                pool.sem_inc(s_pass, 1)
                pool.tensor_copy(tn[:, :, bass.ds(i * L, L)], tnb[:]).then_inc(s_tnc, 1)
            pool.wait_ge(s_tnc, B + 1)

        @block.vector
        def _(dve):
            def centre(i, r):
                dve.wait_ge(s_m[r], i + 1)
                for c in range(CB):
                    op = dve.tensor_tensor(halves(xm[:, r, c, :]), halves(x1[:, c, bass.ds(i * L, L)]), st[r][:],
                                           ALU.subtract)
                op.then_inc(s_xm[r], 1)

            def rdev(i, r):
                dve.wait_ge(s_sd[r], i + 1)
                dve.reciprocal(rs[:, r, :], sd[:, r, :]).then_inc(s_rs[r], 1)
                dve.wait_ge(s_rs[r], i + 1)
                for t in range(TB):
                    op = dve.tensor_scalar(dg[:, r, t, :], ident[:], rs[:, r, t:t + 1], None, ALU.mult)
                op.then_inc(s_dg[r], 1)

            def gate(i):
                g0 = GS * i
                e_of = pr[:].unsqueeze(3).to_broadcast([P, TB, NE, NE])
                j_of = pr[:].unsqueeze(2).to_broadcast([P, TB, NE, NE])
                low = lower[:].unsqueeze(1).to_broadcast([P, TB, NE, NE])
                per_t = sm[:].unsqueeze(2).to_broadcast([P, TB, NE])
                dve.wait_ge(s_lg, i + 1)
                dve.tensor_reduce(mx[:], lgv, AX_X, ALU.max).then_inc(s_g, 1)
                dve.wait_ge(s_g, g0 + 1)
                dve.tensor_tensor(pr[:], lgv, mx[:].unsqueeze(2).to_broadcast([P, TB, NE]), ALU.subtract).then_inc(s_g, 1)
                dve.wait_ge(s_ex, i + 1)
                dve.tensor_reduce(sm[:], pr[:], AX_X, ALU.add).then_inc(s_g, 1)
                dve.wait_ge(s_g, g0 + 3)
                dve.reciprocal(sm[:], sm[:]).then_inc(s_g, 1)
                dve.wait_ge(s_g, g0 + 4)
                dve.tensor_tensor(pr[:], pr[:], per_t, ALU.mult).then_inc(s_g, 1)
                dve.wait_ge(s_g, g0 + 5)
                dve.tensor_tensor(tie[:], j_of, e_of, ALU.is_equal).then_inc(s_g, 1)
                dve.tensor_tensor(above[:], j_of, e_of, ALU.is_gt)
                dve.wait_ge(s_g, g0 + 6)
                dve.tensor_tensor(tie[:], tie[:], low, ALU.mult).then_inc(s_g, 1)
                dve.wait_ge(s_g, g0 + 7)
                dve.tensor_tensor(above[:], above[:], tie[:], ALU.add).then_inc(s_g, 1)
                dve.wait_ge(s_g, g0 + 8)
                dve.tensor_reduce(rank[:], above[:], AX_X, ALU.add).then_inc(s_g, 1)
                dve.wait_ge(s_g, g0 + 9)
                dve.scalar_tensor_tensor(out=pr[:], in0=rank[:], scalar=2.0, in1=pr[:], op0=ALU.is_lt,
                                         op1=ALU.mult).then_inc(s_g, 1)
                dve.wait_ge(s_g, g0 + 10)
                dve.tensor_reduce(sm[:], pr[:], AX_X, ALU.add).then_inc(s_g, 1)
                dve.wait_ge(s_g, g0 + 11)
                dve.tensor_scalar(sm[:], sm[:], 1e-9, None, ALU.add).then_inc(s_g, 1)
                dve.wait_ge(s_g, g0 + 12)
                dve.reciprocal(sm[:], sm[:]).then_inc(s_gr, 1)
                dve.wait_ge(s_gr, i + 1)
                dve.tensor_tensor(gates[:, bass.ds(i * TB, TB), :], pr[:], per_t, ALU.mult).then_inc(s_gate, 1)

            def body(i, norm, token):
                if norm:
                    centre(i, 0)
                    rdev(i, 0)
                if token:
                    for u in range(4):
                        c, h = u // 2, u % 2
                        part = x1[:, c, bass.ds((i - 1) * L + h * (L // 2), L // 2)]
                        dve.wait_ge(s_dct, 4 * (i - 1) + u + 1)
                        dve.tensor_tensor(part, outp[:, h, :], part, ALU.add).then_inc(s_x3, 1)
                if norm:
                    dve.wait_ge(s_rb[0], i + 1)
                    for c in range(CB):
                        op = dve.tensor_tensor(halves(v[:, c, :]), halves(xm[:, 0, c, :]), sta[:], ALU.mult)
                    op.then_inc(s_v, 1)
                if token:
                    dve.wait_ge(s_x3, 4 * i + FREE)
                    centre(i - 1, 1)
                    rdev(i - 1, 1)
                    dve.wait_ge(s_rb[1], i)
                    dve.wait_ge(s_tnc, i)
                    for c in range(CB):
                        op = dve.tensor_tensor(halves(tnb[:, c, :]), halves(xm[:, 1, c, :]), stb[:], ALU.mult)
                    op.then_inc(s_tn, 1)
                    gate(i - 1)
            dve.sem_inc(s_x3, FREE)
            dve.wait_ge(s_w, 16 * 3)
            rounds(dve, body)
            dve.wait_ge(s_gate, B)


def moe_stage(nc, w13_d, w2_d, ident, x1, tn, gates, out_d):
    CB = C // P
    TK = 512
    NB = TK // P
    CHUNKS = B * L // TK
    HB = w2_d.shape[2]
    ORDER = [HB - 1, *range(HB - 1)]
    with ExitStack() as ctx:
        def sb(name, shape, dt=F32):
            return ctx.enter_context(nc.sbuf_tensor("mo_" + name, shape, dt))

        def ps(name, shape):
            return ctx.enter_context(nc.psum_tensor("mo_" + name, shape, F32))

        def sem(name):
            return ctx.enter_context(nc.semaphore("mo_" + name))

        w13 = [sb(f"w13_{k}", [P, 2, CB, HB * P]) for k in range(2)]
        w2 = [sb(f"w2_{k}", [P, HB, C]) for k in range(2)]
        act1 = sb("act1", [P, 2, TK])
        hid = sb("hid", [P, 2, HB, TK])
        acc = sb("acc", [P, CHUNKS * NB, C])
        xo = sb("xo", [P, 2, CB, TK])
        p1 = ps("p1", [P, 2, TK])
        p3 = ps("p3", [P, 2, TK])
        yp = ps("yp", [P, NB, C])
        tp = ps("tp", [P, CB, TK])

        s_zero, s_pass = sem("acc_zeroed"), sem("passed")
        s_wt = [sem(f"weights{k}") for k in range(2)]
        s_p1, s_p3, s_a1, s_hid, s_y, s_acc = [sem(n) for n in ("up_psum", "gate_psum", "silu", "hidden", "y_psum", "acc")]
        s_tp, s_xo = sem("turned"), sem("result")
        s_out = [sem(f"stored{k}") for k in range(2)]
        FREE_A1, FREE_HID, FREE_Y, FREE_ACC = 2, 2, 4, 2

        def steps(eng, expert_begin, step):
            with eng.Fori(0, NE // 2) as ep:
                for slot in range(2):
                    expert_begin(ep, slot)
                    with eng.Fori(0, CHUNKS // 2) as ip:
                        for par in range(2):
                            step((2 * ep + slot) * CHUNKS + 2 * ip + par, 2 * ip + par, slot, par, 2 * ep + slot)

        block = ctx.enter_context(nc.Block())

        @block.sync
        def _(sp):
            for e in range(2):
                sp.dma_start(w13[e][:], w13_d[e]).then_inc(s_wt[e], 16)
                sp.dma_start(w2[e][:], w2_d[e]).then_inc(s_wt[e], 16)
            with sp.Fori(1, NE // 2) as ep:
                for slot in range(2):
                    sp.wait_ge(s_y, 2 * CHUNKS * (2 * ep + slot - 1) + FREE_Y)
                    sp.sem_inc(s_pass, 1)
                    sp.dma_start(w13[slot][:], w13_d[2 * ep + slot]).then_inc(s_wt[slot], 16)
                    sp.dma_start(w2[slot][:], w2_d[2 * ep + slot]).then_inc(s_wt[slot], 16)
            for i in range(CHUNKS):
                sp.wait_ge(s_xo, CB * (i + 1) + CB * 2)
                b, half = i // 2, i % 2
                sp.dma_start(out_d[b].rearrange("(c p) l -> p c l", p=P)[:, :, half * TK:(half + 1) * TK],
                             xo[:, i % 2]).then_inc(s_out[i % 2], 16)
            for k in range(2):
                sp.wait_ge(s_out[k], 16 * CHUNKS // 2)

        @block.tensor
        def _(pe):
            def begin(ep, slot):
                pe.wait_ge(s_wt[slot], 32 * ep + 32)
                pe.sem_inc(s_pass, 1)

            def step(s, i, slot, par, e):
                for q, hb in enumerate(ORDER):
                    u = HB * s + q
                    for which, bank, s_free, free, s_done in ((0, p1, s_a1, FREE_A1, s_p1), (1, p3, s_hid, FREE_HID, s_p3)):
                        pe.wait_ge(s_free, u - 1 + free)
                        for k in range(CB):
                            mm = pe.matmul(bank[:, q % 2, :], w13[slot][:, which, k, hb * P:(hb + 1) * P],
                                           tn[:, k, bass.ds(i * TK, TK)], start=(k == 0), stop=(k == CB - 1))
                        mm.then_inc(s_done, 1)
                for t in range(NB):
                    if t % 2 == 0:
                        pe.wait_ge(s_acc, 2 * s + t // 2 - 1 + FREE_ACC)
                    for q, hb in enumerate(ORDER):
                        if t == 0 and q in (0, HB - 1):
                            pe.wait_ge(s_hid, HB * s + (HB if q else HB - 1) + FREE_HID)
                        mm = pe.matmul(yp[:, t, :], hid[:, par, hb, t * P:(t + 1) * P], w2[slot][:, hb, :],
                                       start=(q == 0), stop=(q == HB - 1))
                    if t % 2:
                        mm.then_inc(s_y, 1)

            pe.sem_inc(s_y, FREE_Y)
            steps(pe, begin, step)
            pe.wait_ge(s_acc, 2 * NE * CHUNKS + FREE_ACC)
            for i in range(CHUNKS):
                for c in range(CB):
                    pe.wait_ge(s_xo, CB * i + c + 1 + CB)
                    for t in range(NB):
                        mm = pe.transpose(tp[:, c, t * P:(t + 1) * P], acc[:, i * NB + t, c * P:(c + 1) * P], ident[:])
                    mm.then_inc(s_tp, 1)

        @block.scalar
        def _(act):
            def step(s, i, slot, par, e):
                for q in range(HB):
                    u = HB * s + q
                    act.wait_ge(s_hid, u - 1 + FREE_HID)
                    act.wait_ge(s_p1, u + 1)
                    act.activation(act1[:, q % 2, :], p1[:, q % 2, :], ACT.Silu).then_inc(s_a1, 1)
            act.sem_inc(s_a1, FREE_A1)
            act.preload_act_table_set("silu_and_others")
            steps(act, lambda ep, slot: None, step)

        @block.gpsimd
        def _(pool):
            pool.memset(acc[:], 0.0).then_inc(s_zero, 1)

        @block.vector
        def _(dve):
            def step(s, i, slot, par, e):
                for q, hb in enumerate(ORDER):
                    u = HB * s + q
                    if q == 0:
                        dve.wait_ge(s_y, 2 * s - 2 + FREE_Y)
                    dve.wait_ge(s_a1, u + 1 + FREE_A1)
                    dve.wait_ge(s_p3, u + 1)
                    dve.tensor_tensor(hid[:, par, hb, :], act1[:, q % 2, :], p3[:, q % 2, :], ALU.mult).then_inc(s_hid, 1)
                for t in range(NB):
                    if t % 2 == 0:
                        dve.wait_ge(s_y, 2 * s + t // 2 + 1 + FREE_Y)
                    part = acc[:, bass.ds(i * NB + t, 1), :].rearrange("p a c -> p (a c)")
                    op = dve.scalar_tensor_tensor(out=part, in0=yp[:, t, :],
                                                  scalar=gates[:, bass.ds(i * NB + t, 1), bass.ds(e, 1)].rearrange("p a b -> p (a b)"),
                                                  in1=part, op0=ALU.mult, op1=ALU.add)
                    if t % 2:
                        op.then_inc(s_acc, 1)
            dve.sem_inc(s_hid, FREE_HID)
            dve.sem_inc(s_acc, FREE_ACC)
            dve.sem_inc(s_xo, 2 * CB)
            dve.wait_ge(s_zero, 1)
            steps(dve, lambda ep, slot: None, step)
            for i in range(CHUNKS):
                if i >= 2:
                    dve.wait_ge(s_out[i % 2], 16 * (i // 2))
                for c in range(CB):
                    dve.wait_ge(s_tp, CB * i + c + 1)
                    dve.tensor_tensor(xo[:, i % 2, c, :], tp[:, c, :], x1[:, c, i * TK:(i + 1) * TK],
                                      ALU.add).then_inc(s_xo, 1)


def whole_program(nc, a, out_d):
    xu_d, xc_d, sz_d, ysum_d = [nc.dram_tensor(f"scratch_{n}", [B, P, k, L], F32, kind="Internal").ap()
                                for n, k in (("xu", C // P), ("xc", DB), ("sz", DB), ("ysum", DB))]
    front_stage(nc, a["x"], a["w_in"], a["ln"], a["w_conv"], a["b_conv"], a["identity"], xu_d, xc_d, sz_d)
    scan_stage(nc, xc_d, a["w_xproj"], a["w_dt"], a["b_dt"], a["A_log"], a["Ds"], a["selector"], a["identity"], ysum_d)
    with ExitStack() as ctx:
        def sb(name, shape):
            return ctx.enter_context(nc.sbuf_tensor("keep_" + name, shape, F32))
        T = B * L
        ident = sb("identity", [P, P])
        x1 = sb("residual", [P, C // P, T])
        tn = sb("normed", [P, C // P, T])
        w0 = sb("router", [P, L // P, NE])
        w0t = sb("router_turned", [NE, L])
        gates = sb("gates", [P, T // P, NE])
        s_ident = ctx.enter_context(nc.semaphore("identity_in"))
        with nc.Block() as block:
            @block.sync
            def _(sp):
                sp.dma_start(ident[:], a["identity"]).then_inc(s_ident, 16)
                sp.wait_ge(s_ident, 16)
        mix_stage(nc, ysum_d, sz_d, xu_d, a["onorm"], a["w_out"], ident, a["Wr"], a["br"], x1, tn, w0, w0t)
        soft_stage(nc, a["W1"], a["W2"], a["Wo"], a["bn"], a["bo"], ident, tn, x1, w0, w0t)
        dct_stage(nc, a["dct"], a["router_w"], a["lower"], ident, x1, tn, gates)
        moe_stage(nc, a["w13"], a["w2"], ident, x1, tn, gates, out_d)



def front_layout(x, w_in, ln_g, ln_b, w_conv, b_conv):
    import numpy as np
    xl = x.reshape(B, C // P, P, L).transpose(0, 2, 1, 3)
    win = w_in.reshape(C // P, P, 2 * DI).transpose(1, 0, 2)
    lng = np.stack([ln_g, ln_b], -1).reshape(C // P, P, 2).transpose(1, 0, 2)
    wcv = w_conv.reshape(DB, P, 9).transpose(1, 0, 2)
    bcv = b_conv.reshape(DB, P).T
    return [np.ascontiguousarray(a) for a in (xl, win, lng, wcv, bcv)]


def scan_layout(w_xproj, w_dt, b_dt, A_log, Ds):
    import numpy as np
    f = np.float32
    wx = np.zeros((P, 4, DB, P), f)
    t = w_xproj.reshape(4, R + 2 * NST, DB, P).transpose(3, 0, 2, 1)
    for q in range(3):
        wx[..., 32 * q:32 * q + 32] = t[..., R:]
    wx[..., 96:96 + R] = t[..., :R]
    wdt = np.zeros((P, 4, DI), f)
    wdt[96:96 + R] = w_dt.transpose(2, 0, 1)
    bdt = b_dt.reshape(4, DB, P).transpose(2, 0, 1)
    alog = A_log.reshape(4, DB, P, NST).transpose(2, 0, 1, 3)
    ds = Ds.reshape(4, DB, P).transpose(2, 1, 0)
    return [np.ascontiguousarray(a) for a in (wx, wdt, bdt, alog, ds)]


def selector():
    import numpy as np
    from concourse import mybir
    s = np.zeros((96, 2 * NST, P), mybir.dt.np(mybir.dt.bfloat16))
    for q in range(3):
        for r in range(32):
            s[32 * q + r, r, :] = 1
    return s


def mix_layout(onorm_g, onorm_b, w_out, Wr, br):
    import numpy as np
    ong = np.stack([onorm_g, onorm_b], -1).reshape(DB, P, 2).transpose(1, 0, 2)
    wout = w_out.reshape(DB, P, C).transpose(1, 0, 2)
    wr = Wr.reshape(C // P, P, NE).transpose(1, 0, 2)
    return [np.ascontiguousarray(a) for a in (ong, wout, wr, br.reshape(1, NE))]


def soft_layout(W1, W2, Wo, b1, g1, be1, m1, v1, b2, g2, be2, m2, v2):
    import numpy as np
    w = [a.reshape(NE, C // P, P, C).transpose(2, 0, 1, 3) for a in (W1, W2, Wo)]
    bn = np.stack([np.stack([a.reshape(NE * C // P, P).T for a in l], 1) for l in ((b1, g1, be1, m1, v1), (b2, g2, be2, m2, v2))], 1)
    return [np.ascontiguousarray(a) for a in (*w, bn)]


def dct_matrix():
    import numpy as np
    def one(n):
        v, j = np.arange(n, dtype=np.float32)[:, None], np.arange(n, dtype=np.float32)[None, :]
        f = np.cos(np.float32(np.pi) * (np.float32(0.5) + j) * v / np.float32(n)) / np.sqrt(np.float32(n))
        return (f * np.where(v != 0, np.sqrt(np.float32(2)), np.float32(1))).astype(np.float32)
    full = np.kron(one(H), one(W)).T.astype(np.float32)
    return np.ascontiguousarray(full.reshape(L // P, P, L).transpose(1, 0, 2))


def lower_mask():
    import numpy as np
    m = np.tril(np.ones((NE, NE), np.float32), -1)
    return np.ascontiguousarray(np.broadcast_to(m, (P, NE, NE)))


def moe_layout(w1, w2, w3):
    import numpy as np
    hid = w1.shape[1]
    hb = -(-hid // P)
    w13 = np.zeros((NE, P, 2, C // P, hb * P), w1.dtype)
    for which, w in enumerate((w1, w3)):
        w13[:, :, which, :, :hid] = w.transpose(0, 2, 1).reshape(NE, C // P, P, hid).transpose(0, 2, 1, 3)
    down = np.zeros((NE, hb * P, C), w2.dtype)
    down[:, :hid] = w2.transpose(0, 2, 1)
    return w13, np.ascontiguousarray(down.reshape(NE, hb, P, C).transpose(0, 2, 1, 3))


def kernel(**inputs):
    import numpy as np
    import concourse.bacc as bacc
    from concourse.bass_utils import run_bass_kernel_spmd
    v = {k: np.asarray(t) for k, t in inputs.items()}
    conv = {k[8:]: t for k, t in v.items() if k.startswith("L0_conv_")}
    ffn0 = {k[7:]: t for k, t in v.items() if k.startswith("L0_ffn_")}
    ffn1 = {k[7:]: t for k, t in v.items() if k.startswith("L1_ffn_")}

    arr = {}
    arr["x"], arr["w_in"], arr["ln"], arr["w_conv"], arr["b_conv"] = front_layout(
        v["x"], *[conv[n] for n in ("w_in", "ln_g", "ln_b", "w_conv", "b_conv")])
    arr["w_xproj"], arr["w_dt"], arr["b_dt"], arr["A_log"], arr["Ds"] = scan_layout(
        *[conv[n] for n in ("w_xproj", "w_dt", "b_dt", "A_log", "Ds")])
    arr["selector"], arr["identity"] = selector(), np.eye(P, dtype=np.float32)
    arr["onorm"], arr["w_out"], arr["Wr"], arr["br"] = mix_layout(
        *[conv[n] for n in ("onorm_g", "onorm_b", "w_out")], ffn0["Wr"], ffn0["br"])
    arr["W1"], arr["W2"], arr["Wo"], arr["bn"] = soft_layout(
        *[ffn0[n] for n in ("W1", "W2", "Wo", "b1", "g1", "be1", "m1", "v1", "b2", "g2", "be2", "m2", "v2")])
    arr["bo"] = ffn0["bo"]
    arr["dct"], arr["lower"] = dct_matrix(), lower_mask()
    arr["router_w"] = np.ascontiguousarray(ffn1["router_w"].T.reshape(C // P, P, NE).transpose(1, 0, 2))
    arr["w13"], arr["w2"] = moe_layout(ffn1["w1"], ffn1["w2"], ffn1["w3"])

    nc = bacc.Bacc("TRN2", target_bir_lowering=False, num_devices=1)
    args = {n: nc.dram_tensor(n + "_in", t.shape, mybir.dt.from_np(t.dtype), kind="ExternalInput").ap()
            for n, t in arr.items()}
    out = nc.dram_tensor("out", [B, C, L], F32, kind="ExternalOutput").ap()
    whole_program(nc, args, out)
    result = run_bass_kernel_spmd(nc, [{n + "_in": t for n, t in arr.items()}], core_ids=[0])
    return result.results[0]["out"].reshape(B, C, H, W)
```

```python
import concourse.bass as bass
from concourse import mybir
from contextlib import ExitStack
F32 = mybir.dt.float32
BF16 = mybir.dt.bfloat16
ALU = mybir.AluOpType
ACT = mybir.ActivationFunctionType
AX_X = mybir.AxisListType.X
P = 128
B, C, H, W = 4, 256, 32, 32
L = H * W
DI = 2 * C
DB = DI // P
NST = 16
NE = 8
R = C // 16


def front_stage(nc, x_d, win_d, lng_d, wconv_d, bconv_d, ident_d, xu_d, xc_d, sz_d):
    CB = C // P
    WP = W + 2
    FREE = 16
    PEB = 2
    DVB = DB - PEB
    XC = 2 * PEB + DVB
    numbers = []
    with ExitStack() as ctx:
        def sb(name, shape, dt=F32):
            return ctx.enter_context(nc.sbuf_tensor("fr_" + name, shape, dt))

        def ps(name, shape):
            return ctx.enter_context(nc.psum_tensor("fr_" + name, shape, F32))

        def sem(name):
            s = ctx.enter_context(nc.semaphore("fr_" + name))
            numbers.append(s.num)
            return s

        x = sb("x", [P, CB, L])
        xm = sb("xm", [P, CB, L])
        sq = sb("sq", [P, CB, L])
        u = sb("u", [P, CB, L])
        xu = sb("xu", [P, CB, L])
        xn = sb("xn", [P, CB, L])
        sd = sb("sd", [P, L // P])
        rs = sb("rs", [P, L // P])
        dg = sb("dg", [P, L // P, P])
        win = sb("win", [P, CB, 2 * DI])
        lng = sb("lng", [P, CB, 2])
        wcv = sb("wcv", [P, DB, 9])
        bcv = sb("bcv", [P, DB])
        ident = sb("ident", [P, P])
        ones = sb("ones", [P, P])
        mean = sb("mean", [P, P])
        eps = sb("eps", [P, 2])
        dconv = sb("dconv", [P, PEB, 9, P])
        xpad = sb("xpad", [P, DB, H + 2, WP])
        cacc = sb("cacc", [P, DVB, L])
        xco = sb("xco", [P, DB, L])
        sz = sb("sz", [P, DB, L])
        stp = ps("stp", [P, 2, L // 2])
        vap = ps("vap", [P, L // P])
        xip = ps("xip", [P, L // 2])
        zp = ps("zp", [P, L // 2])
        cvp = ps("cvp", [P, 2, L // 2])

        s_w, s_x, s_cst, s_dcv = sem("weights_in"), sem("x_in"), sem("consts"), sem("taps_built")
        s_mean, s_xm, s_sq, s_var = sem("mean"), sem("centred"), sem("squared"), sem("var")
        s_sd, s_rs, s_dg, s_rb, s_nrm = sem("dev"), sem("rdev"), sem("rdev_diag"), sem("rdev_bcast"), sem("normed")
        s_xu, s_xust, s_xn = sem("xu"), sem("xu_stored"), sem("xn")
        s_pxi, s_xi, s_pz, s_z, s_szst = (sem("xin_psum"), sem("xin"), sem("z_psum"), sem("z"), sem("sz_stored"))
        s_pad = sem("border_zeroed")
        s_tap = sem("taps")
        s_pcv, s_xc, s_xcst = sem("conv_psum"), sem("xc"), sem("xc_stored")

        def halves(ap):
            return ap.rearrange("p (h l) -> p h l", h=2)

        block = ctx.enter_context(nc.Block())

        def rounds(eng, body):
            body(0, True, False)
            with eng.Fori(1, B) as i:
                body(i, True, True)
            body(B, False, True)

        @block.sync
        def _(sp):
            for dst, s in ((win, win_d), (lng, lng_d), (wcv, wconv_d), (bcv, bconv_d), (ident, ident_d)):
                sp.dma_start(dst[:], s).then_inc(s_w, 16)
            sp.sem_inc(s_xust, FREE)
            sp.sem_inc(s_xcst, FREE)
            sp.sem_inc(s_szst, FREE)
            sp.dma_start(x[:], x_d[0]).then_inc(s_x, 16)

            def body(i, front, conv):
                if front:
                    sp.wait_ge(s_xu, i + 1)
                    sp.dma_start(xu_d[i], xu[:]).then_inc(s_xust, 16)
                    if not (isinstance(i, int) and i == B - 1):
                        nxt = i + 1
                        sp.dma_start(x[:], x_d[nxt]).then_inc(s_x, 16)
                if conv:
                    sp.wait_ge(s_xc, XC * i + FREE)
                    sp.dma_start(xc_d[i - 1], xco[:]).then_inc(s_xcst, 16)
                if front:
                    sp.wait_ge(s_z, 2 * DB * i + 2 * DB + FREE)
                    sp.dma_start(sz_d[i], sz[:]).then_inc(s_szst, 16)
            body(0, True, False)
            with sp.Fori(1, B - 1) as i:
                body(i, True, True)
            body(B - 1, True, True)
            body(B, False, True)
            sp.wait_ge(s_xust, 16 * B + FREE)
            sp.wait_ge(s_xcst, 16 * B + FREE)
            sp.wait_ge(s_szst, 16 * B + FREE)

        @block.tensor
        def _(pe):
            def means(i, r, t):
                for h in range(2):
                    for c in range(CB):
                        mm = pe.matmul(stp[:, h, :], mean[:], halves(t[:, c, :])[:, h, :],
                                       start=(c == 0), stop=(c == CB - 1))
                mm.then_inc(s_mean, 1)

            def variances(i, r):
                pe.wait_ge(s_sq, 2 * i + r + 1)
                for t in range(L // P):
                    for c in range(CB):
                        mm = pe.matmul(vap[:, t:t + 1], sq[:, c, t * P:(t + 1) * P], mean[:, 0:1],
                                       start=(c == 0), stop=(c == CB - 1))
                mm.then_inc(s_var, 1)

            def spread(i, r):
                pe.wait_ge(s_dg, 2 * i + r + 1)
                for t in range(L // P):
                    mm = pe.matmul(stp[:, t // 4, t % 4 * P:(t % 4 + 1) * P], ones[:], dg[:, t, :],
                                   start=True, stop=True)
                mm.then_inc(s_rb, 1)

            def project(i):
                pe.wait_ge(s_xn, 2 * i + 2)
                for v in range(2 * DB):
                    d, h = v // 2, v % 2
                    pe.wait_ge(s_xi, 2 * DB * i + v + FREE)
                    for c in range(CB):
                        mm = pe.matmul(xip[:], win[:, c, d * P:(d + 1) * P], halves(xn[:, c, :])[:, h, :],
                                       start=(c == 0), stop=(c == CB - 1))
                    mm.then_inc(s_pxi, 1)
                    pe.wait_ge(s_z, 2 * DB * i + v + FREE)
                    for c in range(CB):
                        mm = pe.matmul(zp[:], win[:, c, DI + d * P:DI + (d + 1) * P], halves(xn[:, c, :])[:, h, :],
                                       start=(c == 0), stop=(c == CB - 1))
                    mm.then_inc(s_pz, 1)

            def convolve(i, part):
                c, h = part // 2, part % 2
                pe.wait_ge(s_xc, XC * (i - 1) + part - 1 - (DVB if part == 0 else 0) + FREE)
                for t in range(9):
                    r0 = t // 3 + h * (H // 2)
                    mm = pe.matmul(cvp[:, h, :], dconv[:, c, t, :],
                                   xpad[:, c, r0:r0 + H // 2, t % 3:t % 3 + W], start=(t == 0), stop=(t == 8))
                mm.then_inc(s_pcv, 1)

            def body(i, front, conv):
                if front:
                    pe.wait_ge(s_x, 16 * i + 16)
                    means(i, 0, x)
                if conv:
                    pe.wait_ge(s_xi, 2 * DB * i + FREE)
                    convolve(i, 0)
                if front:
                    variances(i, 0)
                if conv:
                    convolve(i, 1)
                if front:
                    spread(i, 0)
                if conv:
                    convolve(i, 2)
                if front:
                    pe.wait_ge(s_nrm, 2 * i + 1)
                    means(i, 1, u)
                if conv:
                    convolve(i, 3)
                if front:
                    variances(i, 1)
                    spread(i, 1)
                    project(i)
            pe.wait_ge(s_w, 16 * 5)
            pe.wait_ge(s_cst, 3)
            pe.wait_ge(s_dcv, 1)
            rounds(pe, body)

        @block.scalar
        def _(act):
            act.sem_inc(s_z, FREE)
            act.sem_inc(s_xc, FREE)

            def square(i, r):
                act.wait_ge(s_xm, 2 * i + r + 1)
                act.activation(sq[:], xm[:], ACT.Square).then_inc(s_sq, 1)

            def deviation(i, r):
                act.wait_ge(s_var, 2 * i + r + 1)
                act.activation(sd[:], vap[:], ACT.Sqrt, bias=eps[:, r:r + 1]).then_inc(s_sd, 1)

            def gate(i):
                act.wait_ge(s_szst, 16 * i + FREE)
                for v in range(2 * DB):
                    act.wait_ge(s_pz, 2 * DB * i + v + 1)
                    act.activation(halves(sz[:, v // 2, :])[:, v % 2, :], zp[:], ACT.Silu).then_inc(s_z, 1)

            def conv_out(i, part):
                c, h = part // 2, part % 2
                if part == 0:
                    act.wait_ge(s_xcst, 16 * i)
                act.wait_ge(s_pcv, 2 * PEB * (i - 1) + part + 1)
                act.activation(halves(xco[:, c, :])[:, h, :], cvp[:, h, :], ACT.Silu,
                               bias=bcv[:, c:c + 1]).then_inc(s_xc, 1)

            def taps_out(i):
                for k in range(DVB):
                    c = PEB + k
                    act.wait_ge(s_tap, 9 * DVB * (i - 1) + 8 * DVB + k + 1)
                    act.activation(xco[:, c, :], cacc[:, k, :], ACT.Silu, bias=bcv[:, c:c + 1]).then_inc(s_xc, 1)

            def body(i, front, conv):
                if front:
                    square(i, 0)
                if conv:
                    conv_out(i, 0)
                if front:
                    deviation(i, 0)
                if conv:
                    conv_out(i, 1)
                    conv_out(i, 2)
                if front:
                    square(i, 1)
                if conv:
                    conv_out(i, 3)
                if front:
                    deviation(i, 1)
                if conv:
                    taps_out(i)
                if front:
                    gate(i)
            act.wait_ge(s_w, 16 * 5)
            act.wait_ge(s_cst, 3)
            rounds(act, body)

        @block.gpsimd
        def _(pool):
            pool.memset(ones[:], 1.0).then_inc(s_cst, 1)
            pool.memset(mean[:], 1.0 / C).then_inc(s_cst, 1)
            pool.memset(eps[:, 0:1], 1e-6)
            pool.memset(eps[:, 1:2], 1e-5).then_inc(s_cst, 1)

            def body(i):
                pool.wait_ge(s_xust, 16 * i + FREE)
                pool.wait_ge(s_nrm, 2 * i + 1)
                pool.tensor_tensor(xu[:], x[:], u[:], ALU.add).then_inc(s_xu, 1)
            with pool.Fori(0, B) as i:
                body(i)

        @block.vector
        def _(dve):
            dve.sem_inc(s_xi, FREE)

            def centre(i, r, t):
                dve.wait_ge(s_mean, 2 * i + r + 1)
                for c in range(CB):
                    op = dve.tensor_tensor(halves(xm[:, c, :]), halves(t[:, c, :]), stp[:], ALU.subtract)
                op.then_inc(s_xm, 1)

            def rdev(i, r):
                dve.wait_ge(s_sd, 2 * i + r + 1)
                dve.reciprocal(rs[:], sd[:]).then_inc(s_rs, 1)
                dve.wait_ge(s_rs, 2 * i + r + 1)
                for t in range(L // P):
                    op = dve.tensor_scalar(dg[:, t, :], ident[:], rs[:, t:t + 1], None, ALU.mult)
                op.then_inc(s_dg, 1)

            def scale(i, r, t):
                dve.wait_ge(s_rb, 2 * i + r + 1)
                for c in range(CB):
                    op = dve.tensor_tensor(halves(t[:, c, :]), halves(xm[:, c, :]), stp[:], ALU.mult)
                op.then_inc(s_nrm, 1)

            def taps(i, lo, hi):
                for t in range(lo, hi):
                    for k in range(DVB):
                        shifted = xpad[:, PEB + k, t // 3:t // 3 + H, t % 3:t % 3 + W]
                        sums = cacc[:, k, :].rearrange("p (a b) -> p a b", b=W)
                        tap = wcv[:, PEB + k, t:t + 1]
                        if t == 0:
                            if k == 0:
                                dve.wait_ge(s_xi, 2 * DB * i + FREE)
                                dve.wait_ge(s_xc, XC * (i - 1) + FREE)
                            op = dve.tensor_scalar(sums, shifted, tap, None, ALU.mult)
                        else:
                            dve.wait_ge(s_tap, 9 * DVB * (i - 1) + DVB * (t - 1) + k + 1)
                            op = dve.scalar_tensor_tensor(out=sums, in0=shifted, scalar=tap, in1=sums,
                                                          op0=ALU.mult, op1=ALU.add)
                        op.then_inc(s_tap, 1)

            def body(i, front, conv):
                if not front:
                    taps(i, 0, 9)
                    return
                centre(i, 0, x)
                if conv:
                    taps(i, 0, 3)
                rdev(i, 0)
                scale(i, 0, u)
                if conv:
                    taps(i, 3, 4)
                centre(i, 1, u)
                if conv:
                    taps(i, 4, 9)
                rdev(i, 1)
                scale(i, 1, xn)
                dve.wait_ge(s_nrm, 2 * i + 2)
                for c in range(CB):
                    dve.tensor_scalar(xn[:, c, :], xn[:, c, :], lng[:, c, 0:1], lng[:, c, 1:2],
                                      ALU.mult, ALU.add).then_inc(s_xn, 1)
                for v in range(2 * DB):
                    d, h = v // 2, v % 2
                    dve.wait_ge(s_pxi, 2 * DB * i + v + 1)
                    dve.tensor_copy(xpad[:, d, 1 + h * (H // 2):1 + (h + 1) * (H // 2), 1:1 + W],
                                    xip[:].rearrange("p (a b) -> p a b", b=W)).then_inc(s_xi, 1)
            dve.memset(xpad[:], 0.0).then_inc(s_pad, 1)
            dve.wait_ge(s_w, 16 * 5)
            for c in range(PEB):
                for t in range(9):
                    op = dve.tensor_scalar(dconv[:, c, t, :], ident[:], wcv[:, c, t:t + 1], None, ALU.mult)
            op.then_inc(s_dcv, 1)
            dve.wait_ge(s_pad, 1)
            rounds(dve, body)
    return range(min(numbers), max(numbers) + 1)


def scan_stage(nc, xc_d, wx_d, wdt_d, bdt_d, alog_d, ds_d, sel_d, ident_d, ysum_d):
    KORDER = (0, 2, 1, 3)
    HALF = L // 2
    GROUPS = 4 * 2 * 2
    STEPS = GROUPS * NST
    FREE_H, FREE_HC, FREE_NS, FREE_DB, FREE_DR, FREE_Y = 4, 4, 4, 4, 2, 16
    with ExitStack() as ctx:
        def sb(name, shape, dt=F32):
            return ctx.enter_context(nc.sbuf_tensor("sc_" + name, shape, dt))

        def ps(name, shape):
            return ctx.enter_context(nc.psum_tensor("sc_" + name, shape, F32))

        def sem(name):
            return ctx.enter_context(nc.semaphore("sc_" + name))

        xc = sb("xc", [P, DB, L])
        xct = sb("xct", [P, DB, L])
        yacc = sb("yacc", [P, DB, L])
        wx = sb("wx", [P, 4, DB, P])
        wdt = sb("wdt", [P, 4, DI])
        bdt = sb("bdt", [P, 4, DB])
        nega = sb("nega", [P, 4, DB, NST])
        ds4 = sb("ds4", [P, DB, 4])
        dsum = sb("dsum", [P, DB])
        sel = sb("sel", [96, 2 * NST, P], BF16)
        ident = sb("ident", [P, P])
        xdbl = sb("xdbl", [P, HALF])
        rest = sb("rest", [96, HALF])
        bcs = sb("bcs", [96, 2, HALF], BF16)
        ab = sb("ab", [P, 2, HALF])
        rl = sb("rl", [P, 2, HALF])
        dt = sb("dt", [P, 2, 2, HALF])
        dtx = sb("dtx", [P, 2, 2, HALF])
        bsb = sb("bsb", [P, 2, HALF])
        dbx = sb("dbx", [P, 4, HALF])
        hst = sb("hst", [P, 2, NST, HALF])
        hc = sb("hc", [P, 4, HALF])
        yps = ps("yps", [P, 2, HALF])
        dap = ps("dap", [P, 2, HALF])
        cps = ps("cps", [P, 2, HALF])
        bps = ps("bps", [P, HALF])
        pps = ps("pps", [P, HALF])

        s_w, s_xc, s_yst, s_pass = sem("weights_in"), sem("xc_in"), sem("y_stored"), sem("passed")
        s_aexp, s_cst, s_xct = sem("a_exp"), sem("consts"), sem("xct_built")
        s_xp, s_xd, s_bcs = sem("xproj"), sem("xdbl"), sem("bcs_split")
        s_dtp, s_dtr, s_ab, s_e, s_ln = sem("dt_pre"), sem("dt_read"), sem("dt_abs"), sem("dt_exp"), sem("dt_ln")
        s_part1, s_rest, s_part2 = sem("part1"), sem("rest"), sem("part2")
        s_dt, s_dtx = sem("dt"), sem("dtx")
        s_bB, s_bc, s_cC = sem("b_bcast"), sem("b_copied"), sem("c_bcast")
        s_da, s_db, s_h, s_hc, s_ns, s_dr = (sem("da"), sem("dbx"), sem("scanned"), sem("hc"), sem("nsum"),
                                             sem("drained"))

        def info(gs):
            k, dp, half = KORDER[gs // 4], gs // 2 % 2, gs % 2
            mem_half = half if k < 2 else 1 - half
            return k, dp, half, mem_half

        def span(gs):
            m = info(gs)[3]
            return slice(m * HALF, (m + 1) * HALF)

        def src(gs):
            return xc if info(gs)[0] in (0, 2) else xct

        def segment(eng, lo, hi, body):
            if hi - lo == 1:
                body(lo)
            elif hi > lo:
                with eng.Fori(lo, hi) as p:
                    body(p)

        def batches(eng, image):
            with eng.Fori(0, B - 1) as b:
                image(b, False)
            image(B - 1, True)

        block = ctx.enter_context(nc.Block())

        @block.sync
        def _(sp):
            sp.sem_inc(s_yst, FREE_Y)
            for dst, s in ((wx, wx_d), (wdt, wdt_d), (bdt, bdt_d), (nega, alog_d), (ds4, ds_d),
                           (sel, sel_d), (ident, ident_d)):
                sp.dma_start(dst[:], s).then_inc(s_w, 16)
            sp.dma_start(xc[:], xc_d[0]).then_inc(s_xc, 16)

            def image(b, last):
                g = b * GROUPS
                if not last:
                    sp.wait_ge(s_xp, g + 8)
                    sp.wait_ge(s_dtx, g + 8)
                    sp.wait_ge(s_dr, 2 * g + 8 + FREE_DR)
                    sp.wait_ge(s_xct, 4 * b + 4)
                    sp.wait_ge(s_w, 16)
                    sp.dma_start(xc[:], xc_d[b + 1]).then_inc(s_xc, 16)
                sp.wait_ge(s_dr, 2 * g + 2 * GROUPS + FREE_DR)
                sp.wait_ge(s_w, 16)
                sp.dma_start(ysum_d[b], yacc[:]).then_inc(s_yst, 16)
            batches(sp, image)
            sp.wait_ge(s_yst, 16 * B + FREE_Y)

        @block.tensor
        def _(pe):
            pe.sem_inc(s_ns, FREE_NS)

            def xproj(b, gs):
                k = info(gs)[0]
                g = b * GROUPS + gs
                if k in (0, 2):
                    pe.wait_ge(s_xc, 16 * b + 16)
                else:
                    pe.wait_ge(s_xct, 4 * b + 4)
                pe.wait_ge(s_dtr, 2 * g + 2)
                for c in range(DB):
                    mm = pe.matmul(pps[:], wx[:, k, c, :], src(gs)[:, c, span(gs)],
                                   start=(c == 0), stop=(c == DB - 1))
                mm.then_inc(s_xp, 1)

            def dt_rows(b, gs, j):
                k, dp, _, _ = info(gs)
                g = b * GROUPS + gs
                pe.wait_ge(s_xd, g + 1)
                if j == 1:
                    pe.wait_ge(s_dtr, 2 * g + 1 + 2)
                d0 = (2 * dp + j) * P
                pe.matmul(pps[:], wdt[:, k, d0:d0 + P], xdbl[:], start=True, stop=True).then_inc(s_dtp, 1)

            def bcast_b(g, gs, n):
                pe.wait_ge(s_bc, g * NST + n + 1)
                pe.wait_ge(s_cst, 1)
                pe.matmul(bps[:], sel[:, n, :], bcs[:, gs % 2, :], start=True, stop=True).then_inc(s_bB, 1)

            def bcast_c(g, gs, n, u):
                pe.wait_ge(s_hc, (g * NST + n) * 2 - 2 + FREE_HC)
                pe.wait_ge(s_cst, 1)
                pe.matmul(cps[:, u % 2, :], sel[:, n + NST, :], bcs[:, gs % 2, :],
                          start=True, stop=True).then_inc(s_cC, 1)

            def nsum(g, n, j, u, first, stop):
                pe.wait_ge(s_hc, (g * NST + n) * 2 + j + 1 + FREE_HC)
                pe.matmul(yps[:, j, :], ident[:], hc[:, 2 * (u % 2) + j, :], start=first, stop=stop,
                          skip_group_check=True).then_inc(s_ns, 1)

            def image(b, last):
                for gs in range(GROUPS):
                    g = b * GROUPS + gs
                    nb, ngs = (b, gs + 1) if gs + 1 < GROUPS else (b + 1, 0)
                    more = not (last and gs + 1 == GROUPS)

                    def pair(p, edge=False):
                        for u in range(2):
                            n = 2 * p + u
                            if not edge or n + 3 < NST:
                                bcast_b(g, gs, n + 3)
                            elif more:
                                if n + 3 == NST:
                                    pe.wait_ge(s_bcs, nb * GROUPS + ngs + 2)
                                bcast_b(nb * GROUPS + ngs, ngs, n + 3 - NST)
                            if not edge or n + 1 < NST:
                                bcast_c(g, gs, n + 1, u + 1)
                            elif more:
                                bcast_c(nb * GROUPS + ngs, ngs, 0, 0)
                            for j in range(2):
                                if edge and n == 0:
                                    pe.wait_ge(s_dr, 2 * g + j - 1 + FREE_DR)
                                nsum(g, n, j, u, edge and n == 0, edge and n == NST - 1)
                    pair(0, True)
                    if more:
                        xproj(nb, ngs)
                    segment(pe, 1, 3, pair)
                    if more:
                        dt_rows(nb, ngs, 0)
                    segment(pe, 3, 5, pair)
                    if more:
                        dt_rows(nb, ngs, 1)
                    segment(pe, 5, 6, pair)
                    pair(6, True)
                    pair(7, True)

            pe.wait_ge(s_w, 16 * 7)
            xproj(0, 0)
            dt_rows(0, 0, 0)
            dt_rows(0, 0, 1)
            pe.wait_ge(s_bcs, 2)
            for n in range(3):
                bcast_b(0, 0, n)
            bcast_c(0, 0, 0, 0)
            batches(pe, image)

        @block.scalar
        def _(act):
            act.preload_act_table_set("natural_log_exp_and_others")
            act.sem_inc(s_dtr, 2)
            act.sem_inc(s_bc, 1)
            act.wait_ge(s_w, 16 * 7)
            act.activation(nega[:], nega[:], ACT.Exp).then_inc(s_aexp, 1)

            def xdbl_copy(b, gs, first=False):
                g = b * GROUPS + gs
                act.wait_ge(s_xp, g + 1)
                act.wait_ge(s_rest, g + 1)
                if not first:
                    act.wait_ge(s_cC, (g - 1) * NST + 1)
                act.activation(bcs[:, gs % 2, :], pps[0:96, :], ACT.Copy).then_inc(s_part1, 1)
                act.activation(xdbl[:], pps[:], ACT.Copy).then_inc(s_xd, 1)

            def second_part(b, gs):
                act.wait_ge(s_rest, b * GROUPS + gs + 2)
                for q in (32, 64):
                    act.activation(bcs[q:q + 32, gs % 2, :], rest[q:q + 32, :], ACT.Copy).then_inc(s_part2, 1)

            def abs_relu(b, gs, j):
                k, dp, _, _ = info(gs)
                g = b * GROUPS + gs
                bias = bdt[:, k, 2 * dp + j:2 * dp + j + 1]
                act.wait_ge(s_dtp, 2 * g + j + 1)
                act.wait_ge(s_dt, g + 1)
                act.activation(ab[:, j, :], pps[:], ACT.Abs, bias=bias).then_inc(s_ab, 1)
                act.activation(rl[:, j, :], pps[:], ACT.Relu, bias=bias).then_inc(s_dtr, 1)

            def exp_ln(b, gs):
                g = b * GROUPS + gs
                act.wait_ge(s_ab, 2 * g + 2)
                act.activation(ab[:], ab[:], ACT.Exp, scale=-1.0).then_inc(s_e, 1)
                act.wait_ge(s_e, g + 1)
                act.activation(ab[:], ab[:], ACT.Ln, bias=1.0).then_inc(s_ln, 1)

            def copy_b(g, n, u):
                act.wait_ge(s_bB, g * NST + n + 1)
                act.wait_ge(s_db, 2 * (g * NST + n) - 2 + FREE_DB)
                act.activation(bsb[:, u % 2, :], bps[:], ACT.Copy).then_inc(s_bc, 1)

            def decay(g, gs, n, j):
                k, dp, _, _ = info(gs)
                act.wait_ge(s_h, (g * NST + n) * 2 + j - 1 + FREE_H)
                act.wait_ge(s_cst, 1)
                act.activation(dap[:, j, :], dt[:, gs % 2, j, :], ACT.Exp,
                               scale=nega[:, k, 2 * dp + j, bass.ds(n, 1)]).then_inc(s_da, 1)

            def turn_block(b, c):
                if c == 0:
                    act.wait_ge(s_xc, 16 * b + 16)
                    act.sem_inc(s_pass, 1)
                act.activation(xct[:, c, :].rearrange("p (w h) -> p w h", h=H),
                               xc[:, c, :].rearrange("p (h w) -> p w h", w=W), ACT.Copy).then_inc(s_xct, 1)

            def image(b, last):
                for gs in range(GROUPS):
                    g = b * GROUPS + gs
                    nb, ngs = (b, gs + 1) if gs + 1 < GROUPS else (b + 1, 0)
                    more = not (last and gs + 1 == GROUPS)

                    def pair(p, edge=False):
                        for u in range(2):
                            n = 2 * p + u
                            for j in range(2):
                                decay(g, gs, n, j)
                            if not edge or n + 2 < NST:
                                copy_b(g, n + 2, u)
                            elif more:
                                copy_b(nb * GROUPS + ngs, n + 2 - NST, u)
                    act.wait_ge(s_dt, g + 2)
                    segment(act, 0, 2, pair)
                    if more:
                        xdbl_copy(nb, ngs)
                    if 1 <= gs <= DB:
                        turn_block(b, gs - 1)
                    segment(act, 2, 4, pair)
                    if more:
                        abs_relu(nb, ngs, 0)
                        second_part(nb, ngs)
                    segment(act, 4, 6, pair)
                    if more:
                        abs_relu(nb, ngs, 1)
                        exp_ln(nb, ngs)
                    segment(act, 6, 7, pair)
                    pair(7, True)

            xdbl_copy(0, 0, True)
            second_part(0, 0)
            abs_relu(0, 0, 0)
            abs_relu(0, 0, 1)
            exp_ln(0, 0)
            copy_b(0, 0, 0)
            copy_b(0, 1, 1)
            act.wait_ge(s_cst, 2)
            batches(act, image)

        @block.gpsimd
        def _(pool):
            pool.sem_inc(s_rest, 1)
            pool.sem_inc(s_dt, 1)
            pool.sem_inc(s_db, FREE_DB)

            def remainder(b, gs):
                g = b * GROUPS + gs
                pool.wait_ge(s_part1, g + 1)
                pool.wait_ge(s_xd, g + 1)
                pool.wait_ge(s_bcs, g + 1)
                pool.tensor_tensor(rest[:], xdbl[0:96, :], bcs[:, gs % 2, :], ALU.subtract).then_inc(s_rest, 1)

            def deltas(b, gs):
                _, dp, _, _ = info(gs)
                g = b * GROUPS + gs
                pool.wait_ge(s_ln, g + 1)
                pool.tensor_tensor(dt[:, gs % 2], rl[:], ab[:], ALU.add).then_inc(s_dt, 1)
                pool.wait_ge(s_dt, g + 2)
                pool.tensor_tensor(dtx[:, gs % 2], dt[:, gs % 2], src(gs)[:, 2 * dp:2 * dp + 2, span(gs)],
                                   ALU.mult).then_inc(s_dtx, 1)

            def image(b, last):
                for gs in range(GROUPS):
                    g = b * GROUPS + gs
                    nb, ngs = (b, gs + 1) if gs + 1 < GROUPS else (b + 1, 0)
                    more = not (last and gs + 1 == GROUPS)

                    def pair(p):
                        for u in range(2):
                            for j in range(2):
                                t = g * NST + 2 * p + u
                                pool.wait_ge(s_bc, t + 2)
                                pool.wait_ge(s_h, 2 * t + j - 3 + FREE_H)
                                pool.tensor_tensor(dbx[:, 2 * u + j, :], dtx[:, gs % 2, j, :], bsb[:, u, :],
                                                   ALU.mult).then_inc(s_db, 1)
                    pool.wait_ge(s_dtx, g + 1)
                    pool.sem_inc(s_pass, 1)
                    segment(pool, 0, 3, pair)
                    if more:
                        remainder(nb, ngs)
                    segment(pool, 3, 7, pair)
                    if more:
                        deltas(nb, ngs)
                    segment(pool, 7, 8, pair)

            remainder(0, 0)
            deltas(0, 0)
            batches(pool, image)

        @block.vector
        def _(dve):
            dve.sem_inc(s_h, FREE_H)
            dve.sem_inc(s_dr, FREE_DR)
            dve.sem_inc(s_bcs, 1)
            dve.sem_inc(s_hc, FREE_HC)
            dve.wait_ge(s_w, 16 * 7)
            dve.tensor_reduce(dsum[:], ds4[:], AX_X, ALU.add).then_inc(s_cst, 1)
            dve.wait_ge(s_aexp, 1)
            dve.tensor_scalar(nega[:], nega[:], -1.0, None, ALU.mult).then_inc(s_cst, 1)

            def drain(b, gs):
                k, dp, _, _ = info(gs)
                g = b * GROUPS + gs
                if gs == 0:
                    dve.wait_ge(s_yst, 16 * b + FREE_Y)
                for j in range(2):
                    c = 2 * dp + j
                    dve.wait_ge(s_ns, 2 * NST * (g + 1) - 1 + j + FREE_NS)
                    if k == 0:
                        out = yacc[:, c, span(gs)]
                        op = dve.scalar_tensor_tensor(out=out, in0=xc[:, c, span(gs)], scalar=dsum[:, c:c + 1],
                                                      in1=yps[:, j, :], op0=ALU.mult, op1=ALU.add)
                    elif k == 2:
                        out = yacc[:, c, span(gs)]
                        op = dve.tensor_tensor(out, yps[:, j, :], out, ALU.add)
                    else:
                        w0 = info(gs)[3] * (W // 2)
                        out = yacc[:, c, :].rearrange("p (h w) -> p w h", w=W)[:, w0:w0 + W // 2, :]
                        op = dve.tensor_tensor(out, yps[:, j, :].rearrange("p (w h) -> p w h", h=H), out, ALU.add)
                    op.then_inc(s_dr, 1)

            def third_part(b, gs):
                g = b * GROUPS + gs
                part = bcs[64:96, gs % 2, :]
                dve.wait_ge(s_part2, 2 * g + 2)
                dve.tensor_tensor(part, rest[64:96, :], part, ALU.subtract).then_inc(s_bcs, 1)

            def image(b, last):
                for gs in range(GROUPS):
                    k, dp, half, _ = info(gs)
                    g = b * GROUPS + gs

                    def ordered(ap):
                        return ap if k < 2 else ap[:, ::-1]

                    def pair(p, first=False):
                        for u in range(2):
                            t = g * NST + 2 * p + u
                            n = 2 * p + u
                            for j in range(2):
                                hs = hst[:, j, n, :]
                                end = hst[:, j, n, HALF - 1:HALF]
                                dve.wait_ge(s_da, 2 * t + j + 1)
                                dve.wait_ge(s_db, 2 * t + j + 1 + FREE_DB)
                                dve.tensor_tensor_scan(hs, ordered(dap[:, j, :]), ordered(dbx[:, 2 * u + j, :]),
                                                       0.0 if half == 0 else end, ALU.mult, ALU.add).then_inc(s_h, 1)
                            dve.wait_ge(s_cC, t + 1)
                            for j in range(2):
                                dve.wait_ge(s_h, 2 * t + j + 1 + FREE_H)
                                dve.wait_ge(s_ns, 2 * t + j - 3 + FREE_NS)
                                dve.tensor_tensor(ordered(hc[:, 2 * u + j, :]), hst[:, j, n, :], ordered(cps[:, u, :]),
                                                  ALU.mult).then_inc(s_hc, 1)
                            if first and u == 0 and gs > 0:
                                drain(b, gs - 1)
                    pair(0, True)
                    segment(dve, 1, 5, pair)
                    if gs + 1 < GROUPS:
                        third_part(b, gs + 1)
                    elif not last:
                        third_part(b + 1, 0)
                    segment(dve, 5, 8, pair)
                drain(b, GROUPS - 1)

            third_part(0, 0)
            batches(dve, image)


def mix_stage(nc, ysum_d, sz_d, xu_d, on_d, wout_d, ident, wr_d, br_d, x1, tn, w0, w0t):
    CB = C // P
    TB = L // P
    FREE = 4
    with ExitStack() as ctx:
        def sb(name, shape, dt=F32):
            return ctx.enter_context(nc.sbuf_tensor("mx_" + name, shape, dt))

        def ps(name, shape):
            return ctx.enter_context(nc.psum_tensor("mx_" + name, shape, F32))

        def sem(name):
            return ctx.enter_context(nc.semaphore("mx_" + name))

        y = sb("y", [P, DB, L])
        ym = sb("ym", [P, DB, L])
        sz = sb("sz", [P, DB, L])
        xu = sb("xu", [P, CB, L])
        sqa = sb("sqa", [P, DB, L])
        yg = sb("yg", [P, DB, L])
        xm = sb("xm", [P, CB, L])
        sqb = sb("sqb", [P, CB, L])
        sd = sb("sd", [P, 2, TB])
        rs = sb("rs", [P, 2, TB])
        dga = sb("dga", [P, TB, P])
        dgb = sb("dgb", [P, TB, P])
        ong = sb("ong", [P, DB, 2])
        wout = sb("wout", [P, DB, C])
        wr = sb("wr", [P, CB, NE])
        br = sb("br", [1, NE])
        ones = sb("ones", [P, P])
        meana = sb("meana", [P, P])
        meanb = sb("meanb", [P, P])
        eps = sb("eps", [P, 1])
        fs = sb("fs", [P, CB, L])
        mx = sb("mx", [P, TB])
        lg = sb("lg", [P, TB, NE])
        sm = sb("sm", [P, TB])
        sta = ps("sta", [P, 2, L // 2])
        stb = ps("stb", [P, 2, L // 2])
        outp = ps("outp", [P, 2, L // 2])
        vaa = ps("vaa", [P, TB])
        vab = ps("vab", [P, TB])

        s_w, s_y, s_sz, s_xu, s_cst = sem("weights_in"), sem("y_in"), sem("sz_in"), sem("xu_in"), sem("consts")
        s_pass = sem("passed")
        s_ma, s_ym, s_sqa, s_va, s_sda, s_rsa, s_dga, s_rba = [sem("gate_" + n) for n in
            ("mean", "centred", "squared", "var", "dev", "rdev", "rdev_diag", "rdev_bcast")]
        s_yn, s_yb, s_yg = sem("gate_normed"), sem("gate_affine"), sem("gated")
        s_out, s_x1 = sem("projected"), sem("x1")
        s_mb, s_xm, s_sqb, s_vb, s_sdb, s_rsb, s_dgb, s_rbb = [sem("tok_" + n) for n in
            ("mean", "centred", "squared", "var", "dev", "rdev", "rdev_diag", "rdev_bcast")]
        s_tn = sem("tn")
        s_fs, s_lg, s_sm, s_ex, s_wt = sem("feat"), sem("logits"), sem("softmax"), sem("exp"), sem("w0t_psum")
        s_w0t = sem("w0t")

        def halves(ap):
            return ap.rearrange("p (h l) -> p h l", h=2)

        def lgp(t):
            return outp[:, 0, t * NE:(t + 1) * NE]

        def rounds(eng, body):
            body(0, True, False)
            with eng.Fori(1, B) as i:
                body(i, True, True)
            body(B, False, True)

        block = ctx.enter_context(nc.Block())

        @block.sync
        def _(sp):
            sp.dma_start(y[:], ysum_d[0]).then_inc(s_y, 16)
            for dst, s in ((ong, on_d), (wout, wout_d), (wr, wr_d), (br, br_d)):
                sp.dma_start(dst[:], s).then_inc(s_w, 16)
            sp.dma_start(sz[:], sz_d[0]).then_inc(s_sz, 16)
            sp.dma_start(xu[:], xu_d[0]).then_inc(s_xu, 16)
            with sp.Fori(1, B) as i:
                sp.wait_ge(s_ym, i)
                sp.sem_inc(s_pass, 1)
                sp.dma_start(y[:], ysum_d[i]).then_inc(s_y, 16)
                sp.wait_ge(s_yg, DB * i + FREE)
                sp.sem_inc(s_pass, 1)
                sp.dma_start(sz[:], sz_d[i]).then_inc(s_sz, 16)
                sp.wait_ge(s_x1, 2 * CB * i + FREE)
                sp.sem_inc(s_pass, 1)
                sp.dma_start(xu[:], xu_d[i]).then_inc(s_xu, 16)

        @block.tensor
        def _(pe):
            def mean_y(i):
                pe.wait_ge(s_y, 16 * i + 16)
                if not isinstance(i, int):
                    pe.wait_ge(s_yn, DB * i)
                for h in range(2):
                    for c in range(DB):
                        mm = pe.matmul(sta[:, h, :], meana[:], halves(y[:, c, :])[:, h, :],
                                       start=(c == 0), stop=(c == DB - 1))
                mm.then_inc(s_ma, 1)

            def variances(s_in, s_done, i, va, sq, mean, blocks):
                pe.wait_ge(s_in, i + 1)
                for t in range(TB):
                    for c in range(blocks):
                        mm = pe.matmul(va[:, t:t + 1], sq[:, c, t * P:(t + 1) * P], mean[:, 0:1],
                                       start=(c == 0), stop=(c == blocks - 1))
                mm.then_inc(s_done, 1)

            def spread(s_in, s_done, i, st, dg):
                pe.wait_ge(s_in, i + 1)
                for t in range(TB):
                    mm = pe.matmul(st[:, t // 4, t % 4 * P:(t % 4 + 1) * P], ones[:], dg[:, t, :],
                                   start=True, stop=True)
                mm.then_inc(s_done, 1)

            def project(i):
                pe.wait_ge(s_yg, DB * i + DB + FREE)
                for v in range(2 * CB):
                    c, h = v // 2, v % 2
                    pe.wait_ge(s_x1, 2 * CB * i + v - 1 + FREE)
                    for k in range(DB):
                        mm = pe.matmul(outp[:, h, :], wout[:, k, c * P:(c + 1) * P], halves(yg[:, k, :])[:, h, :],
                                       start=(k == 0), stop=(k == DB - 1))
                    mm.then_inc(s_out, 1)

            def mean_x(i):
                pe.wait_ge(s_x1, 2 * CB * i + 2 * CB + FREE)
                for h in range(2):
                    for c in range(CB):
                        mm = pe.matmul(stb[:, h, :], meanb[:], x1[:, c, bass.ds(i * L + h * (L // 2), L // 2)],
                                       start=(c == 0), stop=(c == CB - 1))
                mm.then_inc(s_mb, 1)

            def body(i, gate, token):
                if gate:
                    mean_y(i)
                if token:
                    project(i - 1)
                if gate:
                    variances(s_sqa, s_va, i, vaa, sqa, meana, DB)
                if token:
                    mean_x(i - 1)
                if gate:
                    spread(s_dga, s_rba, i, sta, dga)
                if token:
                    variances(s_sqb, s_vb, i - 1, vab, sqb, meanb, CB)
                    spread(s_dgb, s_rbb, i - 1, stb, dgb)
            pe.wait_ge(s_cst, 4)
            pe.wait_ge(s_w, 16 * 4)
            rounds(pe, body)
            pe.wait_ge(s_fs, 4)
            for t in range(TB):
                for c in range(CB):
                    pe.matmul(lgp(t), fs[:, c, t * P:(t + 1) * P], wr[:, c, :],
                              start=(c == 0), stop=False)
                mm = pe.matmul(lgp(t), ones[0:1, :], br[:], start=False, stop=True)
            mm.then_inc(s_lg, 1)
            pe.wait_ge(s_sm, 5)
            for t in range(TB):
                mm = pe.transpose(sta[0:NE, t // 4, t % 4 * P:(t % 4 + 1) * P], w0[:, t, :], ident[:])
            mm.then_inc(s_wt, 1)

        @block.scalar
        def _(act):
            def body(i, gate, token):
                if gate:
                    act.wait_ge(s_ym, i + 1)
                    act.activation(sqa[:], ym[:], ACT.Square).then_inc(s_sqa, 1)
                    act.wait_ge(s_va, i + 1)
                    act.activation(sd[:, 0, :], vaa[:], ACT.Sqrt, bias=eps[:]).then_inc(s_sda, 1)
                if token:
                    act.wait_ge(s_xm, i)
                    act.activation(sqb[:], xm[:], ACT.Square).then_inc(s_sqb, 1)
                if gate:
                    for c in range(DB):
                        act.wait_ge(s_yn, DB * i + c + 1)
                        act.activation(ym[:, c, :], ym[:, c, :], ACT.Identity, scale=ong[:, c, 0:1],
                                       bias=ong[:, c, 1:2]).then_inc(s_yb, 1)
                if token:
                    act.wait_ge(s_vb, i)
                    act.activation(sd[:, 1, :], vab[:], ACT.Sqrt, bias=eps[:]).then_inc(s_sdb, 1)
            act.wait_ge(s_cst, 4)
            act.wait_ge(s_w, 16 * 4)
            rounds(act, body)
            act.wait_ge(s_sm, 2)
            act.activation(lg[:], lg[:], ACT.Exp).then_inc(s_ex, 1)
            act.wait_ge(s_wt, 1)
            act.activation(w0t[:], sta[0:NE].rearrange("p a b -> p (a b)"), ACT.Copy).then_inc(s_w0t, 1)

        @block.gpsimd
        def _(pool):
            pool.memset(ones[:], 1.0).then_inc(s_cst, 1)
            pool.memset(meana[:], 1.0 / DI).then_inc(s_cst, 1)
            pool.memset(meanb[:], 1.0 / C).then_inc(s_cst, 1)
            pool.memset(eps[:], 1e-5).then_inc(s_cst, 1)
            pool.sem_inc(s_yg, FREE)
            with pool.Fori(0, B) as i:
                pool.wait_ge(s_sz, 16 * i + 16)
                for c in range(DB):
                    pool.wait_ge(s_yb, DB * i + c + 1)
                    pool.tensor_tensor(yg[:, c, :], ym[:, c, :], sz[:, c, :], ALU.mult).then_inc(s_yg, 1)

        @block.vector
        def _(dve):
            def rdev(i, r, s_sd, s_rs, s_dg, dg):
                dve.wait_ge(s_sd, i + 1)
                dve.reciprocal(rs[:, r, :], sd[:, r, :]).then_inc(s_rs, 1)
                dve.wait_ge(s_rs, i + 1)
                for t in range(TB):
                    op = dve.tensor_scalar(dg[:, t, :], ident[:], rs[:, r, t:t + 1], None, ALU.mult)
                op.then_inc(s_dg, 1)

            def body(i, gate, token):
                if gate:
                    dve.wait_ge(s_yg, DB * i + FREE)
                    dve.wait_ge(s_ma, i + 1)
                    for c in range(DB):
                        op = dve.tensor_tensor(halves(ym[:, c, :]), halves(y[:, c, :]), sta[:], ALU.subtract)
                    op.then_inc(s_ym, 1)
                if token:
                    dve.wait_ge(s_xu, 16 * i)
                    for v in range(2 * CB):
                        c, h = v // 2, v % 2
                        dve.wait_ge(s_out, 2 * CB * (i - 1) + v + 1)
                        dve.tensor_tensor(x1[:, c, bass.ds((i - 1) * L + h * (L // 2), L // 2)], outp[:, h, :],
                                          halves(xu[:, c, :])[:, h, :], ALU.add).then_inc(s_x1, 1)
                if gate:
                    rdev(i, 0, s_sda, s_rsa, s_dga, dga)
                if token:
                    dve.wait_ge(s_mb, i)
                    dve.wait_ge(s_x1, 2 * CB * i + FREE)
                    for c in range(CB):
                        op = dve.tensor_tensor(halves(xm[:, c, :]),
                                               halves(x1[:, c, bass.ds((i - 1) * L, L)]), stb[:], ALU.subtract)
                    op.then_inc(s_xm, 1)
                if gate:
                    dve.wait_ge(s_rba, i + 1)
                    for c in range(DB):
                        dve.tensor_tensor(halves(ym[:, c, :]), halves(ym[:, c, :]), sta[:],
                                          ALU.mult).then_inc(s_yn, 1)
                if token:
                    rdev(i - 1, 1, s_sdb, s_rsb, s_dgb, dgb)
                    dve.wait_ge(s_rbb, i)
                    for c in range(CB):
                        op = dve.tensor_tensor(halves(tn[:, c, bass.ds((i - 1) * L, L)]), halves(xm[:, c, :]),
                                               stb[:], ALU.mult)
                    op.then_inc(s_tn, 1)
            dve.sem_inc(s_x1, FREE)
            dve.wait_ge(s_w, 16 * 4)
            rounds(dve, body)
            dve.wait_ge(s_tn, B)
            dve.tensor_tensor(fs[:], tn[:, :, 0:L], tn[:, :, L:2 * L], ALU.add).then_inc(s_fs, 1)
            for b in range(2, B):
                dve.wait_ge(s_fs, b - 1)
                dve.tensor_tensor(fs[:], fs[:], tn[:, :, b * L:(b + 1) * L], ALU.add).then_inc(s_fs, 1)
            dve.wait_ge(s_fs, B - 1)
            dve.tensor_scalar(fs[:], fs[:], 1.0 / B, None, ALU.mult).then_inc(s_fs, 1)
            lgv = outp[:, 0, 0:TB * NE].rearrange("p (t e) -> p t e", e=NE)
            dve.wait_ge(s_lg, 1)
            dve.tensor_reduce(mx[:], lgv, AX_X, ALU.max).then_inc(s_sm, 1)
            dve.wait_ge(s_sm, 1)
            dve.tensor_tensor(lg[:], lgv, mx[:].unsqueeze(2).to_broadcast([P, TB, NE]), ALU.subtract).then_inc(s_sm, 1)
            dve.wait_ge(s_ex, 1)
            dve.tensor_reduce(sm[:], lg[:], AX_X, ALU.add).then_inc(s_sm, 1)
            dve.wait_ge(s_sm, 3)
            dve.reciprocal(sm[:], sm[:]).then_inc(s_sm, 1)
            dve.wait_ge(s_sm, 4)
            dve.tensor_tensor(w0[:], lg[:], sm[:].unsqueeze(2).to_broadcast([P, TB, NE]), ALU.mult).then_inc(s_sm, 1)
            dve.wait_ge(s_w0t, 1)


def soft_stage(nc, w1_d, w2_d, wo_d, bn_d, bo_d, ident, tn, x1, w0, w0t, cleared_d):
    CB = C // P
    TK = 512
    NB = TK // P
    CHUNKS = B * L // TK
    with ExitStack() as ctx:
        def sb(name, shape, dt=F32):
            return ctx.enter_context(nc.sbuf_tensor("so_" + name, shape, dt))

        def ps(name, shape):
            return ctx.enter_context(nc.psum_tensor("so_" + name, shape, F32))

        def sem(name):
            return ctx.enter_context(nc.semaphore("so_" + name))

        w1 = sb("w1", [P, NE, CB, C])
        w2 = sb("w2", [P, NE, CB, C])
        wo = sb("wo", [P, NE, CB, C])
        bn = sb("bn", [P, 2, 5, NE * CB])
        bns = sb("bns", [P, 2, NE * CB])
        bnt = sb("bnt", [P, 2, NE * CB])
        bo = sb("bo", [NE, C])
        eps = sb("eps", [P, 1])
        ROWS = 8
        zero = sb("zero", [P, ROWS * C])
        h1 = sb("h1", [P, 2, CB, TK])
        h2 = sb("h2", [P, 2, CB, TK])
        acc0 = sb("acc0", [P, NB, C])
        acc = sb("acc", [P, NB, C])
        ap = ps("ap", [P, CB, TK])
        bp = ps("bp", [P, CB, TK])
        yp = ps("yp", [P, NB, C])
        tp = ps("tp", [P, CB, TK])

        s_zero, s_clear = sem("zero"), sem("cleared")
        s_w, s_eps, s_bn, s_sd = sem("weights_in"), sem("eps"), sem("bn_step"), sem("bn_dev")
        s_pa, s_h1, s_pb, s_h2, s_py, s_acc = [sem(n) for n in ("h1_psum", "h1", "h2_psum", "h2", "y_psum", "acc")]
        s_pbo, s_acc0, s_pt, s_x2 = [sem(n) for n in ("bias_psum", "bias_acc", "acc_turned", "x2")]

        block = ctx.enter_context(nc.Block())

        @block.sync
        def _(sp):
            for dst, s in ((bn, bn_d), (bo, bo_d), (w1, w1_d), (w2, w2_d), (wo, wo_d)):
                sp.dma_start(dst[:], s).then_inc(s_w, 16)
            sp.wait_ge(s_zero, 1)
            parts = cleared_d.rearrange("(n p k) c -> n p (k c)", p=P, k=ROWS)
            for n in range(parts.shape[0]):
                sp.dma_start(parts[n], zero[:]).then_inc(s_clear, 16)
            sp.wait_ge(s_clear, 16 * parts.shape[0])

        @block.tensor
        def _(pe):
            pe.sem_inc(s_pb, 4)
            pe.sem_inc(s_py, 4)
            pe.sem_inc(s_pt, 1)

            def first(s, i, e):
                for o in range(CB):
                    pe.wait_ge(s_h1, 2 * s + o + 1)
                    for k in range(CB):
                        mm = pe.matmul(ap[:, o, :], w1[:, e, k, o * P:(o + 1) * P],
                                       tn[:, k, bass.ds(i * TK, TK)], start=(k == 0), stop=(k == CB - 1))
                    mm.then_inc(s_pa, 1)

            def second(s, e):
                pe.wait_ge(s_h1, 2 * s + 2 + 2)
                for o in range(CB):
                    pe.wait_ge(s_h2, 2 * s + o + 1)
                    for k in range(CB):
                        mm = pe.matmul(bp[:, o, :], w2[:, e, k, o * P:(o + 1) * P], h1[:, e % 2, k, :],
                                       start=(k == 0), stop=(k == CB - 1))
                    mm.then_inc(s_pb, 1)

            def third(s, e):
                pe.wait_ge(s_h2, 2 * s + 2 + 2)
                for q in range(2):
                    pe.wait_ge(s_acc, 2 * s + q + 1)
                    for t in (2 * q, 2 * q + 1):
                        for k in range(CB):
                            mm = pe.matmul(yp[:, t, :], h2[:, e % 2, k, t * P:(t + 1) * P], wo[:, e, k, :],
                                           start=(k == 0), stop=(k == CB - 1))
                    mm.then_inc(s_py, 1)

            def bias_sums(i, half):
                pe.wait_ge(s_x2, CB * (i - 1) + 2)
                for t in range(NB):
                    tok = (half * NB + t) * P
                    mm = pe.matmul(tp[:, t // 2, t % 2 * C:(t % 2 + 1) * C], w0t[:, tok:tok + P], bo[:],
                                   start=True, stop=True)
                mm.then_inc(s_pbo, 1)

            def turn(i, last=False):
                pe.wait_ge(s_acc, 2 * NE * (i + 1) + 2)
                if not last:
                    pe.wait_ge(s_acc0, i + 2)
                else:
                    pe.wait_ge(s_x2, CB * i + 2)
                for t in range(NB):
                    for c in range(CB):
                        mm = pe.transpose(tp[:, c, t * P:(t + 1) * P], acc[:, t, c * P:(c + 1) * P], ident[:])
                mm.then_inc(s_pt, 1)

            def image(b):
                for half in range(2):
                    i = 2 * b + half
                    for e in range(NE):
                        s = i * NE + e
                        begun = not isinstance(b, int) or b > 0 or half > 0
                        first(s, i, e)
                        if begun or e >= 1:
                            second(s - 1, (e - 1) % NE)
                        if begun and e == 2:
                            turn(i - 1)
                        if begun or e >= 2:
                            third(s - 2, (e - 2) % NE)
                        if e == 4 and not (isinstance(b, int) and b == B - 1 and half == 1):
                            bias_sums(i + 1, 1 - half)
            pe.wait_ge(s_w, 16 * 5)
            for t in range(NB):
                mm = pe.matmul(tp[:, t // 2, t % 2 * C:(t % 2 + 1) * C], w0t[:, t * P:(t + 1) * P], bo[:],
                               start=True, stop=True)
            mm.then_inc(s_pbo, 1)
            pe.wait_ge(s_acc0, 1)
            image(0)
            with pe.Fori(1, B - 1) as b:
                image(b)
            image(B - 1)
            s_end = CHUNKS * NE
            second(s_end - 1, NE - 1)
            third(s_end - 2, NE - 2)
            third(s_end - 1, NE - 1)
            turn(CHUNKS - 1, True)

        @block.scalar
        def _(act):
            act.sem_inc(s_h1, 2)
            act.sem_inc(s_h2, 2)
            act.wait_ge(s_w, 16 * 5)
            act.wait_ge(s_eps, 1)
            act.activation(bns[:], bn[:, :, 4, :], ACT.Sqrt, bias=eps[:]).then_inc(s_sd, 1)
            act.wait_ge(s_bn, 5)

            def relu1(s, e):
                act.wait_ge(s_pb, 2 * s + 2)
                for o in range(CB):
                    col = e * CB + o
                    act.wait_ge(s_pa, 2 * s + o + 1)
                    act.activation(h1[:, e % 2, o, :], ap[:, o, :], ACT.Relu, scale=bns[:, 0, col:col + 1],
                                   bias=bnt[:, 0, col:col + 1]).then_inc(s_h1, 1)

            def relu2(s, e):
                act.wait_ge(s_py, 2 * s + 2)
                for o in range(CB):
                    col = e * CB + o
                    act.wait_ge(s_pb, 2 * s + o + 1 + 4)
                    act.activation(h2[:, e % 2, o, :], bp[:, o, :], ACT.Relu, scale=bns[:, 1, col:col + 1],
                                   bias=bnt[:, 1, col:col + 1]).then_inc(s_h2, 1)

            def copy_bias(i):
                act.wait_ge(s_pbo, i + 1)
                if not (isinstance(i, int) and i == 0):
                    act.wait_ge(s_acc, 2 * NE * (i - 1) + 2 + 2)
                act.activation(acc0[:], tp[:].rearrange("p a (t c) -> p (a t) c", c=C), ACT.Copy).then_inc(s_acc0, 1)

            def image(b):
                for half in range(2):
                    i = 2 * b + half
                    for e in range(NE):
                        s = i * NE + e
                        relu1(s, e)
                        if not isinstance(b, int) or b > 0 or half > 0 or e >= 1:
                            relu2(s - 1, (e - 1) % NE)
                        if e == 4 and not (isinstance(b, int) and b == B - 1 and half == 1):
                            copy_bias(i + 1)
            copy_bias(0)
            image(0)
            with act.Fori(1, B - 1) as b:
                image(b)
            image(B - 1)
            relu2(CHUNKS * NE - 1, NE - 1)

        @block.gpsimd
        def _(pool):
            pool.memset(eps[:], 1e-3).then_inc(s_eps, 1)
            pool.memset(zero[:], 0.0).then_inc(s_zero, 1)

        @block.vector
        def _(dve):
            dve.sem_inc(s_acc, 2)
            dve.sem_inc(s_x2, 2)
            dve.wait_ge(s_w, 16 * 5)
            dve.wait_ge(s_sd, 1)
            dve.reciprocal(bns[:], bns[:]).then_inc(s_bn, 1)
            dve.tensor_tensor(bnt[:], bn[:, :, 0, :], bn[:, :, 3, :], ALU.subtract).then_inc(s_bn, 1)
            dve.wait_ge(s_bn, 2)
            dve.tensor_tensor(bns[:], bns[:], bn[:, :, 1, :], ALU.mult).then_inc(s_bn, 1)
            dve.wait_ge(s_bn, 3)
            dve.tensor_tensor(bnt[:], bnt[:], bns[:], ALU.mult).then_inc(s_bn, 1)
            dve.wait_ge(s_bn, 4)
            dve.tensor_tensor(bnt[:], bnt[:], bn[:, :, 2, :], ALU.add).then_inc(s_bn, 1)

            def add_step(s, i, half, e):
                if e == 0:
                    dve.wait_ge(s_pt, i + 1)
                    dve.wait_ge(s_acc0, i + 1)
                for q in range(2):
                    dve.wait_ge(s_py, 2 * s + q + 1 + 4)
                    if e > 0:
                        dve.wait_ge(s_acc, 2 * (s - 1) + q + 1 + 2)
                    for t in (2 * q, 2 * q + 1):
                        op = dve.scalar_tensor_tensor(out=acc[:, t, :], in0=yp[:, t, :],
                                                      scalar=w0[:, half * NB + t, e:e + 1],
                                                      in1=(acc0 if e == 0 else acc)[:, t, :],
                                                      op0=ALU.mult, op1=ALU.add)
                    op.then_inc(s_acc, 1)

            def add_chunk(i):
                dve.wait_ge(s_pt, i + 2)
                for c in range(CB):
                    part = x1[:, c, bass.ds(i * TK, TK)]
                    dve.tensor_tensor(part, tp[:, c, :], part, ALU.add).then_inc(s_x2, 1)

            def image(b):
                for half in range(2):
                    i = 2 * b + half
                    for e in range(NE):
                        s = i * NE + e
                        begun = not isinstance(b, int) or b > 0 or half > 0
                        if begun and e == 2:
                            add_chunk(i - 1)
                        if e >= 2:
                            add_step(s - 2, i, half, e - 2)
                        elif begun:
                            add_step(s - 2, i - 1, 1 - half, e - 2 + NE)
            image(0)
            with dve.Fori(1, B - 1) as b:
                image(b)
            image(B - 1)
            for e in (NE - 2, NE - 1):
                add_step((CHUNKS - 1) * NE + e, CHUNKS - 1, 1, e)
            add_chunk(CHUNKS - 1)


def dct_stage(nc, dct_d, rw_d, lower_d, ident, x1, tokens, gates, ranks):
    CB = C // P
    TB = L // P
    FREE = 4
    with ExitStack() as ctx:
        def sb(name, shape, dt=F32):
            return ctx.enter_context(nc.sbuf_tensor("dc_" + name, shape, dt))

        def ps(name, shape):
            return ctx.enter_context(nc.psum_tensor("dc_" + name, shape, F32))

        def sem(name):
            return ctx.enter_context(nc.semaphore("dc_" + name))

        dct = sb("dct", [P, TB, L])
        rw = sb("rw", [P, CB, NE])
        lower = sb("lower", [P, NE, NE])
        xm = sb("xm", [P, 2, CB, L])
        sq = sb("sq", [P, 2, CB, L])
        v = sb("v", [P, CB, L])
        tnb = sb("tnb", [P, CB, L])
        vt = sb("vt", [P, TB, C])
        sd = sb("sd", [P, 2, TB])
        rs = sb("rs", [P, 2, TB])
        dg = sb("dg", [P, 2, TB, P])
        ones = sb("ones", [P, P])
        mean = sb("mean", [P, P])
        eps = sb("eps", [P, 2])
        mx = sb("mx", [P, TB])
        pr = sb("pr", [P, TB, NE])
        sm = sb("sm", [P, TB])
        above = sb("above", [P, TB, NE, NE])
        tie = sb("tie", [P, TB, NE, NE])
        sta = ps("sta", [P, 2, L // 2])
        stb = ps("stb", [P, 2, L // 2])
        outp = ps("outp", [P, 2, L // 2])
        vaa = ps("vaa", [P, TB])
        vab = ps("vab", [P, TB + TB * NE])
        st, va = (sta, stb), (vaa[:], vab[:, 0:TB])
        lgv = vab[:, TB:TB + TB * NE].rearrange("p (t e) -> p t e", e=NE)

        s_w, s_cst, s_trn, s_tok = sem("weights_in"), sem("consts"), sem("tn_turn_psum"), sem("tokens")
        s_m, s_xm, s_sq, s_va, s_sd, s_rs, s_dg, s_rb = [[sem(f"norm{r}_{n}") for r in range(2)] for n in
            ("mean", "centred", "squared", "var", "dev", "rdev", "rdev_diag", "rdev_bcast")]
        s_v, s_tr, s_vt, s_dct, s_x3, s_tn = [sem(n) for n in ("v", "turn_psum", "turned", "dct_psum", "x3", "tn")]
        s_lg, s_ex, s_g, s_gate = [sem(n) for n in ("logits", "exp", "gate_step", "gates")]
        s_gr = sem("gate_scale")
        GS = 12

        def halves(ap):
            return ap.rearrange("p (h l) -> p h l", h=2)

        def rounds(eng, body):
            body(0, True, False)
            with eng.Fori(1, B) as i:
                body(i, True, True)
            body(B, False, True)

        block = ctx.enter_context(nc.Block())

        @block.sync
        def _(sp):
            for dst, s in ((rw, rw_d), (lower, lower_d), (dct, dct_d)):
                sp.dma_start(dst[:], s).then_inc(s_w, 16)

        @block.tensor
        def _(pe):
            def means(i, r):
                for h in range(2):
                    for c in range(CB):
                        mm = pe.matmul(st[r][:, h, :], mean[:], x1[:, c, bass.ds(i * L + h * (L // 2), L // 2)],
                                       start=(c == 0), stop=(c == CB - 1))
                mm.then_inc(s_m[r], 1)

            def variances(i, r):
                pe.wait_ge(s_sq[r], i + 1)
                for t in range(TB):
                    for c in range(CB):
                        mm = pe.matmul(va[r][:, t:t + 1], sq[:, r, c, t * P:(t + 1) * P], mean[:, 0:1],
                                       start=(c == 0), stop=(c == CB - 1))
                mm.then_inc(s_va[r], 1)

            def spread(i, r):
                pe.wait_ge(s_dg[r], i + 1)
                for t in range(TB):
                    mm = pe.matmul(st[r][:, t // 4, t % 4 * P:(t % 4 + 1) * P], ones[:], dg[:, r, t, :],
                                   start=True, stop=True)
                mm.then_inc(s_rb[r], 1)

            def turn(i):
                pe.wait_ge(s_v, i + 1)
                for u in range(4):
                    if u < 2:
                        pe.wait_ge(s_x3, 4 * i + FREE)
                    else:
                        pe.wait_ge(s_vt, 4 * i + u - 1)
                    for t in (2 * u, 2 * u + 1):
                        for c in range(CB):
                            col = (t % 2) * C + c * P
                            mm = pe.transpose(outp[:, u % 2, col:col + P], v[:, c, t * P:(t + 1) * P], ident[:])
                    mm.then_inc(s_tr, 1)

            def transform(i, c):
                for h in range(2):
                    if c == 0:
                        pe.wait_ge(s_vt, 4 * i + 4)
                        pe.wait_ge(s_tok, 4 * i + FREE)
                    else:
                        pe.wait_ge(s_x3, 4 * i + 2 * c + h - 1 + FREE)
                    for t in range(TB):
                        mm = pe.matmul(outp[:, h, :], vt[:, t, c * P:(c + 1) * P], halves(dct[:, t, :])[:, h, :],
                                       start=(t == 0), stop=(t == TB - 1))
                    mm.then_inc(s_dct, 1)

            def route(i):
                pe.wait_ge(s_tn, i + 1)
                for t in range(TB):
                    for c in range(CB):
                        mm = pe.matmul(vab[:, TB + t * NE:TB + (t + 1) * NE],
                                       tnb[:, c, t * P:(t + 1) * P], rw[:, c, :],
                                       start=(c == 0), stop=(c == CB - 1))
                mm.then_inc(s_lg, 1)

            def turn_tokens(i, after_turn):
                for u in range(4):
                    if u >= 2:
                        pe.wait_ge(s_tok, 4 * (i - 1) + u - 1 + FREE)
                    elif after_turn:
                        pe.wait_ge(s_vt, 4 * i + u + 3)
                    for t in (2 * u, 2 * u + 1):
                        for c in range(CB):
                            col = (t % 2) * C + c * P
                            mm = pe.transpose(outp[:, u % 2, col:col + P], tnb[:, c, t * P:(t + 1) * P], ident[:])
                    mm.then_inc(s_trn, 1)

            def body(i, norm, token):
                if norm:
                    means(i, 0)
                if token:
                    transform(i - 1, 0)
                if norm:
                    variances(i, 0)
                if token:
                    transform(i - 1, 1)
                if norm:
                    spread(i, 0)
                if token:
                    pe.wait_ge(s_x3, 4 * i + FREE)
                    means(i - 1, 1)
                if norm:
                    turn(i)
                if token:
                    variances(i - 1, 1)
                    spread(i - 1, 1)
                    route(i - 1)
                    turn_tokens(i, norm)
            pe.wait_ge(s_cst, 3)
            pe.wait_ge(s_w, 16 * 3)
            rounds(pe, body)

        @block.scalar
        def _(act):
            def square(i, r):
                act.wait_ge(s_xm[r], i + 1)
                act.activation(sq[:, r], xm[:, r], ACT.Square).then_inc(s_sq[r], 1)

            def deviation(i, r):
                act.wait_ge(s_va[r], i + 1)
                act.activation(sd[:, r, :], va[r], ACT.Sqrt, bias=eps[:, r:r + 1]).then_inc(s_sd[r], 1)

            def body(i, norm, token):
                if norm:
                    square(i, 0)
                    deviation(i, 0)
                if token:
                    square(i - 1, 1)
                if norm:
                    for u in range(4):
                        act.wait_ge(s_tr, 4 * i + u + 1)
                        act.activation(vt[:, 2 * u:2 * u + 2, :], outp[:, u % 2, :].rearrange("p (t c) -> p t c", c=C),
                                       ACT.Copy).then_inc(s_vt, 1)
                if token:
                    deviation(i - 1, 1)
                    act.wait_ge(s_g, GS * (i - 1) + 2)
                    act.activation(pr[:], pr[:], ACT.Exp).then_inc(s_ex, 1)
                    for u in range(4):
                        act.wait_ge(s_trn, 4 * (i - 1) + u + 1)
                        act.activation(tokens[:, bass.ds((i - 1) * TB + 2 * u, 2), :],
                                       outp[:, u % 2, :].rearrange("p (t c) -> p t c", c=C),
                                       ACT.Copy).then_inc(s_tok, 1)
            act.sem_inc(s_tok, FREE)
            act.wait_ge(s_cst, 3)
            rounds(act, body)

        @block.gpsimd
        def _(pool):
            pool.memset(ones[:], 1.0).then_inc(s_cst, 1)
            pool.memset(mean[:], 1.0 / C).then_inc(s_cst, 1)
            pool.memset(eps[:, 0:1], 1e-6)
            pool.memset(eps[:, 1:2], 1e-5).then_inc(s_cst, 1)

        @block.vector
        def _(dve):
            def centre(i, r):
                dve.wait_ge(s_m[r], i + 1)
                for c in range(CB):
                    op = dve.tensor_tensor(halves(xm[:, r, c, :]), halves(x1[:, c, bass.ds(i * L, L)]), st[r][:],
                                           ALU.subtract)
                op.then_inc(s_xm[r], 1)

            def rdev(i, r):
                dve.wait_ge(s_sd[r], i + 1)
                dve.reciprocal(rs[:, r, :], sd[:, r, :]).then_inc(s_rs[r], 1)
                dve.wait_ge(s_rs[r], i + 1)
                for t in range(TB):
                    op = dve.tensor_scalar(dg[:, r, t, :], ident[:], rs[:, r, t:t + 1], None, ALU.mult)
                op.then_inc(s_dg[r], 1)

            def gate(i):
                g0 = GS * i
                e_of = pr[:].unsqueeze(3).to_broadcast([P, TB, NE, NE])
                j_of = pr[:].unsqueeze(2).to_broadcast([P, TB, NE, NE])
                low = lower[:].unsqueeze(1).to_broadcast([P, TB, NE, NE])
                per_t = sm[:].unsqueeze(2).to_broadcast([P, TB, NE])
                dve.wait_ge(s_lg, i + 1)
                dve.tensor_reduce(mx[:], lgv, AX_X, ALU.max).then_inc(s_g, 1)
                dve.wait_ge(s_g, g0 + 1)
                dve.tensor_tensor(pr[:], lgv, mx[:].unsqueeze(2).to_broadcast([P, TB, NE]), ALU.subtract).then_inc(s_g, 1)
                dve.wait_ge(s_ex, i + 1)
                dve.tensor_reduce(sm[:], pr[:], AX_X, ALU.add).then_inc(s_g, 1)
                dve.wait_ge(s_g, g0 + 3)
                dve.reciprocal(sm[:], sm[:]).then_inc(s_g, 1)
                dve.wait_ge(s_g, g0 + 4)
                dve.tensor_tensor(pr[:], pr[:], per_t, ALU.mult).then_inc(s_g, 1)
                dve.wait_ge(s_g, g0 + 5)
                dve.tensor_tensor(tie[:], j_of, e_of, ALU.is_equal).then_inc(s_g, 1)
                dve.tensor_tensor(above[:], j_of, e_of, ALU.is_gt)
                dve.wait_ge(s_g, g0 + 6)
                dve.tensor_tensor(tie[:], tie[:], low, ALU.mult).then_inc(s_g, 1)
                dve.wait_ge(s_g, g0 + 7)
                dve.tensor_tensor(above[:], above[:], tie[:], ALU.add).then_inc(s_g, 1)
                dve.wait_ge(s_g, g0 + 8)
                rank = ranks[:, bass.ds(i * TB, TB), :]
                dve.tensor_reduce(rank, above[:], AX_X, ALU.add).then_inc(s_g, 1)
                dve.wait_ge(s_g, g0 + 9)
                dve.scalar_tensor_tensor(out=pr[:], in0=rank, scalar=2.0, in1=pr[:], op0=ALU.is_lt,
                                         op1=ALU.mult).then_inc(s_g, 1)
                dve.wait_ge(s_g, g0 + 10)
                dve.tensor_reduce(sm[:], pr[:], AX_X, ALU.add).then_inc(s_g, 1)
                dve.wait_ge(s_g, g0 + 11)
                dve.tensor_scalar(sm[:], sm[:], 1e-9, None, ALU.add).then_inc(s_g, 1)
                dve.wait_ge(s_g, g0 + 12)
                dve.reciprocal(sm[:], sm[:]).then_inc(s_gr, 1)
                dve.wait_ge(s_gr, i + 1)
                dve.tensor_tensor(gates[:, bass.ds(i * TB, TB), :], pr[:], per_t, ALU.mult).then_inc(s_gate, 1)

            def body(i, norm, token):
                if norm:
                    centre(i, 0)
                    rdev(i, 0)
                if token:
                    for u in range(4):
                        c, h = u // 2, u % 2
                        part = x1[:, c, bass.ds((i - 1) * L + h * (L // 2), L // 2)]
                        dve.wait_ge(s_dct, 4 * (i - 1) + u + 1)
                        dve.tensor_tensor(part, outp[:, h, :], part, ALU.add).then_inc(s_x3, 1)
                if norm:
                    dve.wait_ge(s_rb[0], i + 1)
                    for c in range(CB):
                        op = dve.tensor_tensor(halves(v[:, c, :]), halves(xm[:, 0, c, :]), sta[:], ALU.mult)
                    op.then_inc(s_v, 1)
                if token:
                    dve.wait_ge(s_x3, 4 * i + FREE)
                    centre(i - 1, 1)
                    rdev(i - 1, 1)
                    dve.wait_ge(s_rb[1], i)
                    dve.wait_ge(s_tok, 4 * (i - 1) + FREE)
                    for c in range(CB):
                        op = dve.tensor_tensor(halves(tnb[:, c, :]), halves(xm[:, 1, c, :]), stb[:], ALU.mult)
                    op.then_inc(s_tn, 1)
                    gate(i - 1)
            dve.sem_inc(s_x3, FREE)
            dve.wait_ge(s_w, 16 * 3)
            rounds(dve, body)
            dve.wait_ge(s_gate, B)


SLOT_TILE = 256
TOP = 2
TOKEN_BLOCKS = B * L // P
TILES = TOP * B * L // SLOT_TILE + NE


def dispatch_stage(nc, table_d, upper_d, tokens, gates, ranks, slots, weight_rows, gsel, sorted_d):
    TB, FULL = TOKEN_BLOCKS, B * L // SLOT_TILE
    with ExitStack() as ctx:
        def sb(name, shape, dt=F32):
            return ctx.enter_context(nc.sbuf_tensor("di_" + name, shape, dt))

        def ps(name, shape):
            return ctx.enter_context(nc.psum_tensor("di_" + name, shape, F32))

        def sem(name):
            return ctx.enter_context(nc.semaphore("di_" + name))

        table = sb("table", [P, FULL + TILES + 1])
        upper = sb("upper", [P, P])
        ones = sb("ones", [P, P])
        mask = sb("mask", [P, TB, NE])
        sel = sb("sel", [P, TOP, TB, NE])
        upto = sb("upto", [P, NE, TB])
        pos = sb("pos", [P, TB, NE])
        over = sb("over", [P, NE, FULL])
        tiles = sb("tiles", [P, NE])
        tend = sb("tend", [P, NE])
        base = sb("base", [P, NE])
        prod = sb("prod", [P, TOP, TB, NE])
        prodg = sb("prodg", [P, TOP, TB, NE])
        slotf = sb("slotf", [P, TOP, TB])
        passed = sb("passed", [P, TILES, NE])
        owner = sb("owner", [P, TILES])
        row = [sb(f"row{k}", [P, C]) for k in range(2)]
        idx = [sb(f"idx{k}", [P, TOP], mybir.dt.uint32) for k in range(2)]
        before = ps("before", [P, TB, NE])
        count = ps("count", [P, TB, NE])

        s_t, s_ones, s_pass, s_d, s_g = [sem(n) for n in ("table_in", "ones", "passed_on", "slot_step", "gate_step")]
        s_pe, s_row, s_idx = sem("counted"), sem("row"), sem("index")
        s_sc = [sem(f"scattered{k}") for k in range(2)]
        SLOTS_DONE = 14 + NE

        block = ctx.enter_context(nc.Block())

        def rounds(eng, body):
            body(0, True)
            with eng.Fori(1, TB // 2) as r:
                body(r, False)

        @block.sync
        def _(sp):
            sp.dma_start(table[:], table_d).then_inc(s_t, 16)
            sp.dma_start(upper[:], upper_d).then_inc(s_t, 16)

        @block.tensor
        def _(pe):
            pe.wait_ge(s_t, 32)
            pe.wait_ge(s_ones, 1)
            pe.wait_ge(s_d, 1)
            flat = mask[:].rearrange("p t e -> p (t e)")
            pe.matmul(before[:].rearrange("p t e -> p (t e)"), upper[:], flat, start=True, stop=True)
            pe.matmul(count[:].rearrange("p t e -> p (t e)"), ones[:], flat, start=True, stop=True).then_inc(s_pe, 1)

        @block.scalar
        def _(act):
            def body(r, first):
                for k in range(2):
                    if not first:
                        act.wait_ge(s_sc[k], 32 * r)
                    act.activation(row[k][:], tokens[:, bass.ds(2 * r + k, 1), :].rearrange("p t c -> p (t c)"),
                                   ACT.Copy).then_inc(s_row, 1)
            rounds(act, body)

        @block.gpsimd
        def _(pool):
            pool.memset(ones[:], 1.0).then_inc(s_ones, 1)
            pool.wait_ge(s_d, SLOTS_DONE)

            def body(r, first):
                for k in range(2):
                    if not first:
                        pool.wait_ge(s_sc[k], 32 * r)
                        pool.sem_inc(s_pass, 1)
                    pool.tensor_copy(idx[k][:], slots[:, :, bass.ds(2 * r + k, 1)].rearrange("p a t -> p (a t)")).then_inc(s_idx, 1)
                    pool.wait_ge(s_row, 2 * r + k + 1)
                    pool.sem_inc(s_pass, 1)
                    pool.wait_ge(s_idx, 2 * r + k + 1)
                    pool.sem_inc(s_pass, 1)
                    for a in range(TOP):
                        pool.indirect_dma_start(sorted_d, bass.IndirectOffsetOnAxis(ap=idx[k][:, a:a + 1], axis=0),
                                                row[k][:], None).then_inc(s_sc[k], 16)
            rounds(pool, body)
            for k in range(2):
                pool.wait_ge(s_sc[k], 32 * TB // 2)

        @block.vector
        def _(dve):
            def after(n):
                dve.wait_ge(s_d, n)

            def spread(ap, dim, shape):
                return ap.unsqueeze(dim).to_broadcast(shape)
            by_choice, blocks = [P, TOP, TB, NE], ones[:, 0:TB]
            starts = spread(table[:, 0:FULL], 1, [P, NE, FULL])
            numbers = spread(table[:, FULL:FULL + TILES], 2, [P, TILES, NE])
            dve.tensor_scalar(mask[:], ranks[:], float(TOP), None, ALU.is_lt).then_inc(s_d, 1)
            for a in range(TOP):
                dve.tensor_scalar(sel[:, a], ranks[:], float(a), None, ALU.is_equal).then_inc(s_d, 1)
            dve.wait_ge(s_ones, 1)
            dve.wait_ge(s_pe, 1)
            for e in range(NE):
                dve.tensor_tensor_scan(upto[:, e, :], blocks, count[:, :, e], 0.0, ALU.mult, ALU.add).then_inc(s_d, 1)
            after(3 + NE)
            dve.tensor_tensor(pos[:], upto[:].rearrange("p e t -> p t e"), count[:], ALU.subtract).then_inc(s_d, 1)
            dve.wait_ge(s_t, 32)
            dve.tensor_tensor(over[:], upto[:, :, TB - 1:TB].to_broadcast([P, NE, FULL]), starts,
                              ALU.is_gt).then_inc(s_d, 1)
            after(5 + NE)
            dve.tensor_reduce(tiles[:], over[:], AX_X, ALU.add).then_inc(s_d, 1)
            after(6 + NE)
            dve.tensor_tensor_scan(tend[:], ones[:, 0:NE], tiles[:], 0.0, ALU.mult, ALU.add).then_inc(s_d, 1)
            after(7 + NE)
            dve.tensor_tensor(base[:], tend[:], tiles[:], ALU.subtract).then_inc(s_d, 1)
            dve.tensor_tensor(pos[:], pos[:], before[:], ALU.add).then_inc(s_d, 1)
            after(9 + NE)
            dve.scalar_tensor_tensor(out=pos[:], in0=spread(base[:], 1, [P, TB, NE]), scalar=float(SLOT_TILE), in1=pos[:],
                                     op0=ALU.mult, op1=ALU.add).then_inc(s_d, 1)
            after(10 + NE)
            dve.tensor_tensor(prod[:], sel[:], spread(pos[:], 1, by_choice), ALU.mult).then_inc(s_d, 1)
            dve.tensor_tensor(prodg[:], sel[:], spread(gates[:], 1, by_choice), ALU.mult).then_inc(s_d, 1)
            after(12 + NE)
            dve.tensor_reduce(slotf[:], prod[:], AX_X, ALU.add).then_inc(s_d, 1)
            after(13 + NE)
            dve.tensor_copy(slots[:], slotf[:]).then_inc(s_d, 1)
            dve.tensor_reduce(gsel[:], prodg[:], AX_X, ALU.add).then_inc(s_g, 1)
            dve.tensor_tensor(passed[:], spread(tend[:], 1, [P, TILES, NE]), numbers, ALU.is_le).then_inc(s_g, 1)
            dve.wait_ge(s_g, 2)
            dve.tensor_reduce(owner[:], passed[:], AX_X, ALU.add).then_inc(s_g, 1)
            dve.wait_ge(s_g, 3)
            dve.tensor_scalar(owner[:], owner[:], float(NE - 1), float(P), ALU.min, ALU.mult).then_inc(s_g, 1)
            dve.wait_ge(s_g, 4)
            dve.tensor_scalar(weight_rows[:], owner[:], table[:, FULL + TILES:], None, ALU.add).then_inc(s_g, 1)
            dve.wait_ge(s_g, 5)


def moe_stage(nc, w13_d, w2_d, sorted_d, ident, weight_rows, y_d):
    CB = C // P
    NB = SLOT_TILE // P
    HB = -(-w2_d.shape[1] // C)
    W13 = w13_d.shape[1]
    HID = W13 // (2 * CB)
    SIZE = [min(P, HID - q * P) for q in range(HB)]
    PIECE = [slice(q * W13 // HB, (q + 1) * W13 // HB) for q in range(HB)]
    RING = 4
    TURNS = TILES // RING
    BANKS = 3
    PAIRS = ((0, 0), (0, 1), (1, 0))
    F32R = mybir.dt.float32r
    with ExitStack() as ctx:
        def sb(name, shape, dt=F32):
            return ctx.enter_context(nc.sbuf_tensor("mo_" + name, shape, dt))

        def ps(name, shape):
            return ctx.enter_context(nc.psum_tensor("mo_" + name, shape, F32))

        def sem(name):
            return ctx.enter_context(nc.semaphore("mo_" + name))

        w13 = [sb(f"w13_{k}", [P, W13]) for k in range(2)]
        w2 = [sb(f"w2_{k}", [P, HB * C]) for k in range(2)]
        w13s = [sb(f"w13s_{k}", [P, 2, W13], F32R) for k in range(2)]
        w2s = [sb(f"w2s_{k}", [P, 2, HB * C], F32R) for k in range(2)]
        widx = [sb(f"widx{k}", [P, 1], mybir.dt.uint32) for k in range(2)]
        xr = [sb(f"xr{k}", [P, NB, C]) for k in range(RING)]
        xt = sb("xt", [P, 2, 2, CB, SLOT_TILE], F32R)
        act1 = sb("act1", [P, 2, SLOT_TILE])
        hidf = sb("hidf", [P, 2, SLOT_TILE])
        hid = sb("hid", [P, 2, 2, HB, SLOT_TILE], F32R)
        yo = [sb(f"yo{k}", [P, NB, C]) for k in range(2)]
        tp = ps("tp", [P, CB, SLOT_TILE])
        up = ps("up", [P, BANKS, 2, SLOT_TILE])
        yp = ps("yp", [P, 2, NB, 2 * C])

        s_pass, s_idx = sem("passed_on"), sem("weight_index")
        s_wt = [sem(f"weights{k}") for k in range(2)]
        s_xr = [sem(f"rows{k}") for k in range(RING)]
        s_yst = [sem(f"y_stored{k}") for k in range(2)]
        s_whi, s_wlo, s_w2hi, s_w2lo = sem("w13_hi"), sem("w13_lo"), sem("w2_hi"), sem("w2_lo")
        s_tp, s_xhi, s_xlo, s_up, s_a1 = [sem(n) for n in ("turned", "rows_hi", "rows_lo", "up_psum", "silu")]
        s_hid, s_hhi, s_hlo, s_y, s_yo = [sem(n) for n in ("hidden", "hidden_hi", "hidden_lo", "y_psum", "y")]

        def wait(eng, s, value):
            if not isinstance(value, int) or value > 0:
                eng.wait_ge(s, value)

        def turns(eng, tile):
            for j in range(RING):
                tile(j, j, 0, False)
            with eng.Fori(1, TURNS - 1) as r:
                for j in range(RING):
                    tile(RING * r + j, j, r, False)
            for j in range(RING):
                tile(RING * (TURNS - 1) + j, j, TURNS - 1, j == RING - 1)

        block = ctx.enter_context(nc.Block())

        @block.sync
        def _(sp):
            def load(t, j, r):
                wait(sp, s_tp, RING * r - RING + j + 1)
                sp.dma_start(xr[j][:], sorted_d[bass.ds(t * SLOT_TILE, SLOT_TILE), :].rearrange(
                    "(h p) c -> p h c", p=P)).then_inc(s_xr[j], 16)

            def store(t, k):
                sp.wait_ge(s_yo, t + 1)
                sp.dma_start(y_d[bass.ds(t * SLOT_TILE, SLOT_TILE), :].rearrange("(h p) c -> p h c", p=P),
                             yo[k][:]).then_inc(s_yst[k], 16)
            for j in range(RING):
                load(j, j, 0)
            with sp.Fori(1, TURNS) as r:
                for j in range(RING):
                    store(RING * (r - 1) + j, j % 2)
                    load(RING * r + j, j, r)
            for j in range(RING):
                store(RING * (TURNS - 1) + j, j % 2)
            for k in range(2):
                sp.wait_ge(s_yst[k], 16 * TILES // 2)

        @block.gpsimd
        def _(pool):
            def gather(t, k):
                pool.tensor_copy(widx[k][:], weight_rows[:, bass.ds(t, 1)]).then_inc(s_idx, 1)
                pool.wait_ge(s_idx, t + 1)
                pool.sem_inc(s_pass, 1)
                for w, w_d in ((w13[k], w13_d), (w2[k], w2_d)):
                    pool.indirect_dma_start(w[:], None, w_d, bass.IndirectOffsetOnAxis(ap=widx[k][:, 0:1], axis=0)
                                            ).then_inc(s_wt[k], 16)

            def split(t, k):
                pool.wait_ge(s_w2hi, t + 1)
                pool.tensor_tensor(w2s[k][:, 1, :], w2[k][:], w2s[k][:, 0, :], ALU.subtract).then_inc(s_w2lo, 1)

            def tile(t, j, r, last):
                split(t, j % 2)
                if not (isinstance(r, int) and r == TURNS - 1 and j >= RING - 2):
                    pool.wait_ge(s_w2lo, t + 1)
                    pool.sem_inc(s_pass, 1)
                    pool.wait_ge(s_wlo, HB * (t + 1))
                    pool.sem_inc(s_pass, 1)
                    gather(t + 2, j % 2)
            gather(0, 0)
            gather(1, 1)
            turns(pool, tile)

        @block.tensor
        def _(pe):
            def turn(t, j, r):
                pe.wait_ge(s_xr[j], 16 * r + 16)
                wait(pe, s_xlo, t)
                for c in range(CB):
                    for h in range(NB):
                        mm = pe.transpose(tp[:, c, h * P:(h + 1) * P], xr[j][:, h, c * P:(c + 1) * P], ident[:])
                mm.then_inc(s_tp, 1)

            def tile(t, j, r, last):
                k2 = j % 2
                pe.wait_ge(s_wlo, HB * (t + 1))
                pe.wait_ge(s_xlo, t + 1)
                for q in range(HB):
                    wait(pe, s_hid, HB * t + q + 1 - BANKS)
                    for which in range(2):
                        for c in range(CB):
                            col = (which * CB + c) * HID + q * P
                            for n, (a, b) in enumerate(PAIRS):
                                mm = pe.matmul(up[0:SIZE[q], q % BANKS, which, :], w13s[k2][:, a, col:col + SIZE[q]],
                                               xt[:, k2, b, c, :], start=(c == 0 and n == 0),
                                               stop=(c == CB - 1 and n == len(PAIRS) - 1))
                    mm.then_inc(s_up, 1)
                if not last:
                    turn(t + 1, (j + 1) % RING, r if j + 1 < RING else r + 1)
                wait(pe, s_yo, t - 1)
                pe.wait_ge(s_w2lo, t + 1)
                for q in range(HB):
                    if q in (0, HB - 1):
                        pe.wait_ge(s_hlo, HB * t + (HB if q else HB - 1))
                    for h in range(NB):
                        for n, (a, b) in enumerate(PAIRS):
                            mm = pe.matmul(yp[:, k2, h, 0:C], hid[0:SIZE[q], k2, a, q, h * P:(h + 1) * P],
                                           w2s[k2][0:SIZE[q], b, q * C:(q + 1) * C], start=(q == 0 and n == 0),
                                           stop=(q == HB - 1 and n == len(PAIRS) - 1))
                mm.then_inc(s_y, 1)
            turn(0, 0, 0)
            turns(pe, tile)

        @block.scalar
        def _(act):
            act.preload_act_table_set("silu_and_others")

            def weights_hi(t, k, use, q):
                if q == 0:
                    act.wait_ge(s_wt[k], 32 * use + 32)
                    wait(act, s_y, t - 1)
                act.activation(w13s[k][:, 0, PIECE[q]], w13[k][:, PIECE[q]], ACT.Copy).then_inc(s_whi, 1)

            def w2_hi(t, k):
                act.activation(w2s[k][:, 0, :], w2[k][:], ACT.Copy).then_inc(s_w2hi, 1)

            def rows_hi(t, k):
                act.wait_ge(s_tp, t + 1)
                wait(act, s_up, HB * (t - 1))
                act.activation(xt[:, k, 0], tp[:], ACT.Copy).then_inc(s_xhi, 1)

            def hidden_hi(t, k, q):
                act.wait_ge(s_hid, HB * t + q + 1)
                act.activation(hid[0:SIZE[q], k, 0, q, :], hidf[0:SIZE[q], q % 2, :], ACT.Copy).then_inc(s_hhi, 1)

            def tile(t, j, r, last):
                wait(act, s_y, t - 1)
                for q in range(HB):
                    u = HB * t + q
                    wait(act, s_hid, u - 1)
                    act.wait_ge(s_up, u + 1)
                    act.activation(act1[0:SIZE[q], q % 2, :], up[0:SIZE[q], q % BANKS, 0, :], ACT.Silu).then_inc(s_a1, 1)
                    if q > 0:
                        hidden_hi(t, j % 2, q - 1)
                    if not last:
                        weights_hi(t + 1, (j + 1) % 2, 2 * r + (j + 1) // 2, q)
                hidden_hi(t, j % 2, HB - 1)
                if not last:
                    rows_hi(t + 1, (j + 1) % 2)
                    w2_hi(t + 1, (j + 1) % 2)
            for q in range(HB):
                weights_hi(0, 0, 0, q)
            rows_hi(0, 0)
            w2_hi(0, 0)
            turns(act, tile)

        @block.vector
        def _(dve):
            def weights_lo(t, k, q):
                if q == 0:
                    wait(dve, s_y, t - 1)
                dve.wait_ge(s_whi, HB * t + q + 1)
                dve.tensor_tensor(w13s[k][:, 1, PIECE[q]], w13[k][:, PIECE[q]], w13s[k][:, 0, PIECE[q]],
                                  ALU.subtract).then_inc(s_wlo, 1)

            def rows_lo(t, k):
                dve.wait_ge(s_xhi, t + 1)
                dve.tensor_tensor(xt[:, k, 1], tp[:], xt[:, k, 0], ALU.subtract).then_inc(s_xlo, 1)

            def hidden_lo(t, k, q):
                dve.wait_ge(s_hhi, HB * t + q + 1)
                dve.tensor_tensor(hid[0:SIZE[q], k, 1, q, :], hidf[0:SIZE[q], q % 2, :], hid[0:SIZE[q], k, 0, q, :],
                                  ALU.subtract).then_inc(s_hlo, 1)

            def y_out(t, k, before):
                wait(dve, s_yst[k], 16 * before)
                dve.wait_ge(s_y, t + 1)
                dve.tensor_copy(yo[k][:], yp[:, k, :, 0:C]).then_inc(s_yo, 1)

            def tile(t, j, r, last):
                k2 = j % 2
                for q in range(HB):
                    dve.wait_ge(s_a1, HB * t + q + 1)
                    wait(dve, s_hlo, HB * t + q - 1)
                    dve.tensor_tensor(hidf[0:SIZE[q], q % 2, :], act1[0:SIZE[q], q % 2, :],
                                      up[0:SIZE[q], q % BANKS, 1, :], ALU.mult).then_inc(s_hid, 1)
                    if q == 0 and not (isinstance(t, int) and t == 0):
                        y_out(t - 1, 1 - k2, 2 * r + (j + 1) // 2 - 1)
                    if q > 0:
                        hidden_lo(t, k2, q - 1)
                    if q > 0 and not last:
                        weights_lo(t + 1, 1 - k2, q - 1)
                hidden_lo(t, k2, HB - 1)
                if not last:
                    weights_lo(t + 1, 1 - k2, HB - 1)
                if not last:
                    rows_lo(t + 1, 1 - k2)
            for q in range(HB):
                weights_lo(0, 0, q)
            rows_lo(0, 0)
            turns(dve, tile)
            y_out(TILES - 1, 1, TILES // 2 - 1)


def combine_stage(nc, ident, x1, slots, gsel, y_d, out_d):
    CB = C // P
    RING = 4
    TURNS = TOKEN_BLOCKS // RING
    with ExitStack() as ctx:
        def sb(name, shape, dt=F32):
            return ctx.enter_context(nc.sbuf_tensor("co_" + name, shape, dt))

        def sem(name):
            return ctx.enter_context(nc.semaphore("co_" + name))

        idx = [sb(f"idx{k}", [P, TOP], mybir.dt.uint32) for k in range(RING)]
        y = [[sb(f"y{k}_{a}", [P, C]) for a in range(TOP)] for k in range(RING)]
        acc = [sb(f"acc{k}", [P, C]) for k in range(2)]
        acc0 = [sb(f"acc0_{k}", [P, C]) for k in range(2)]
        xo = [sb(f"xo{k}", [P, CB, RING * P]) for k in range(2)]
        tp = ctx.enter_context(nc.psum_tensor("co_tp", [P, 2, CB, C], F32))
        s_pass, s_idx, s_a0, s_acc, s_tp, s_xo = [sem(n) for n in ("passed_on", "index", "first", "sum", "turned", "result")]
        s_y = [sem(f"y_in{k}") for k in range(RING)]
        s_out = [sem(f"stored{k}") for k in range(2)]

        def turns(eng, body):
            for half in range(2):
                body(half, half, 0)
            with eng.Fori(1, TURNS // 2) as r:
                for half in range(2):
                    body(2 * r + half, half, r)

        def wait(eng, s, value):
            if not isinstance(value, int) or value > 0:
                eng.wait_ge(s, value)

        block = ctx.enter_context(nc.Block())

        @block.sync
        def _(sp):
            def body(i, half, r):
                sp.wait_ge(s_xo, RING * (i + 1))
                sp.dma_start(out_d[bass.ds(r, 1)].rearrange("b (c p) l -> p (b c) l", p=P)[:, :, half * RING * P:(half + 1) * RING * P],
                             xo[half][:]).then_inc(s_out[half], 16)
            turns(sp, body)
            for k in range(2):
                sp.wait_ge(s_out[k], 16 * TURNS // 2)

        @block.gpsimd
        def _(pool):
            def body(i, half, r):
                for j in range(RING):
                    if not (isinstance(i, int) and i == 0):
                        pool.wait_ge(s_acc, RING * (i - 1) + j + 1)
                        pool.sem_inc(s_pass, 1)
                    pool.tensor_copy(idx[j][:], slots[:, :, bass.ds(RING * i + j, 1)].rearrange("p a t -> p (a t)")
                                     ).then_inc(s_idx, 1)
                    pool.wait_ge(s_idx, RING * i + j + 1)
                    pool.sem_inc(s_pass, 1)
                    for a in range(TOP):
                        pool.indirect_dma_start(y[j][a][:], None, y_d,
                                                bass.IndirectOffsetOnAxis(ap=idx[j][:, a:a + 1], axis=0)
                                                ).then_inc(s_y[j], 16)
            turns(pool, body)

        @block.tensor
        def _(pe):
            def body(i, half, r):
                for j in range(RING):
                    t = RING * i + j
                    pe.wait_ge(s_acc, t + 1)
                    wait(pe, s_xo, t - 1)
                    for c in range(CB):
                        mm = pe.transpose(tp[:, j % 2, c, 0:P], acc[j % 2][:, c * P:(c + 1) * P], ident[:])
                    mm.then_inc(s_tp, 1)
            turns(pe, body)

        @block.scalar
        def _(act):
            def body(i, half, r):
                for j in range(RING):
                    t = RING * i + j
                    act.wait_ge(s_y[j], 32 * i + 32)
                    wait(act, s_acc, t - 1)
                    act.sem_inc(s_pass, 1)
                    act.activation(acc0[j % 2][:], y[j][0][:], ACT.Copy,
                                   scale=gsel[:, 0, bass.ds(t, 1)]).then_inc(s_a0, 1)
            turns(act, body)

        @block.vector
        def _(dve):
            def body(i, half, r):
                for j in range(RING + 1):
                    t = RING * i + j
                    if j < RING:
                        dve.wait_ge(s_a0, t + 1)
                        dve.wait_ge(s_y[j], 32 * i + 32)
                        wait(dve, s_tp, t - 1)
                        dve.scalar_tensor_tensor(out=acc[j % 2][:], in0=y[j][1][:], scalar=gsel[:, 1, bass.ds(t, 1)],
                                                 in1=acc0[j % 2][:], op0=ALU.mult, op1=ALU.add).then_inc(s_acc, 1)
                    if j == 0:
                        wait(dve, s_out[half], 16 * r)
                    else:
                        dve.wait_ge(s_tp, t)
                        dve.tensor_tensor(xo[half][:, :, (j - 1) * P:j * P], tp[:, (j - 1) % 2, :, 0:P],
                                          x1[:, :, bass.ds((t - 1) * P, P)], ALU.add).then_inc(s_xo, 1)
            turns(dve, body)


def whole_program(nc, a, out_d):
    xu_d, xc_d, sz_d, ysum_d = [nc.dram_tensor(f"scratch_{n}", [B, P, k, L], F32, kind="Internal").ap()
                                for n, k in (("xu", C // P), ("xc", DB), ("sz", DB), ("ysum", DB))]
    used = front_stage(nc, a["x"], a["w_in"], a["ln"], a["w_conv"], a["b_conv"], a["identity"], xu_d, xc_d, sz_d)
    with nc.Block() as block:
        @block.gpsimd
        def _(pool):
            pool.sem_clear(used)
    scan_stage(nc, xc_d, a["w_xproj"], a["w_dt"], a["b_dt"], a["A_log"], a["Ds"], a["selector"], a["identity"], ysum_d)
    sorted_d, y_d = [nc.dram_tensor(f"scratch_{n}", [TILES * SLOT_TILE, C], F32, kind="Internal").ap()
                     for n in ("sorted", "y")]
    with ExitStack() as ctx:
        def sb(name, shape, dt=F32, within=ctx):
            return within.enter_context(nc.sbuf_tensor("keep_" + name, shape, dt))
        T = B * L
        ident = sb("identity", [P, P])
        x1 = sb("residual", [P, C // P, T])
        s_ident = ctx.enter_context(nc.semaphore("identity_in"))
        with nc.Block() as block:
            @block.sync
            def _(sp):
                sp.dma_start(ident[:], a["identity"]).then_inc(s_ident, 16)
                sp.wait_ge(s_ident, 16)
        with ExitStack() as layer0:
            tn = sb("normed", [P, C // P, T], within=layer0)
            w0 = sb("router", [P, L // P, NE], within=layer0)
            w0t = sb("router_turned", [NE, L], within=layer0)
            mix_stage(nc, ysum_d, sz_d, xu_d, a["onorm"], a["w_out"], ident, a["Wr"], a["br"], x1, tn, w0, w0t)
            soft_stage(nc, a["W1"], a["W2"], a["Wo"], a["bn"], a["bo"], ident, tn, x1, w0, w0t, sorted_d)
        slots = sb("slots", [P, TOP, TOKEN_BLOCKS], mybir.dt.uint32)
        gsel = sb("chosen_gates", [P, TOP, TOKEN_BLOCKS])
        weight_rows = sb("weight_rows", [P, TILES], mybir.dt.uint32)
        with ExitStack() as routing:
            tokens = sb("tokens", [P, TOKEN_BLOCKS, C], within=routing)
            gates = sb("gates", [P, TOKEN_BLOCKS, NE], within=routing)
            ranks = sb("ranks", [P, TOKEN_BLOCKS, NE], within=routing)
            dct_stage(nc, a["dct"], a["router_w"], a["lower"], ident, x1, tokens, gates, ranks)
            dispatch_stage(nc, a["routing_table"], a["upper"], tokens, gates, ranks, slots, weight_rows, gsel, sorted_d)
        moe_stage(nc, a["w13"], a["w2"], sorted_d, ident, weight_rows, y_d)
        combine_stage(nc, ident, x1, slots, gsel, y_d, out_d)



def front_layout(x, w_in, ln_g, ln_b, w_conv, b_conv):
    import numpy as np
    xl = x.reshape(B, C // P, P, L).transpose(0, 2, 1, 3)
    win = w_in.reshape(C // P, P, 2 * DI).transpose(1, 0, 2)
    lng = np.stack([ln_g, ln_b], -1).reshape(C // P, P, 2).transpose(1, 0, 2)
    wcv = w_conv.reshape(DB, P, 9).transpose(1, 0, 2)
    bcv = b_conv.reshape(DB, P).T
    return [np.ascontiguousarray(a) for a in (xl, win, lng, wcv, bcv)]


def scan_layout(w_xproj, w_dt, b_dt, A_log, Ds):
    import numpy as np
    f = np.float32
    wx = np.zeros((P, 4, DB, P), f)
    t = w_xproj.reshape(4, R + 2 * NST, DB, P).transpose(3, 0, 2, 1)
    for q in range(3):
        wx[..., 32 * q:32 * q + 32] = t[..., R:]
    wx[..., 96:96 + R] = t[..., :R]
    wdt = np.zeros((P, 4, DI), f)
    wdt[96:96 + R] = w_dt.transpose(2, 0, 1)
    bdt = b_dt.reshape(4, DB, P).transpose(2, 0, 1)
    alog = A_log.reshape(4, DB, P, NST).transpose(2, 0, 1, 3)
    ds = Ds.reshape(4, DB, P).transpose(2, 1, 0)
    return [np.ascontiguousarray(a) for a in (wx, wdt, bdt, alog, ds)]


def selector():
    import numpy as np
    from concourse import mybir
    s = np.zeros((96, 2 * NST, P), mybir.dt.np(mybir.dt.bfloat16))
    for q in range(3):
        for r in range(32):
            s[32 * q + r, r, :] = 1
    return s


def mix_layout(onorm_g, onorm_b, w_out, Wr, br):
    import numpy as np
    ong = np.stack([onorm_g, onorm_b], -1).reshape(DB, P, 2).transpose(1, 0, 2)
    wout = w_out.reshape(DB, P, C).transpose(1, 0, 2)
    wr = Wr.reshape(C // P, P, NE).transpose(1, 0, 2)
    return [np.ascontiguousarray(a) for a in (ong, wout, wr, br.reshape(1, NE))]


def soft_layout(W1, W2, Wo, b1, g1, be1, m1, v1, b2, g2, be2, m2, v2):
    import numpy as np
    w = [a.reshape(NE, C // P, P, C).transpose(2, 0, 1, 3) for a in (W1, W2, Wo)]
    bn = np.stack([np.stack([a.reshape(NE * C // P, P).T for a in l], 1) for l in ((b1, g1, be1, m1, v1), (b2, g2, be2, m2, v2))], 1)
    return [np.ascontiguousarray(a) for a in (*w, bn)]


def dct_matrix():
    import numpy as np
    def one(n):
        v, j = np.arange(n, dtype=np.float32)[:, None], np.arange(n, dtype=np.float32)[None, :]
        f = np.cos(np.float32(np.pi) * (np.float32(0.5) + j) * v / np.float32(n)) / np.sqrt(np.float32(n))
        return (f * np.where(v != 0, np.sqrt(np.float32(2)), np.float32(1))).astype(np.float32)
    full = np.kron(one(H), one(W)).T.astype(np.float32)
    return np.ascontiguousarray(full.reshape(L // P, P, L).transpose(1, 0, 2))


def lower_mask():
    import numpy as np
    m = np.tril(np.ones((NE, NE), np.float32), -1)
    return np.ascontiguousarray(np.broadcast_to(m, (P, NE, NE)))


def routing_table():
    import numpy as np
    full = np.arange(B * L // SLOT_TILE) * SLOT_TILE
    row = np.concatenate([full, np.arange(TILES)]).astype(np.float32)
    return np.concatenate([np.broadcast_to(row, (P, row.size)), np.arange(P, dtype=np.float32)[:, None]], 1)


def upper_mask():
    import numpy as np
    return np.triu(np.ones((P, P), np.float32), 1)


def moe_layout(w1, w2, w3):
    import numpy as np
    hid = w1.shape[1]
    hb = -(-hid // P)
    w13 = np.stack([w.transpose(0, 2, 1).reshape(NE, C // P, P, hid) for w in (w1, w3)], 1)
    down = np.zeros((NE, hb * P, C), w2.dtype)
    down[:, :hid] = w2.transpose(0, 2, 1)
    return (np.ascontiguousarray(w13.transpose(0, 3, 1, 2, 4)).reshape(NE * P, -1),
            np.ascontiguousarray(down.reshape(NE, hb, P, C).transpose(0, 2, 1, 3)).reshape(NE * P, -1))


def kernel(**inputs):
    import numpy as np
    import concourse.bacc as bacc
    from concourse.bass_utils import run_bass_kernel_spmd
    v = {k: np.asarray(t) for k, t in inputs.items()}
    conv = {k[8:]: t for k, t in v.items() if k.startswith("L0_conv_")}
    ffn0 = {k[7:]: t for k, t in v.items() if k.startswith("L0_ffn_")}
    ffn1 = {k[7:]: t for k, t in v.items() if k.startswith("L1_ffn_")}

    arr = {}
    arr["x"], arr["w_in"], arr["ln"], arr["w_conv"], arr["b_conv"] = front_layout(
        v["x"], *[conv[n] for n in ("w_in", "ln_g", "ln_b", "w_conv", "b_conv")])
    arr["w_xproj"], arr["w_dt"], arr["b_dt"], arr["A_log"], arr["Ds"] = scan_layout(
        *[conv[n] for n in ("w_xproj", "w_dt", "b_dt", "A_log", "Ds")])
    arr["selector"], arr["identity"] = selector(), np.eye(P, dtype=np.float32)
    arr["onorm"], arr["w_out"], arr["Wr"], arr["br"] = mix_layout(
        *[conv[n] for n in ("onorm_g", "onorm_b", "w_out")], ffn0["Wr"], ffn0["br"])
    arr["W1"], arr["W2"], arr["Wo"], arr["bn"] = soft_layout(
        *[ffn0[n] for n in ("W1", "W2", "Wo", "b1", "g1", "be1", "m1", "v1", "b2", "g2", "be2", "m2", "v2")])
    arr["bo"] = ffn0["bo"]
    arr["dct"], arr["lower"] = dct_matrix(), lower_mask()
    arr["routing_table"], arr["upper"] = routing_table(), upper_mask()
    arr["router_w"] = np.ascontiguousarray(ffn1["router_w"].T.reshape(C // P, P, NE).transpose(1, 0, 2))
    arr["w13"], arr["w2"] = moe_layout(ffn1["w1"], ffn1["w2"], ffn1["w3"])

    nc = bacc.Bacc("TRN2", target_bir_lowering=False, num_devices=1)
    args = {n: nc.dram_tensor(n + "_in", t.shape, mybir.dt.from_np(t.dtype), kind="ExternalInput").ap()
            for n, t in arr.items()}
    out = nc.dram_tensor("out", [B, C, L], F32, kind="ExternalOutput").ap()
    whole_program(nc, args, out)
    result = run_bass_kernel_spmd(nc, [{n + "_in": t for n, t in arr.items()}], core_ids=[0])
    return result.results[0]["out"].reshape(B, C, H, W)
```
